# Optimizing a Trainium2 kernel written in Bass

```python
import numpy as np
import jax
import jax.numpy as jnp

def _softmax(x, axis=-1):
    return jax.nn.softmax(x, axis=axis)

def _gelu(x):
    return jax.nn.gelu(x, approximate=True)

def _silu(x):
    return jax.nn.silu(x)

def _sigmoid(x):
    return jax.nn.sigmoid(x)

def _layernorm(x, axis=-1, eps=1e-05):
    m = jnp.mean(x, axis=axis, keepdims=True)
    v = jnp.var(x, axis=axis, keepdims=True)
    return (x - m) / jnp.sqrt(v + eps)

def _scatter_add(tgt, idx, src, axis=0):
    return tgt.at[idx].add(src)

def _segment_sum(src, seg, n):
    return jax.ops.segment_sum(src, seg, n)
kernel_name = 'mk_adaln_ffn_d2_seqx_r8_0b7ab0'

def setup_inputs(seed: int=0):
    np.random.seed(seed)
    _w = jnp.asarray

    def _rec_inputs():
        import jax
        import jax.numpy as jnp
        _rk = jax.random.key(seed)
        x = -0.000125 + 0.9999 * jax.random.normal(jax.random.fold_in(_rk, 1), (128, 32, 128), jnp.float32)
        _lenS = 32 - jax.random.randint(jax.random.fold_in(_rk, 7), (128,), 0, max(1, 32 // 4) + 1, jnp.int32)
        _lenS2 = 32 - jax.random.randint(jax.random.fold_in(_rk, 8), (128,), 0, max(1, 32 // 4) + 1, jnp.int32)
        cond_512 = 0.00782532 + 1.00527 * jax.random.normal(jax.random.fold_in(_rk, 11), (128, 64), jnp.float32)
        itok_BxS_0_999 = jax.random.randint(jax.random.fold_in(_rk, 12), (128, 32), 0, 125, jnp.int32)
        itok_BxS_0_4 = jax.random.randint(jax.random.fold_in(_rk, 13), (128, 32), 0, 5, jnp.int32)
        cond_64 = 0.0990542 + 1.04422 * jax.random.normal(jax.random.fold_in(_rk, 15), (128, 64), jnp.float32)
        fside_Bx32_0 = -0.136436 + 0.990155 * jax.random.normal(jax.random.fold_in(_rk, 16), (128, 32), jnp.float32)
        _validS = jnp.arange(32)[None, :] < _lenS[:, None]
        _validS2 = jnp.arange(32)[None, :] < _lenS2[:, None]
        _causal = jnp.tril(jnp.ones((32, 32), dtype=bool))
        mask_BxS_ik0 = jnp.where(jnp.broadcast_to(_validS[:, :], (128, 32)), 0, 1).astype(jnp.int32)
        return (x, cond_512, itok_BxS_0_999, itok_BxS_0_4, cond_64, fside_Bx32_0, mask_BxS_ik0)
    x, cond_512, itok_BxS_0_999, itok_BxS_0_4, cond_64, fside_Bx32_0, mask_BxS_ik0 = _rec_inputs()

    def _L0_cond_setup():
        import jax, jax.numpy as jnp
        import numpy as np
        IN_DIM = 128
        OUT_DIM = 128
        MU_DIM = 64
        K = 30
        key = jax.random.key(seed)
        k1, k2, k3, k4, k5 = jax.random.split(key, 5)
        B, S = (16, 256)
        x = jax.random.normal(k1, (B, S, IN_DIM), dtype=jnp.float32)
        mu = jax.random.normal(k2, (B, MU_DIM), dtype=jnp.float32)
        W_dec = jax.random.normal(k3, (MU_DIM, (IN_DIM + 1) * K), dtype=jnp.float32) / np.sqrt(MU_DIM)
        b_dec = jax.random.normal(k4, ((IN_DIM + 1) * K,), dtype=jnp.float32) * 0.01
        V = jax.random.normal(k5, (K, OUT_DIM), dtype=jnp.float32) / np.sqrt(K)
        return {'x': x, 'mu': mu, 'W_dec': W_dec, 'b_dec': b_dec, 'V': V}
    _L0_cond_all = _L0_cond_setup()
    _L0_cond_in = {k: v for k, v in _L0_cond_all.items() if k in ('W_dec', 'b_dec', 'V')}
    del _L0_cond_all

    def _L0_ffn_setup():
        import jax, jax.numpy as jnp
        import numpy as np
        B, S, D, H, O, E, K = (4, 256, 128, 256, 128, 8, 2)
        key = jax.random.key(seed)
        ks = jax.random.split(key, 7)
        sc = 0.02
        return {'x': jax.random.normal(ks[0], (B, S, D), dtype=jnp.float32), 'Wg': jax.random.normal(ks[1], (E, D), dtype=jnp.float32) * sc, 'bg': jnp.zeros((E,), dtype=jnp.float32), 'W1': jax.random.normal(ks[2], (E, H, D), dtype=jnp.float32) * sc, 'b1': jnp.zeros((E, H), dtype=jnp.float32), 'W2': jax.random.normal(ks[3], (E, O, H), dtype=jnp.float32) * sc, 'b2': jnp.zeros((E, O), dtype=jnp.float32)}
    _L0_ffn_all = _L0_ffn_setup()
    _L0_ffn_in = {k: v for k, v in _L0_ffn_all.items() if k in ('Wg', 'bg', 'W1', 'b1', 'W2', 'b2')}
    del _L0_ffn_all

    def _L1_cond_setup():
        import jax, jax.numpy as jnp
        import numpy as np
        EPS = 1e-05

        def _ln(x, g, b):
            m = jnp.mean(x, axis=-1, keepdims=True)
            v = jnp.mean((x - m) ** 2, axis=-1, keepdims=True)
            return (x - m) * jax.lax.rsqrt(v + EPS) * g + b

        def _mlp_ln(s, W1, b1, W2, b2, g, b):
            h = jax.nn.silu(s @ W1 + b1) @ W2 + b2
            return _ln(h, g, b)
        key = jax.random.key(seed)
        B, S, D = (4, 256, 128)
        MEM, NOI, RES = (64, 64, 32)
        ks = jax.random.split(key, 40)
        ki = iter(range(40))

        def nrm(shape, scale=0.02):
            return jax.random.normal(ks[next(ki)], shape, jnp.float32) * scale

        def gamma(shape):
            return jnp.ones(shape, jnp.float32) + nrm(shape)
        inp = {'x': jax.random.normal(ks[next(ki)], (B, S, D), jnp.float32), 'pathway_ids': jax.random.randint(ks[next(ki)], (B, S), 0, 125), 'compartment_ids': jax.random.randint(ks[next(ki)], (B, S), 0, 5), 'time_steps': jax.random.randint(ks[next(ki)], (B, S), 0, 5), 'scale_type': jax.random.randint(ks[next(ki)], (B, S), 0, 3), 'memory_state': jax.random.normal(ks[next(ki)], (B, MEM), jnp.float32), 'noise_state': jax.random.normal(ks[next(ki)], (B, NOI), jnp.float32), 'resource_state': jax.random.normal(ks[next(ki)], (B, RES), jnp.float32), 'pw_g': gamma((125, D)), 'pw_b': nrm((125, D)), 'cp_g': gamma((5, D)), 'cp_b': nrm((5, D)), 'tm_g': gamma((5, D)), 'tm_b': nrm((5, D)), 'ms_g': gamma((3, D)), 'ms_b': nrm((3, D)), 'mem_W1': nrm((MEM, D)), 'mem_b1': jnp.zeros((D,)), 'mem_W2': nrm((D, D)), 'mem_b2': jnp.zeros((D,)), 'mem_g': gamma((D,)), 'mem_be': jnp.zeros((D,)), 'noi_W1': nrm((NOI, D)), 'noi_b1': jnp.zeros((D,)), 'noi_W2': nrm((D, D)), 'noi_b2': jnp.zeros((D,)), 'noi_g': gamma((D,)), 'noi_be': jnp.zeros((D,)), 'res_W1': nrm((RES, D)), 'res_b1': jnp.zeros((D,)), 'res_W2': nrm((D, D)), 'res_b2': jnp.zeros((D,)), 'res_g': gamma((D,)), 'res_be': jnp.zeros((D,)), 'int_W1': nrm((6 * D, D)), 'int_b1': jnp.zeros((D,)), 'int_W2': nrm((D, D)), 'int_b2': jnp.zeros((D,)), 'int_g': gamma((D,)), 'int_be': jnp.zeros((D,)), 'aw': jnp.ones((6,), jnp.float32) / 6.0}
        return inp
    _L1_cond_all = _L1_cond_setup()
    _L1_cond_in = {k: v for k, v in _L1_cond_all.items() if k in ('pw_g', 'pw_b', 'cp_g', 'cp_b', 'tm_g', 'tm_b', 'ms_g', 'ms_b', 'mem_W1', 'mem_b1', 'mem_W2', 'mem_b2', 'mem_g', 'mem_be', 'noi_W1', 'noi_b1', 'noi_W2', 'noi_b2', 'noi_g', 'noi_be', 'res_W1', 'res_b1', 'res_W2', 'res_b2', 'res_g', 'res_be', 'int_W1', 'int_b1', 'int_W2', 'int_b2', 'int_g', 'int_be', 'aw')}
    del _L1_cond_all

    def _L1_ffn_setup():
        import jax, jax.numpy as jnp
        import numpy as np
        D_IN, D_HID = (128, 512)

        def _ternary(key, shape):
            return jax.random.randint(key, shape, -1, 2).astype(jnp.float32)

        def _tlin(x, w, s):
            return jnp.einsum('bsi,oi->bso', x, w) * s
        key = jax.random.key(seed)
        ks = jax.random.split(key, 12)
        inv = lambda fan: 1.0 / np.sqrt(fan).astype(np.float32)
        return {'x': jax.random.normal(ks[0], (4, 256, D_IN), dtype=jnp.float32), 'w1_w': _ternary(ks[1], (D_HID, D_IN)), 'w1_s': jax.random.uniform(ks[2], (D_HID,), dtype=jnp.float32) * inv(D_IN), 'w2_w': _ternary(ks[3], (D_HID, D_IN)), 'w2_s': jax.random.uniform(ks[4], (D_HID,), dtype=jnp.float32) * inv(D_IN), 'h1_w': _ternary(ks[5], (D_HID, D_HID)), 'h1_s': jax.random.uniform(ks[6], (D_HID,), dtype=jnp.float32) * inv(D_HID), 'h2_w': _ternary(ks[7], (D_HID, D_HID)), 'h2_s': jax.random.uniform(ks[8], (D_HID,), dtype=jnp.float32) * inv(D_HID), 'w3_w': _ternary(ks[9], (D_IN, D_HID)), 'w3_s': jax.random.uniform(ks[10], (D_IN,), dtype=jnp.float32) * inv(D_HID)}
    _L1_ffn_all = _L1_ffn_setup()
    _L1_ffn_in = {k: v for k, v in _L1_ffn_all.items() if k in ('w1_w', 'w1_s', 'w2_w', 'w2_s', 'h1_w', 'h1_s', 'h2_w', 'h2_s', 'w3_w', 'w3_s')}
    del _L1_ffn_all
    return {'x': x, 'cond_512': cond_512, 'itok_BxS_0_999': itok_BxS_0_999, 'itok_BxS_0_4': itok_BxS_0_4, 'cond_64': cond_64, 'fside_Bx32_0': fside_Bx32_0, 'mask_BxS_ik0': mask_BxS_ik0, 'L0_cond_W_dec': _L0_cond_in['W_dec'], 'L0_cond_b_dec': _L0_cond_in['b_dec'], 'L0_cond_V': _L0_cond_in['V'], 'L0_ffn_Wg': _L0_ffn_in['Wg'], 'L0_ffn_bg': _L0_ffn_in['bg'], 'L0_ffn_W1': _L0_ffn_in['W1'], 'L0_ffn_b1': _L0_ffn_in['b1'], 'L0_ffn_W2': _L0_ffn_in['W2'], 'L0_ffn_b2': _L0_ffn_in['b2'], 'L1_cond_pw_g': _L1_cond_in['pw_g'], 'L1_cond_pw_b': _L1_cond_in['pw_b'], 'L1_cond_cp_g': _L1_cond_in['cp_g'], 'L1_cond_cp_b': _L1_cond_in['cp_b'], 'L1_cond_tm_g': _L1_cond_in['tm_g'], 'L1_cond_tm_b': _L1_cond_in['tm_b'], 'L1_cond_ms_g': _L1_cond_in['ms_g'], 'L1_cond_ms_b': _L1_cond_in['ms_b'], 'L1_cond_mem_W1': _L1_cond_in['mem_W1'], 'L1_cond_mem_b1': _L1_cond_in['mem_b1'], 'L1_cond_mem_W2': _L1_cond_in['mem_W2'], 'L1_cond_mem_b2': _L1_cond_in['mem_b2'], 'L1_cond_mem_g': _L1_cond_in['mem_g'], 'L1_cond_mem_be': _L1_cond_in['mem_be'], 'L1_cond_noi_W1': _L1_cond_in['noi_W1'], 'L1_cond_noi_b1': _L1_cond_in['noi_b1'], 'L1_cond_noi_W2': _L1_cond_in['noi_W2'], 'L1_cond_noi_b2': _L1_cond_in['noi_b2'], 'L1_cond_noi_g': _L1_cond_in['noi_g'], 'L1_cond_noi_be': _L1_cond_in['noi_be'], 'L1_cond_res_W1': _L1_cond_in['res_W1'], 'L1_cond_res_b1': _L1_cond_in['res_b1'], 'L1_cond_res_W2': _L1_cond_in['res_W2'], 'L1_cond_res_b2': _L1_cond_in['res_b2'], 'L1_cond_res_g': _L1_cond_in['res_g'], 'L1_cond_res_be': _L1_cond_in['res_be'], 'L1_cond_int_W1': _L1_cond_in['int_W1'], 'L1_cond_int_b1': _L1_cond_in['int_b1'], 'L1_cond_int_W2': _L1_cond_in['int_W2'], 'L1_cond_int_b2': _L1_cond_in['int_b2'], 'L1_cond_int_g': _L1_cond_in['int_g'], 'L1_cond_int_be': _L1_cond_in['int_be'], 'L1_cond_aw': _L1_cond_in['aw'], 'L1_ffn_w1_w': _L1_ffn_in['w1_w'], 'L1_ffn_w1_s': _L1_ffn_in['w1_s'], 'L1_ffn_w2_w': _L1_ffn_in['w2_w'], 'L1_ffn_w2_s': _L1_ffn_in['w2_s'], 'L1_ffn_h1_w': _L1_ffn_in['h1_w'], 'L1_ffn_h1_s': _L1_ffn_in['h1_s'], 'L1_ffn_h2_w': _L1_ffn_in['h2_w'], 'L1_ffn_h2_s': _L1_ffn_in['h2_s'], 'L1_ffn_w3_w': _L1_ffn_in['w3_w'], 'L1_ffn_w3_s': _L1_ffn_in['w3_s']}

def reference(x, cond_512, itok_BxS_0_999, itok_BxS_0_4, cond_64, fside_Bx32_0, mask_BxS_ik0, L0_cond_W_dec, L0_cond_b_dec, L0_cond_V, L0_ffn_Wg, L0_ffn_bg, L0_ffn_W1, L0_ffn_b1, L0_ffn_W2, L0_ffn_b2, L1_cond_pw_g, L1_cond_pw_b, L1_cond_cp_g, L1_cond_cp_b, L1_cond_tm_g, L1_cond_tm_b, L1_cond_ms_g, L1_cond_ms_b, L1_cond_mem_W1, L1_cond_mem_b1, L1_cond_mem_W2, L1_cond_mem_b2, L1_cond_mem_g, L1_cond_mem_be, L1_cond_noi_W1, L1_cond_noi_b1, L1_cond_noi_W2, L1_cond_noi_b2, L1_cond_noi_g, L1_cond_noi_be, L1_cond_res_W1, L1_cond_res_b1, L1_cond_res_W2, L1_cond_res_b2, L1_cond_res_g, L1_cond_res_be, L1_cond_int_W1, L1_cond_int_b1, L1_cond_int_W2, L1_cond_int_b2, L1_cond_int_g, L1_cond_int_be, L1_cond_aw, L1_ffn_w1_w, L1_ffn_w1_s, L1_ffn_w2_w, L1_ffn_w2_s, L1_ffn_h1_w, L1_ffn_h1_s, L1_ffn_h2_w, L1_ffn_h2_s, L1_ffn_w3_w, L1_ffn_w3_s):
    import jax
    import jax.numpy as jnp

    def _L0_cond_ref(x, mu, W_dec, b_dec, V):
        import jax, jax.numpy as jnp
        import numpy as np
        IN_DIM = 128
        OUT_DIM = 128
        MU_DIM = 64
        K = 30
        B = mu.shape[0]
        U = (mu @ W_dec + b_dec).reshape(B, IN_DIM + 1, K)
        param = jnp.einsum('bik,kj->bij', U, V)
        weight = param[:, :-1, :]
        bias = param[:, -1, :]
        out = jnp.einsum('bsd,bde->bse', x, weight)
        out = out + bias[:, None, :]
        return out

    def _L0_ffn_ref(x, Wg, bg, W1, b1, W2, b2):
        import jax, jax.numpy as jnp
        import numpy as np
        B, S, D, H, O, E, K = (4, 256, 128, 256, 128, 8, 2)
        b, s, d = x.shape
        xf = x.reshape(b * s, d)
        gate = xf @ Wg.T + bg
        topk_scores, topk_idx = jax.lax.top_k(gate, K)
        w = jax.nn.softmax(topk_scores, axis=-1)
        h = jnp.einsum('td,ehd->teh', xf, W1) + b1[None]
        h = jax.nn.gelu(h, approximate=False)
        o = jnp.einsum('teh,eoh->teo', h, W2) + b2[None]
        sel = jnp.take_along_axis(o, topk_idx[:, :, None], axis=1)
        out = jnp.einsum('tko,tk->to', sel, w)
        return out.reshape(b, s, -1)

    def _L1_cond_ref(x, pathway_ids, compartment_ids, time_steps, scale_type, memory_state, noise_state, resource_state, pw_g, pw_b, cp_g, cp_b, tm_g, tm_b, ms_g, ms_b, mem_W1, mem_b1, mem_W2, mem_b2, mem_g, mem_be, noi_W1, noi_b1, noi_W2, noi_b2, noi_g, noi_be, res_W1, res_b1, res_W2, res_b2, res_g, res_be, int_W1, int_b1, int_W2, int_b2, int_g, int_be, aw):
        import jax, jax.numpy as jnp
        import numpy as np
        EPS = 1e-05

        def _ln(x, g, b):
            m = jnp.mean(x, axis=-1, keepdims=True)
            v = jnp.mean((x - m) ** 2, axis=-1, keepdims=True)
            return (x - m) * jax.lax.rsqrt(v + EPS) * g + b

        def _mlp_ln(s, W1, b1, W2, b2, g, b):
            h = jax.nn.silu(s @ W1 + b1) @ W2 + b2
            return _ln(h, g, b)
        h = _ln(x, pw_g[pathway_ids], pw_b[pathway_ids])
        h = _ln(h, cp_g[compartment_ids], cp_b[compartment_ids])
        t = _ln(x, tm_g[time_steps], tm_b[time_steps])
        m = x + _mlp_ln(memory_state, mem_W1, mem_b1, mem_W2, mem_b2, mem_g, mem_be)[:, None, :]
        n = x + _mlp_ln(noise_state, noi_W1, noi_b1, noi_W2, noi_b2, noi_g, noi_be)[:, None, :]
        r = x + _mlp_ln(resource_state, res_W1, res_b1, res_W2, res_b2, res_g, res_be)[:, None, :]
        s = _ln(x, ms_g[scale_type], ms_b[scale_type])
        w = jax.nn.softmax(aw)
        cat = jnp.concatenate([w[0] * h, w[1] * t, w[2] * m, w[3] * n, w[4] * r, w[5] * s], axis=-1)
        return _mlp_ln(cat, int_W1, int_b1, int_W2, int_b2, int_g, int_be)

    def _L1_ffn_ref(x, w1_w, w1_s, w2_w, w2_s, h1_w, h1_s, h2_w, h2_s, w3_w, w3_s):
        import jax, jax.numpy as jnp
        import numpy as np
        D_IN, D_HID = (128, 512)

        def _ternary(key, shape):
            return jax.random.randint(key, shape, -1, 2).astype(jnp.float32)

        def _tlin(x, w, s):
            return jnp.einsum('bsi,oi->bso', x, w) * s
        h = jax.nn.silu(_tlin(x, w1_w, w1_s)) * _tlin(x, w2_w, w2_s)
        h = jax.nn.gelu(_tlin(h, h1_w, h1_s), approximate=False)
        h = jax.nn.gelu(_tlin(h, h2_w, h2_s), approximate=False)
        return _tlin(h, w3_w, w3_s)
    x = x + _L0_ffn_ref(_L0_cond_ref(x, cond_512, L0_cond_W_dec, L0_cond_b_dec, L0_cond_V), L0_ffn_Wg, L0_ffn_bg, L0_ffn_W1, L0_ffn_b1, L0_ffn_W2, L0_ffn_b2)
    x = x + _L1_ffn_ref(_L1_cond_ref(x, itok_BxS_0_999, itok_BxS_0_4, itok_BxS_0_4, mask_BxS_ik0, cond_512, cond_64, fside_Bx32_0, L1_cond_pw_g, L1_cond_pw_b, L1_cond_cp_g, L1_cond_cp_b, L1_cond_tm_g, L1_cond_tm_b, L1_cond_ms_g, L1_cond_ms_b, L1_cond_mem_W1, L1_cond_mem_b1, L1_cond_mem_W2, L1_cond_mem_b2, L1_cond_mem_g, L1_cond_mem_be, L1_cond_noi_W1, L1_cond_noi_b1, L1_cond_noi_W2, L1_cond_noi_b2, L1_cond_noi_g, L1_cond_noi_be, L1_cond_res_W1, L1_cond_res_b1, L1_cond_res_W2, L1_cond_res_b2, L1_cond_res_g, L1_cond_res_be, L1_cond_int_W1, L1_cond_int_b1, L1_cond_int_W2, L1_cond_int_b2, L1_cond_int_g, L1_cond_int_be, L1_cond_aw), L1_ffn_w1_w, L1_ffn_w1_s, L1_ffn_w2_w, L1_ffn_w2_s, L1_ffn_h1_w, L1_ffn_h1_s, L1_ffn_h2_w, L1_ffn_h2_s, L1_ffn_w3_w, L1_ffn_w3_s)
    return x

_drawn_inputs = setup_inputs


def setup_inputs(seed=0):
    import zlib

    import numpy as np

    out = dict(_drawn_inputs(seed))
    spreads = {'L0_ffn_bg': (0.0, 0.1),
     'L0_ffn_b1': (0.0, 0.1),
     'L0_ffn_b2': (0.0, 0.1),
     'L1_cond_mem_b1': (0.0, 0.1),
     'L1_cond_mem_b2': (0.0, 0.1),
     'L1_cond_mem_be': (0.0, 0.1),
     'L1_cond_noi_b1': (0.0, 0.1),
     'L1_cond_noi_b2': (0.0, 0.1),
     'L1_cond_noi_be': (0.0, 0.1),
     'L1_cond_res_b1': (0.0, 0.1),
     'L1_cond_res_b2': (0.0, 0.1),
     'L1_cond_res_be': (0.0, 0.1),
     'L1_cond_int_b1': (0.0, 0.1),
     'L1_cond_int_b2': (0.0, 0.1),
     'L1_cond_int_be': (0.0, 0.1),
     'L1_cond_aw': (0.1666666716337204, 0.2)}
    factors = {}
    for name, (base, spread) in spreads.items():
        noise = np.random.default_rng([zlib.crc32(name.encode()), seed]).standard_normal(out[name].shape)
        drawn = base * np.exp(spread * noise) if base else spread * noise
        out[name] = jnp.asarray(drawn.astype(out[name].dtype))
    for name, factor in factors.items():
        out[name] = (out[name] * factor).astype(out[name].dtype)
    return out
```

```python
from contextlib import ExitStack

import concourse.bass as bass
from concourse import mybir

ALU = mybir.AluOpType
ACT = mybir.ActivationFunctionType
AX_X = mybir.AxisListType.X
F32 = mybir.dt.float32
F32R = mybir.dt.float32r
I32 = mybir.dt.int32
U32 = mybir.dt.uint32

P = 128
EPS = 1e-5
MASKED = -3.0e38


class Steps:

    def __init__(self, eng, sem, per_block, b):
        self.eng, self.sem, self.n, self.b, self.k = eng, sem, per_block, b, 0

    def __call__(self, ins):
        self.k += 1
        ins.then_inc(self.sem, 1)
        self.eng.wait_ge(self.sem, self.b * self.n + self.k)

    def end(self):
        assert self.k == self.n, (self.k, self.n)


def build(nc, A, out):
    B, D = A["cond_512T"].shape[1], P
    TOK = A["xT"].shape[1]
    S = TOK // B
    T = 512
    NB = TOK // T
    TT = T // P
    BB = T // S
    MU, KR = A["cond_512T"].shape[0], A["V"].shape[0]
    E = A["WgT"].shape[1]
    NH = A["W1T"].shape[1] // P
    HE = NH // E
    FC = A["w12T"].shape[1] // (2 * P)
    NP_, NC_, NM_ = A["pgb"].shape[0], A["ctg"].shape[0], A["msg"].shape[0]
    NI = NC_ + NM_
    RING = 3
    assert E == 8 and NI == 8 and NH % 4 == 0 and FC == 4

    with ExitStack() as ctx:
        def sb(name, shape, dt=F32, stack=ctx):
            return stack.enter_context(nc.sbuf_tensor(name, shape, dt))

        def sem(name):
            return ctx.enter_context(nc.semaphore(name))

        bank = [ctx.enter_context(nc.psum_tensor(f"bank{i}", [P, T], F32)) for i in range(8)]
        HB = bank[0:4]
        OACC = bank[4]
        X0, X1, X2 = bank[5:8]

        W1 = [sb(f"W1_{p}", [P, NH * P], F32R) for p in "hl"]
        W2 = [sb(f"W2_{p}", [P, NH, P], F32R) for p in "hl"]
        w12 = [sb(f"w12_{p}", [P, 2, FC * P], F32R) for p in "hl"]
        h1w = [sb(f"h1w_{p}", [P, FC, FC * P], F32R) for p in "hl"]
        h2w = [sb(f"h2w_{p}", [P, FC, FC * P], F32R) for p in "hl"]
        w3 = [sb(f"w3_{p}", [P, FC, P], F32R) for p in "hl"]
        wmix = [sb(f"wmix_{p}", [P, 4, P], F32R) for p in "hl"]
        wint = [sb(f"wint_{p}", [P, P], F32R) for p in "hl"]
        wg = [sb(f"wg_{p}", [P, E], F32R) for p in "hl"]
        tab8 = [sb(f"tab8_{p}", [NI, P], F32R) for p in "hl"]
        vec = [sb(f"vec_{p}", [P, P], F32R) for p in "hl"]
        ib2 = [sb(f"ib2_{p}", [1, P], F32R) for p in "hl"]
        ident = sb("ident", [P, P])
        identR = sb("identR", [P, P], F32R)
        onesR = sb("onesR", [1, P], F32R)
        Vw = sb("Vw", [KR, P])
        ub = sb("ub", [KR, B])
        b1c = sb("b1c", [P, NH])
        b2e = sb("b2e", [40, P])
        bgt = sb("bgt", [P, E])
        desc8 = sb("desc8", [P, E])
        iota8 = sb("iota8", [NI, 1])
        igb = sb("igb", [P, 2])
        fsc = sb("fsc", [P, 5 * FC])
        hs1 = sb("hs1", [P, FC])
        cs12 = sb("cs12", [P, FC])
        onesf = sb("onesf", [1, P])
        mhalf = sb("mhalf", [P, TT])
        ixp = sb("ixp", [P, TOK // P], I32)
        ixc = sb("ixc", [P, TOK // P], I32)
        ixm = sb("ixm", [P, TOK // P], I32)

        early = ExitStack()
        Wdec = sb("Wdec", [MU + 1, (D + 1) * KR], stack=early)
        Uall = sb("Uall", [P, B, KR], stack=early)
        stage = [sb(f"stage{i}", [P, 2048], stack=early) for i in range(2)]
        muT = sb("muT", [MU + 1, B], stack=early)
        sT = sb("sT", [64, 3, B], stack=early)
        sW1 = sb("sW1", [64, 3, P], stack=early)
        sW2 = sb("sW2", [P, 3, P], stack=early)
        sb1 = sb("sb1", [P, 3], stack=early)
        sbc = sb("sbc", [P, 3, 3, P], stack=early)
        iW1 = sb("iW1", [P, 6, P], stack=early)
        ibb = sb("ibb", [P, P], stack=early)
        tbT = sb("tbT", [P, 3, NI], stack=early)
        aw6 = sb("aw6", [P, 6], stack=early)
        aw_e = sb("aw_e", [P, 6], stack=early)
        awx = sb("awx", [P, 4], stack=early)
        wsc = sb("wsc", [P, 6, P], stack=early)
        sz = sb("sz", [P, 3 * B], stack=early)
        sth = sb("sth", [P, 3 * B], stack=early)
        sa = sb("sa", [P, 3 * B], stack=early)
        sy = sb("sy", [P, 3, P], stack=early)
        syT = sb("syT", [P, 3 * B], stack=early)
        iW2 = sb("iW2", [P, P], stack=early)
        wgf = sb("wgf", [P, E], stack=early)
        ib2f = sb("ib2f", [1, P], stack=early)
        wintf = sb("wintf", [P, P], stack=early)
        wmixf = sb("wmixf", [P, 4, P], stack=early)
        tab8f = sb("tab8f", [NI, P], stack=early)
        vecf = sb("vecf", [P, P], stack=early)
        sbn = sb("sbn", [P, 3, 6], stack=early)
        smv = sb("smv", [P, 3, 2], stack=early)
        sve = sb("sve", [P, 3], stack=early)
        srs = sb("srs", [P, 3], stack=early)
        early.close()

        gwb = sb("gwb", [P, E, T])
        hA = [sb(f"hA_{p}", [P, FC, T], F32R) for p in "hl"]
        hB = [sb(f"hB_{p}", [P, 4, T], F32R) for p in "hl"]
        G = sb("G", [P, RING, T])
        Q = sb("Q", [P, RING, T])
        cx, ct, cs_, ch = [[sb(f"c{k}_{p}", [P, T], F32R) for p in "hl"] for k in "xtsh"]
        xT = sb("xT", [P, T])
        Ub = sb("Ub", [P, BB, KR])
        rows = sb("rows", [40, T])
        idx8 = sb("idx8", [NI, T], I32)
        condR = [sb(f"cond_{p}", [P, T], F32R) for p in "hl"]
        x1T = sb("x1T", [P, T])
        keep = sb("keep", [P, T])
        oh8 = sb("oh8", [NI, T], F32R)
        fin = [sb(f"fin_{p}", [P, T], F32R) for p in "hl"]
        gp = sb("gp", [P, TT, 2 * P])
        gc = sb("gc", [P, TT, 2 * P])
        gm = sb("gm", [P, TT, P])
        xh = sb("xh", [P, TT, P])
        tt = sb("tt", [P, TT, P])
        ss = sb("ss", [P, TT, P])
        hh = sb("hh", [P, TT, P])
        bn6 = sb("bn6", [P, 3, TT, 6])
        mv = sb("mv", [P, 3, TT, 2])
        ve = sb("ve", [P, 3, TT])
        rstd = sb("rstd", [P, 3, TT])
        gt = sb("gt", [P, TT, E])
        g1 = sb("g1", [P, 2, TT, E])
        gk = sb("gk", [P, 2, TT, E])
        gmx = sb("gmx", [P, 2, TT])
        gkx = sb("gkx", [P, 2, TT])
        gd = sb("gd", [P, TT])
        gth = sb("gth", [P, TT])
        gw2 = sb("gw2", [P, 2, TT])
        gw = sb("gw", [P, TT, E])
        ixb = sb("ixb", [P, 3, TT], I32)

        U_dram = nc.dram_tensor("U_scratch", [P, B * KR], F32, kind="Internal").ap()
        gw_dram = nc.dram_tensor("gw_scratch", [E, T], F32, kind="Internal").ap()

        ld_cond, ld_small, ld_state = sem("ld_cond"), sem("ld_small"), sem("ld_state")
        passed = sem("passed")
        ld_w = [sem(f"ld_w{i}") for i in range(6)]
        ones_row, u_mm, u_even, u_odd, u_stored, ident_r = (sem(n) for n in (
            "ones_row", "u_mm", "u_even", "u_odd", "u_stored", "ident_r"))
        w_hi, w_lo, small_src, small_hi, small_lo = (sem(n) for n in ("w_hi", "w_lo", "small_src", "small_hi", "small_lo"))
        aw_max, aw_exp, s_mm, sz_ready, s_th, sa_ready, sy_mm, sv_ready, srs_ready, sy_ready, syT_mm, syT_ready, wsc_ready, fold_mm, \
            ub_mm, dve_setup = (sem(n) for n in (
                "aw_max", "aw_exp", "s_mm", "sz_ready", "s_th", "sa_ready", "sy_mm", "sv_ready", "srs_ready", "sy_ready",
                "syT_mm", "syT_ready", "wsc_ready", "fold_mm", "ub_mm", "dve_setup"))
        x_in, u_in, t_mm, t_ready, cond_mm, cond_hi, cond_lo = (sem(n) for n in (
            "x_in", "u_in", "t_mm", "t_ready", "cond_mm", "cond_hi", "cond_lo"))
        gate_mm, gate_steps, gate_d, gate_th, gw_parts, gw_ready, gwT_mm, gwT_ready, gw_stored, gwb_in = (sem(n) for n in (
            "gate_mm", "gate_steps", "gate_d", "gate_th", "gw_parts", "gw_ready", "gwT_mm", "gwT_ready", "gw_stored", "gwb_in"))
        m_mm, m_gelu, m_mul, m_hi, m_lo, m_used, o_mm, x1_ready = (sem(n) for n in (
            "m_mm", "m_gelu", "m_mul", "m_hi", "m_lo", "m_used", "o_mm", "x1_ready"))
        x1_hi, x1_lo, xtok_mm, bn_steps, ve_ready, rstd_ready, xh_ready, ts_ready = (sem(n) for n in (
            "x1_hi", "x1_lo", "xtok_mm", "bn_steps", "ve_ready", "rstd_ready", "xh_ready", "ts_ready"))
        h_steps, h_ready, oh_ready, idx8_in, ixb_ready, gathered, kept = (sem(n) for n in (
            "h_steps", "h_ready", "oh_ready", "idx8_in", "ixb_ready", "gathered", "kept"))
        tr_mm, tr_hi, tr_lo, z_mm, z_th, a_ready, a_hi, a_lo, y_mm, yn_ready, yT_mm, f_full, f_hi, f_lo = (sem(n) for n in (
            "tr_mm", "tr_hi", "tr_lo", "z_mm", "z_th", "a_ready", "a_hi", "a_lo", "y_mm", "yn_ready", "yT_mm",
            "f_full", "f_hi", "f_lo"))
        n_mm, n_th, n_u, n_h, n_g, n_hi, n_lo, n_out, stored = (sem(n) for n in (
            "n_mm", "n_th", "n_u", "n_h", "n_g", "n_hi", "n_lo", "n_out", "stored"))

        NMM = 3 * FC + 1
        GATE_STEPS = 13
        NSET_W, NSMALL = 6, 6

        def settled(eng):
            eng.sem_inc(passed, 1)

        def flat(t):
            v = t[tuple(slice(None) for _ in t.shape)]
            return v if len(t.shape) == 2 else v.rearrange("p a b -> p (a b)")

        small_ops = [(wgf[:, :], (wg[0][:, :], wg[1][:, :])), (ib2f[:, :], (ib2[0][:, :], ib2[1][:, :])),
                     (wintf[:, :], (wint[0][:, :], wint[1][:, :])), (flat(wmixf), (flat(wmix[0]), flat(wmix[1]))),
                     (tab8f[:, :], (tab8[0][:, :], tab8[1][:, :])), (vecf[:, :], (vec[0][:, :], vec[1][:, :]))]

        block = ctx.enter_context(nc.Block())

        WINDOW = [("F", 0), ("A", 0), ("F", 1), ("C", 0), ("F", 2), ("A", 1), ("F", 3), ("A", 2),
                  ("F", 4), ("C", 1), ("F", 5), ("A", 3), ("F", 6), ("C", 2), ("F", 7), ("F", 8), ("C", 3),
                  ("F", 9), ("C", 4), ("F", 10), ("F", 11), ("C", 5), ("F", 12)]

        def window(stages, f=None, a=None, c=None):
            for kind, k in WINDOW:
                blk = {"F": f, "A": a, "C": c}[kind]
                if blk is not None:
                    stages[kind](blk, k)

        def schedule(eng, stages, M):
            window(stages, a=0)
            M(0)
            window(stages, a=1, c=0)
            M(1)
            window(stages, f=0, a=2, c=1)
            with eng.Fori(2, NB - 1) as i:
                M(i)
                window(stages, f=i - 1, a=i + 1, c=i)
            M(NB - 1)
            window(stages, f=NB - 2, c=NB - 1)
            window(stages, f=NB - 1)

        def first(b, n=1):
            return isinstance(b, int) and b < n

        @block.sync
        def _(sp):
            sp.dma_start(Wdec[0:MU, :], A["W_dec"]).then_inc(ld_cond, 16)
            sp.dma_start(Wdec[MU:MU + 1, :], A["b_dec"]).then_inc(ld_cond, 16)
            sp.dma_start(muT[0:MU, :], A["cond_512T"]).then_inc(ld_cond, 16)
            for dst, src in ((ident[:, :], "ident"), (Vw[:, :], "V"), (wgf[:, :], "WgT"), (b1c[:, :], "b1T"),
                             (b2e[32:40, :], "b2"), (iota8[:, :], "iota8"), (igb[:, :], "igb"),
                             (fsc[:, :], "fsc"), (ixp[:, :], "ixp"), (ixc[:, :], "ixc"), (ixm[:, :], "ixm"),
                             (ib2f[:, :], "int_b2"), (tbT[:, :, :], "tbT")):
                sp.dma_start(dst, A[src]).then_inc(ld_small, 16)
            for dst, src in ((bgt[:, :], "bg"), (desc8[:, :], "desc8")):
                sp.dma_start(dst, A[src].partition_broadcast(P)).then_inc(ld_small, 16)
            for n, (s_, w_) in enumerate((("cond_512T", "mem_W1"), ("cond_64T", "noi_W1"), ("sideT", "res_W1"))):
                k = A[s_].shape[0]
                sp.dma_start(sT[0:k, n, :], A[s_]).then_inc(ld_state, 16)
                sp.dma_start(sW1[0:k, n, :], A[w_]).then_inc(ld_state, 16)
            sp.dma_start(sW2[:, :, :], A["sW2"]).then_inc(ld_state, 16)
            sp.dma_start(sb1[:, :], A["sb1"]).then_inc(ld_state, 16)
            sp.dma_start(sbc[:, :, :, :], A["sbc"].partition_broadcast(P)).then_inc(ld_state, 16)
            sp.dma_start(iW1[:, :, :], A["int_W1"]).then_inc(ld_state, 16)
            sp.dma_start(ibb[:, :], A["int_b1"].partition_broadcast(P)).then_inc(ld_state, 16)
            sp.dma_start(aw6[:, :], A["aw"].partition_broadcast(P)).then_inc(ld_state, 16)
            sp.dma_start(iW2[:, :], A["int_W2"]).then_inc(ld_state, 16)
            for n, (src, width) in enumerate((("W1T", 2048), ("W2T", 2048), ("w12T", 1024), ("h1T", 2048),
                                              ("h2T", 2048), ("w3T", 512))):
                if n >= 2:
                    sp.wait_ge(w_lo, n - 1)
                sp.dma_start(stage[n % 2][:, 0:width], A[src]).then_inc(ld_w[n], 16)

            def load_x(b):
                if not first(b):
                    sp.wait_ge(x1_ready, b)
                sp.dma_start(xT[:, :], A["xT"][:, bass.ds(b * T, T)]).then_inc(x_in, 16)
                if not first(b):
                    sp.wait_ge(t_mm, b)
                sp.dma_start(Ub[:, :, :], U_dram[:, bass.ds(b * BB * KR, BB * KR)]).then_inc(u_in, 16)

            def load_idx(b):
                if not first(b):
                    sp.wait_ge(oh_ready, b)
                sp.dma_start(idx8[0:NC_, :], A["ic_row"][:, bass.ds(b * T, T)]
                             .partition_broadcast(NC_)).then_inc(idx8_in, 16)
                sp.dma_start(idx8[NC_:NI, :], A["im_row"][:, bass.ds(b * T, T)]
                             .partition_broadcast(NM_)).then_inc(idx8_in, 16)

            def spread_gw(b):
                sp.wait_ge(gwT_ready, b + 1)
                if not first(b):
                    sp.wait_ge(gwb_in, b * 16)
                    sp.wait_ge(m_mul, b * NH)
                sp.dma_start(gw_dram[:, :], rows[32:40, :]).then_inc(gw_stored, 16)
                sp.wait_ge(gw_stored, b * 16 + 16)
                sp.dma_start(gwb[:, :, :], gw_dram.partition_broadcast(P)).then_inc(gwb_in, 16)

            def store(b):
                sp.wait_ge(n_out, b + 1)
                sp.dma_start(out[:, bass.ds(b * T, T)], keep[:, :]).then_inc(stored, 16)

            sp.wait_ge(u_even, KR // 2)
            sp.wait_ge(u_odd, KR // 2)
            sp.dma_start(U_dram[:, :], Uall[:, :, :]).then_inc(u_stored, 16)
            sp.wait_ge(u_stored, 16)
            load_x(0)
            load_idx(0)
            sp.wait_ge(w_lo, NSET_W)
            sp.wait_ge(small_lo, NSMALL)
            spread_gw(0)
            load_x(1)
            spread_gw(1)
            load_idx(1)
            load_x(2)
            spread_gw(2)
            load_idx(2)
            store(0)
            with sp.Fori(2, NB - 1) as i:
                load_x(i + 1)
                spread_gw(i + 1)
                load_idx(i + 1)
                store(i - 1)
            store(NB - 2)
            store(NB - 1)
            sp.wait_ge(stored, 16 * NB)

        @block.tensor
        def _(pe):
            pe.wait_ge(ld_cond, 48)
            pe.wait_ge(ones_row, 1)
            wd = Wdec[:, :].rearrange("m (i k) -> m i k", k=KR)
            for k in range(KR):
                if k >= 4:
                    pe.wait_ge(u_odd if k % 2 else u_even, k // 2 - 1)
                pe.matmul(HB[k % 4][:, 0:B], wd[:, 0:D, k], muT[:, :], start=True, stop=True).then_inc(u_mm, 1)
            pe.matmul(X0[0:KR, 0:B], wd[:, D, :], muT[:, :], start=True, stop=True).then_inc(ub_mm, 1)
            pe.wait_ge(ld_state, 16 * 13)
            for n, k in enumerate((64, 64, 32)):
                mm = pe.matmul(X1[:, n * B:(n + 1) * B], sW1[0:k, n, :], sT[0:k, n, :], start=True, stop=True)
            mm.then_inc(s_mm, 1)
            pe.wait_ge(sa_ready, 1)
            for n in range(3):
                mm = pe.matmul(X2[:, n * P:(n + 1) * P], sa[:, n * B:(n + 1) * B], sW2[:, n, :], start=True, stop=True)
            mm.then_inc(sy_mm, 1)
            pe.wait_ge(sy_ready, 1)
            pe.wait_ge(ld_small, 16 * 15)
            for n in range(3):
                mm = pe.transpose(X1[:, n * P:(n + 1) * P], sy[:, n, :], ident[:, :])
            mm.then_inc(syT_mm, 1)
            pe.wait_ge(syT_ready, 1)
            pe.wait_ge(wsc_ready, 1)
            for n in range(3):
                pe.matmul(X2[:, 0:P], syT[:, n * B:(n + 1) * B], wsc[:, 2 + n, :], start=(n == 0), stop=(n == 2))
            for n, w_ in enumerate((0, 1, 5)):
                mm = pe.matmul(OACC[0:NI, 0:P], tbT[:, n, :], wsc[:, w_, :], start=(n == 0), stop=(n == 2))
            mm.then_inc(fold_mm, 1)
            pe.wait_ge(small_lo, NSMALL)

            def A_stage(b, k):
                if k == 0:
                    pe.wait_ge(x_in, b * 16 + 16)
                    pe.wait_ge(u_in, b * 16 + 16)
                    if not first(b):
                        pe.wait_ge(gwT_ready, b)
                    for j in range(BB):
                        mm = pe.matmul(X0[0:KR, j * S:(j + 1) * S], Ub[:, j, :], xT[:, j * S:(j + 1) * S],
                                       start=True, stop=True)
                    mm.then_inc(t_mm, 1)
                elif k == 1:
                    pe.wait_ge(t_ready, b + 1)
                    if not first(b):
                        pe.wait_ge(x1_ready, b)
                    pe.matmul(OACC[:, :], Vw[:, :], rows[0:KR, :], start=True, stop=True).then_inc(cond_mm, 1)
                elif k == 2:
                    pe.wait_ge(cond_lo, b + 1)
                    for t in range(TT):
                        for n, (a, w_) in enumerate(((0, 0), (0, 1), (1, 0))):
                            mm = pe.matmul(X0[:, t * E:(t + 1) * E], condR[a][:, t * P:(t + 1) * P], wg[w_][:, :],
                                           start=(n == 0), stop=(n == 2))
                    mm.then_inc(gate_mm, 1)
                else:
                    pe.wait_ge(gw_ready, b + 1)
                    for t in range(TT):
                        mm = pe.transpose(X0[0:E, t * P:(t + 1) * P], gw[:, t, :], ident[:, :])
                    mm.then_inc(gwT_mm, 1)

            def M(b):
                lag = 3
                pe.wait_ge(gwT_ready, b + 1)
                pe.wait_ge(cond_lo, b + 1)
                pe.matmul(OACC[:, :], b2e[32:40, :], rows[32:40, :], start=True, stop=False)
                for c in range(NH + lag):
                    if c < NH:
                        if c >= 4:
                            pe.wait_ge(m_gelu, b * NH + c - 3)
                        elif not first(b, 2):
                            if c == 0:
                                pe.wait_ge(n_out, b - 1)
                            pe.wait_ge(n_g, (b - 1) * 2 * FC)
                        for n, (a, x_) in enumerate(((0, 0), (0, 1), (1, 0))):
                            mm = pe.matmul(HB[c % 4][:, :], W1[a][:, c * P:(c + 1) * P], condR[x_][:, :],
                                           start=(n == 0), stop=(n == 2))
                        mm.then_inc(m_mm, 1)
                    if c >= lag:
                        q = c - lag
                        pe.wait_ge(m_lo, b * NH + q + 1)
                        for n, (a, x_) in enumerate(((0, 0), (1, 0), (0, 1))):
                            mm = pe.matmul(OACC[:, :], W2[a][:, q, :], hB[x_][:, q % 4, :],
                                           start=False, stop=(q == NH - 1 and n == 2))
                        mm.then_inc(m_used, 1)

            def C_stage(b, k):
                if k == 0:
                    pe.wait_ge(x1_ready, b + 1)
                    if not first(b):
                        pe.wait_ge(f_full, b)
                    for t in range(TT):
                        mm = pe.transpose(X1[:, t * P:(t + 1) * P], x1T[:, t * P:(t + 1) * P], ident[:, :])
                    mm.then_inc(xtok_mm, 1)
                elif k == 2:
                    for n, (src, dst) in enumerate(((tt, X2), (ss, X1), (hh, X2))):
                        if n == 0:
                            pe.wait_ge(ts_ready, b * 2 + 1)
                            if not first(b):
                                pe.wait_ge(yn_ready, b)
                        elif n == 1:
                            pe.wait_ge(ts_ready, b * 2 + 2)
                            pe.wait_ge(xh_ready, b + 1)
                        else:
                            pe.wait_ge(h_ready, b + 1)
                            pe.wait_ge(tr_lo, b * 3 + 1)
                        for t in range(TT):
                            mm = pe.transpose(dst[:, t * P:(t + 1) * P], src[:, t, :], ident[:, :])
                        mm.then_inc(tr_mm, 1)
                elif k == 3:
                    pe.wait_ge(tr_lo, b * 3 + 2)
                    seqs = identR[:, bass.ds(b * BB, BB)].unsqueeze(2).broadcast_to([P, BB, S])
                    pe.matmul(X1[:, :], vec[0][:, :], seqs, start=True, stop=False)
                    pe.matmul(X1[:, :], vec[1][:, :], seqs, start=False, stop=False)
                    pe.wait_ge(oh_ready, b + 1)
                    pe.matmul(X1[:, :], tab8[0][:, :], oh8[0:NI, :], start=False, stop=False)
                    pe.matmul(X1[:, :], tab8[1][:, :], oh8[0:NI, :], start=False, stop=False)
                    pe.wait_ge(x1_lo, b + 1)
                    for m, src in enumerate((cx, ct, cs_, ch)):
                        if m == 3:
                            pe.wait_ge(tr_lo, b * 3 + 3)
                        for n, (a, x_) in enumerate(((0, 0), (0, 1), (1, 0))):
                            mm = pe.matmul(X1[:, :], wmix[a][:, m, :], src[x_][:, :],
                                           start=False, stop=(m == 3 and n == 2))
                    mm.then_inc(z_mm, 1)
                elif k == 4:
                    pe.wait_ge(a_lo, b + 1)
                    for t in range(TT):
                        o = X2[:, t * P:(t + 1) * P]
                        pe.matmul(o, onesR[:, :], ib2[0][:, :], start=True, stop=False)
                        pe.matmul(o, onesR[:, :], ib2[1][:, :], start=False, stop=False)
                        for n, (x_, a) in enumerate(((0, 0), (0, 1), (1, 0))):
                            mm = pe.matmul(o, ct[x_][:, t * P:(t + 1) * P], wint[a][:, :], start=False, stop=(n == 2))
                    mm.then_inc(y_mm, 1)
                elif k == 5:
                    pe.wait_ge(yn_ready, b + 1)
                    pe.wait_ge(a_ready, b + 1)
                    for t in range(TT):
                        mm = pe.transpose(X1[:, t * P:(t + 1) * P], hh[:, t, :], ident[:, :])
                    mm.then_inc(yT_mm, 1)

            def F_stage(b, k):
                last = isinstance(b, int) and b == NB - 1
                if k < FC:
                    if k == 0:
                        pe.wait_ge(f_lo, b + 1)
                        if last:
                            pe.wait_ge(n_out, b)
                            pe.wait_ge(n_g, b * 2 * FC)
                        else:
                            pe.wait_ge(m_gelu, (b + 2) * NH)
                    elif k >= 2:
                        pe.wait_ge(n_h, b * FC + k - 1)
                    for w_ in range(2):
                        o = HB[2 * (k % 2) + w_]
                        for n, (a, x_) in enumerate(((0, 0), (0, 1), (1, 0))):
                            mm = pe.matmul(o[:, :], w12[a][:, w_, k * P:(k + 1) * P], fin[x_][:, :],
                                           start=(n == 0), stop=(n == 2))
                    mm.then_inc(n_mm, 1)
                    return
                layer, c = (k // FC, k % FC)
                w, src = ((h1w, hA), (h2w, hB), (w3, hA))[layer - 1]
                if layer == 1:
                    pe.wait_ge(n_h, b * FC + (3 if c < 2 else 4))
                elif layer == 2:
                    pe.wait_ge(n_g, b * 2 * FC + c + 1)
                else:
                    pe.wait_ge(n_g, b * 2 * FC + FC + 1)
                for kc in range(FC):
                    if c == 0:
                        pe.wait_ge(n_lo, b * 3 * FC + (layer - 1) * FC + kc + 1)
                    for n, (a, x_) in enumerate(((0, 0), (0, 1), (1, 0))):
                        mm = pe.matmul(HB[c][:, :], w[a][:, kc, c * P:(c + 1) * P], src[x_][:, kc, :],
                                       start=(kc == 0 and n == 0), stop=(kc == FC - 1 and n == 2))
                mm.then_inc(n_mm, 1)

            schedule(pe, {"A": A_stage, "C": C_stage, "F": F_stage}, M)

        @block.scalar
        def _(act):
            act.wait_ge(aw_max, 1)
            act.activation(aw_e[:, :], aw6[:, :], ACT.Exp, bias=awx[:, 1:2], accum_out=awx[:, 2:3]).then_inc(aw_exp, 1)
            for k in range(1, KR, 2):
                act.wait_ge(u_mm, k + 1)
                act.activation(Uall[:, :, k], HB[k % 4][:, 0:B], ACT.Copy).then_inc(u_odd, 1)
            act.wait_ge(sz_ready, 1)
            act.activation(sth[:, :], sz[:, :], ACT.Tanh, scale=0.5).then_inc(s_th, 1)

            def big_hi(n, dst):
                act.wait_ge(ld_w[n], 16)
                act.activation(dst, stage[n % 2][:, 0:dst.free_size()], ACT.Copy).then_inc(w_hi, 1)

            big_hi(0, W1[0][:, :])
            big_hi(1, flat(W2[0]))
            act.wait_ge(syT_mm, 1)
            act.activation(syT[:, :], X1[:, 0:3 * B], ACT.Copy).then_inc(syT_ready, 1)
            act.activation(identR[:, :], ident[:, :], ACT.Copy).then_inc(ident_r, 1)
            big_hi(2, flat(w12[0]))
            for n, (src, dst) in enumerate(small_ops):
                act.wait_ge(small_src, n + 1)
                act.activation(dst[0], src, ACT.Copy).then_inc(small_hi, 1)
            big_hi(3, flat(h1w[0]))
            big_hi(4, flat(h2w[0]))
            big_hi(5, flat(w3[0]))

            def A_stage(b, k):
                if k == 1:
                    act.wait_ge(cond_mm, b + 1)
                    if not first(b):
                        act.wait_ge(m_mm, b * NH)
                    act.activation(condR[0][:, :], OACC[:, :], ACT.Copy).then_inc(cond_hi, 1)
                elif k == 2:
                    act.wait_ge(gate_d, b + 1)
                    act.activation(gth[:, :], gd[:, :], ACT.Tanh, scale=0.5).then_inc(gate_th, 1)
                elif k == 3:
                    act.wait_ge(gwT_mm, b + 1)
                    if not first(b):
                        act.wait_ge(gw_stored, b * 16)
                        act.wait_ge(m_mm, b * NH)
                    act.activation(rows[32:40, :], X0[0:E, :], ACT.Copy).then_inc(gwT_ready, 1)

            def M(b):
                def hi(c):
                    act.wait_ge(m_mul, b * NH + c + 1)
                    if c >= 4:
                        act.wait_ge(m_used, b * NH + c - 3)
                    elif not first(b, 2):
                        act.wait_ge(n_mm, (b - 1) * NMM)
                    act.activation(hB[0][:, c % 4, :], Q[:, c % RING, :], ACT.Copy).then_inc(m_hi, 1)

                if first(b):
                    act.wait_ge(w_lo, NSET_W)
                    act.wait_ge(small_lo, NSMALL)
                elif not first(b, 2):
                    act.wait_ge(n_lo, (b - 1) * 3 * FC)
                for c in range(NH):
                    act.wait_ge(m_mm, b * NH + c + 1)
                    if c >= RING:
                        act.wait_ge(m_mul, b * NH + c - RING + 1)
                    act.activation(G[:, c % RING, :], HB[c % 4][:, :], ACT.Gelu, bias=b1c[:, c:c + 1]).then_inc(m_gelu, 1)
                    if c >= 1:
                        hi(c - 1)
                hi(NH - 1)

            def C_stage(b, k):
                if k == 0:
                    act.wait_ge(x1_ready, b + 1)
                    if not first(b):
                        act.wait_ge(z_mm, b)
                    act.activation(cx[0][:, :], x1T[:, :], ACT.Copy).then_inc(x1_hi, 1)
                elif k == 2:
                    for n, (src, dst) in enumerate(((X2, ct), (X1, cs_), (X2, ch))):
                        act.wait_ge(tr_mm, b * 3 + n + 1)
                        if n == 0 and not first(b):
                            act.wait_ge(y_mm, b)
                        act.activation(dst[0][:, :], src[:, :], ACT.Copy).then_inc(tr_hi, 1)
                elif k == 3:
                    act.wait_ge(z_mm, b + 1)
                    act.activation(flat(tt), X1[:, :], ACT.Tanh, scale=0.5).then_inc(z_th, 1)
                    act.wait_ge(a_ready, b + 1)
                    act.activation(ct[0][:, :], flat(ss), ACT.Copy).then_inc(a_hi, 1)
                elif k == 5:
                    act.wait_ge(f_full, b + 1)
                    act.activation(fin[0][:, :], flat(xh), ACT.Copy).then_inc(f_hi, 1)

            def F_stage(b, k):
                if k < FC:
                    def hi(c):
                        act.wait_ge(n_h, b * FC + c + 1)
                        act.activation(hA[0][:, c, :], Q[:, c % RING, :], ACT.Copy).then_inc(n_hi, 1)
                    act.wait_ge(n_mm, b * NMM + k + 1)
                    if k == 0 and not first(b):
                        act.wait_ge(n_lo, b * 3 * FC)
                    if k >= RING:
                        act.wait_ge(n_h, b * FC + k - RING + 1)
                    act.activation(G[:, k % RING, :], HB[2 * (k % 2)][:, :], ACT.Tanh, scale=hs1[:, k:k + 1]).then_inc(n_th, 1)
                    if k >= 1:
                        hi(k - 1)
                    if k == FC - 1:
                        hi(k)
                elif k < 3 * FC:
                    c = k % FC
                    dst = hB if k < 2 * FC else hA
                    act.wait_ge(n_mm, b * NMM + k + 1)
                    act.wait_ge(n_lo, b * 3 * FC + k - RING + 1)
                    act.activation(G[:, k % RING, :], HB[c][:, :], ACT.Gelu, scale=fsc[:, k + FC:k + FC + 1])\
                       .then_inc(n_g, 1)
                    act.wait_ge(n_g, b * 2 * FC + k - FC + 1)
                    act.activation(dst[0][:, c, :], G[:, k % RING, :], ACT.Copy).then_inc(n_hi, 1)

            schedule(act, {"A": A_stage, "C": C_stage, "F": F_stage}, M)

        @block.vector
        def _(dve):
            dve.memset(muT[MU:MU + 1, :], 1.0)
            dve.memset(onesf[:, :], 1.0)
            dve.memset(mhalf[:, :], -0.5).then_inc(ones_row, 1)
            dve.wait_ge(ones_row, 1)
            dve.tensor_copy(onesR[:, :], onesf[:, :])
            step = Steps(dve, dve_setup, 0, 0)
            dve.wait_ge(ld_state, 16 * 13)
            step(dve.reduce_max(awx[:, 0:1], aw6[:, :], AX_X))
            dve.tensor_scalar(awx[:, 1:2], awx[:, 0:1], -1.0, None, ALU.mult).then_inc(aw_max, 1)
            for k in range(0, KR, 2):
                dve.wait_ge(u_mm, k + 1)
                dve.tensor_copy(Uall[:, :, k], HB[k % 4][:, 0:B]).then_inc(u_even, 1)
            dve.wait_ge(ub_mm, 1)
            dve.tensor_copy(ub[:, :], X0[0:KR, 0:B])
            dve.wait_ge(s_mm, 1)
            for n in range(3):
                last = dve.tensor_scalar(sz[:, n * B:(n + 1) * B], X1[:, n * B:(n + 1) * B], sb1[:, n:n + 1], None, ALU.add)
            last.then_inc(sz_ready, 1)
            dve.wait_ge(aw_exp, 1)
            step(dve.reciprocal(awx[:, 3:4], awx[:, 2:3]))
            step(dve.tensor_scalar(aw_e[:, :], aw_e[:, :], awx[:, 3:4], None, ALU.mult))
            for n in range(6):
                last = dve.tensor_scalar(wsc[:, n, :], iW1[:, n, :], aw_e[:, n:n + 1], None, ALU.mult)
            last.then_inc(wsc_ready, 1)
            dve.wait_ge(s_th, 1)
            step(dve.scalar_tensor_tensor(out=sa[:, :], in0=sth[:, :], scalar=1.0, in1=sz[:, :], op0=ALU.add, op1=ALU.mult))
            dve.tensor_scalar(sa[:, :], sa[:, :], 0.5, None, ALU.mult).then_inc(sa_ready, 1)
            dve.wait_ge(sy_mm, 1)
            step(dve.tensor_tensor(sy[:, :, :], X2[:, 0:3 * P].rearrange("p (n d) -> p n d", n=3), sbc[:, 0, :, :], ALU.add))
            for n in range(3):
                ins = dve.bn_stats(sbn[:, n, :], sy[:, n, :])
            step(ins)
            for n in range(3):
                ins = dve.bn_aggr(smv[:, n, :], sbn[:, n, :])
            step(ins)
            dve.tensor_scalar(sve[:, :], smv[:, :, 1], EPS, None, ALU.add).then_inc(sv_ready, 1)
            dve.wait_ge(srs_ready, 1)
            for n in range(3):
                ins = dve.tensor_scalar(sy[:, n, :], sy[:, n, :], smv[:, n, 0:1], srs[:, n:n + 1], ALU.subtract, ALU.mult)
            step(ins)
            step(dve.tensor_tensor(sy[:, :, :], sy[:, :, :], sbc[:, 1, :, :], ALU.mult))
            dve.tensor_tensor(sy[:, :, :], sy[:, :, :], sbc[:, 2, :, :], ALU.add).then_inc(sy_ready, 1)
            dve.wait_ge(ld_small, 16 * 15)
            dve.tensor_scalar(wintf[:, :], iW2[:, :], 0.5, None, ALU.mult).then_inc(small_src, 3)
            dve.wait_ge(wsc_ready, 1)
            step(dve.tensor_tensor(wmixf[:, 0, :], wsc[:, 2, :], wsc[:, 3, :], ALU.add))
            dve.tensor_tensor(wmixf[:, 0, :], wmixf[:, 0, :], wsc[:, 4, :], ALU.add)
            dve.tensor_copy(wmixf[:, 1, :], wsc[:, 1, :])
            dve.tensor_copy(wmixf[:, 2, :], wsc[:, 5, :])
            dve.tensor_copy(wmixf[:, 3, :], wsc[:, 0, :]).then_inc(small_src, 1)
            step(dve.tensor_scalar(hs1[:, :], fsc[:, 0:FC], 0.5, None, ALU.mult))
            dve.tensor_tensor(cs12[:, :], hs1[:, :], fsc[:, FC:2 * FC], ALU.mult)
            dve.wait_ge(fold_mm, 1)
            dve.tensor_copy(tab8f[:, :], OACC[0:NI, 0:P]).then_inc(small_src, 1)
            dve.tensor_tensor(vecf[:, :], X2[:, 0:P], ibb[:, :], ALU.add).then_inc(small_src, 1)

            def big_lo(n, w):
                dve.wait_ge(w_hi, n + 1)
                dst = flat(w[1])
                dve.tensor_tensor(dst, stage[n % 2][:, 0:dst.free_size()], flat(w[0]).bitcast(F32), ALU.subtract)\
                   .then_inc(w_lo, 1)

            big_lo(0, W1)
            big_lo(1, W2)
            for n, (src, dst) in enumerate(small_ops):
                dve.wait_ge(small_hi, n + 1)
                dve.tensor_tensor(dst[1], src, dst[0].bitcast(F32), ALU.subtract).then_inc(small_lo, 1)
            for n, w in ((2, w12), (3, h1w), (4, h2w), (5, w3)):
                big_lo(n, w)

            def layer_norm(b, n, src, dst, step):
                for t in range(TT):
                    ins = dve.bn_stats(bn6[:, n, t, :], src(t))
                step(ins)
                settled(dve)
                for t in range(TT):
                    ins = dve.bn_aggr(mv[:, n, t, :], bn6[:, n, t, :])
                step(ins)
                dve.tensor_scalar(ve[:, n, :], mv[:, n, :, 1], EPS, None, ALU.add).then_inc(ve_ready, 1)
                dve.wait_ge(rstd_ready, b * 3 + n + 1)
                for t in range(TT):
                    ins = dve.tensor_scalar(dst[:, t, :], src(t), mv[:, n, t, 0:1], rstd[:, n, t:t + 1],
                                            ALU.subtract, ALU.mult)
                return ins

            def per_tile(v):
                return v.unsqueeze(2).broadcast_to([P, TT, E])

            def A_stage(b, k):
                if k == 0:
                    dve.wait_ge(t_mm, b + 1)
                    if not first(b):
                        dve.wait_ge(cond_mm, b)
                    dve.tensor_tensor(rows[0:KR, :].rearrange("k (b s) -> k b s", b=BB),
                                      X0[0:KR, :].rearrange("k (b s) -> k b s", b=BB),
                                      ub[:, bass.ds(b * BB, BB)].unsqueeze(2).broadcast_to([KR, BB, S]), ALU.add)\
                       .then_inc(t_ready, 1)
                elif k == 1:
                    dve.wait_ge(cond_hi, b + 1)
                    dve.tensor_tensor(condR[1][:, :], OACC[:, :], condR[0][:, :].bitcast(F32), ALU.subtract)\
                       .then_inc(cond_lo, 1)
                elif k == 2:
                    step = Steps(dve, gate_steps, GATE_STEPS, b)
                    dve.wait_ge(gate_mm, b + 1)
                    if not first(b):
                        dve.wait_ge(gw_ready, b)
                    step(dve.tensor_tensor(gt[:, :, :], X0[:, 0:TT * E].rearrange("p (t e) -> p t e", t=TT),
                                           bgt[:, :].unsqueeze(1).broadcast_to([P, TT, E]), ALU.add))
                    for r in range(2):
                        step(dve.reduce_max(gmx[:, r, :], gt[:, :, :], AX_X))
                        step(dve.tensor_tensor(gk[:, r, :, :], gt[:, :, :], per_tile(gmx[:, r, :]), ALU.is_equal))
                        step(dve.tensor_tensor(gk[:, r, :, :], gk[:, r, :, :],
                                               desc8[:, :].unsqueeze(1).broadcast_to([P, TT, E]), ALU.mult))
                        step(dve.reduce_max(gkx[:, r, :], gk[:, r, :, :], AX_X))
                        step(dve.tensor_tensor(g1[:, r, :, :], gk[:, r, :, :], per_tile(gkx[:, r, :]), ALU.is_equal))
                        if r == 0:
                            step(dve.scalar_tensor_tensor(out=gt[:, :, :], in0=g1[:, 0, :, :], scalar=MASKED,
                                                          in1=gt[:, :, :], op0=ALU.mult, op1=ALU.add))
                    dve.tensor_tensor(gd[:, :], gmx[:, 0, :], gmx[:, 1, :], ALU.subtract).then_inc(gate_d, 1)
                    dve.wait_ge(gate_th, b + 1)
                    dve.tensor_scalar(gw2[:, 0, :], gth[:, :], 0.5, 0.5, ALU.mult, ALU.add)
                    step(dve.tensor_scalar(gw2[:, 1, :], gth[:, :], -0.5, 0.5, ALU.mult, ALU.add))
                    for r in range(2):
                        ins = dve.tensor_tensor(g1[:, r, :, :], g1[:, r, :, :], per_tile(gw2[:, r, :]), ALU.mult)
                    ins.then_inc(gw_parts, 1)
                    dve.wait_ge(gw_parts, b + 1)
                    if not first(b):
                        dve.wait_ge(gwT_mm, b)
                    dve.tensor_tensor(gw[:, :, :], g1[:, 0, :, :], g1[:, 1, :, :], ALU.add).then_inc(gw_ready, 1)
                    step.end()

            def M(b):
                def lo(c):
                    dve.wait_ge(m_hi, b * NH + c + 1)
                    dve.tensor_tensor(hB[1][:, c % 4, :], Q[:, c % RING, :], hB[0][:, c % 4, :].bitcast(F32), ALU.subtract)\
                       .then_inc(m_lo, 1)

                dve.wait_ge(gwb_in, b * 16 + 16)
                if not first(b, 2):
                    dve.wait_ge(n_lo, (b - 1) * 3 * FC)
                for c in range(NH):
                    dve.wait_ge(m_gelu, b * NH + c + 1)
                    if c >= RING:
                        dve.wait_ge(m_lo, b * NH + c - RING + 1)
                    dve.tensor_tensor(Q[:, c % RING, :], G[:, c % RING, :], gwb[:, c // HE, :], ALU.mult).then_inc(m_mul, 1)
                    if c >= 1:
                        lo(c - 1)
                lo(NH - 1)
                dve.wait_ge(m_used, b * NH + NH)
                dve.wait_ge(x_in, b * 16 + 16)
                if not first(b):
                    dve.wait_ge(kept, b)
                    dve.wait_ge(xtok_mm, b)
                dve.tensor_tensor(x1T[:, :], OACC[:, :], xT[:, :], ALU.add).then_inc(x1_ready, 1)

            def C_stage(b, k):
                if k == 0:
                    dve.wait_ge(x1_hi, b + 1)
                    dve.tensor_tensor(cx[1][:, :], x1T[:, :], cx[0][:, :].bitcast(F32), ALU.subtract).then_inc(x1_lo, 1)
                    step = Steps(dve, bn_steps, 6, b)
                    if not first(b):
                        dve.wait_ge(f_lo, b)
                    dve.wait_ge(xtok_mm, b + 1)
                    if not first(b):
                        dve.wait_ge(ts_ready, b * 2)
                        dve.wait_ge(f_hi, b)
                    layer_norm(b, 0, lambda t: X1[:, t * P:(t + 1) * P], xh, step).then_inc(xh_ready, 1)
                elif k == 1:
                    step = Steps(dve, h_steps, 3, b)
                    dve.wait_ge(xh_ready, b + 1)
                    dve.wait_ge(gathered, (b + 1) * 16 * 3 * TT)
                    if not first(b):
                        dve.wait_ge(yT_mm, b)
                    step(dve.tensor_tensor(hh[:, :, :], xh[:, :, :], gp[:, :, 0:P], ALU.mult))
                    step(dve.tensor_tensor(hh[:, :, :], hh[:, :, :], gp[:, :, P:2 * P], ALU.add))
                    step2 = Steps(dve, bn_steps, 6, b)
                    step2.k = 2
                    step(layer_norm(b, 1, lambda t: hh[:, t, :], hh, step2))
                    dve.tensor_tensor(hh[:, :, :], hh[:, :, :], gc[:, :, 0:P], ALU.mult).then_inc(h_ready, 1)
                    step.end()
                    dve.wait_ge(idx8_in, (b + 1) * 32)
                    dve.tensor_scalar(oh8[:, :], idx8[:, :], iota8[:, :], None, ALU.is_equal).then_inc(oh_ready, 1)
                elif k == 2:
                    for n, (src, dst) in enumerate(((X2, ct), (X1, cs_), (X2, ch))):
                        dve.wait_ge(tr_hi, b * 3 + n + 1)
                        dve.tensor_tensor(dst[1][:, :], src[:, :], dst[0][:, :].bitcast(F32), ALU.subtract)\
                           .then_inc(tr_lo, 1)
                elif k == 3:
                    dve.wait_ge(z_th, b + 1)
                    dve.scalar_tensor_tensor(out=flat(ss), in0=flat(tt), scalar=1.0, in1=X1[:, :],
                                             op0=ALU.add, op1=ALU.mult).then_inc(a_ready, 1)
                    dve.wait_ge(a_hi, b + 1)
                    dve.tensor_tensor(ct[1][:, :], flat(ss), ct[0][:, :].bitcast(F32), ALU.subtract).then_inc(a_lo, 1)
                elif k == 4:
                    step = Steps(dve, bn_steps, 6, b)
                    step.k = 4
                    dve.wait_ge(y_mm, b + 1)
                    layer_norm(b, 2, lambda t: X2[:, t * P:(t + 1) * P], hh, step).then_inc(yn_ready, 1)
                    step.end()
                elif k == 5:
                    dve.wait_ge(yT_mm, b + 1)
                    dve.tensor_scalar(flat(xh), X1[:, :], igb[:, 0:1], igb[:, 1:2], ALU.mult, ALU.add).then_inc(f_full, 1)
                    dve.wait_ge(f_hi, b + 1)
                    dve.tensor_tensor(fin[1][:, :], flat(xh), fin[0][:, :].bitcast(F32), ALU.subtract).then_inc(f_lo, 1)

            def F_stage(b, k):
                if k < FC:
                    def lo(c):
                        dve.wait_ge(n_hi, b * 3 * FC + c + 1)
                        dve.tensor_tensor(hA[1][:, c, :], Q[:, c % RING, :], hA[0][:, c, :].bitcast(F32), ALU.subtract)\
                           .then_inc(n_lo, 1)
                    dve.wait_ge(n_th, b * FC + k + 1)
                    if k == 0:
                        last = isinstance(b, int) and b == NB - 1
                        dve.wait_ge(n_lo, b * 3 * FC) if last else dve.wait_ge(m_lo, (b + 2) * NH)
                    elif k >= RING:
                        dve.wait_ge(n_lo, b * 3 * FC + k - RING + 1)
                    dve.scalar_tensor_tensor(out=Q[:, k % RING, :], in0=G[:, k % RING, :], scalar=1.0,
                                             in1=HB[2 * (k % 2)][:, :], op0=ALU.add, op1=ALU.mult).then_inc(n_u, 1)
                    dve.wait_ge(n_u, b * FC + k + 1)
                    dve.scalar_tensor_tensor(out=Q[:, k % RING, :], in0=Q[:, k % RING, :], scalar=cs12[:, k:k + 1],
                                             in1=HB[2 * (k % 2) + 1][:, :], op0=ALU.mult, op1=ALU.mult).then_inc(n_h, 1)
                    if k >= 1:
                        lo(k - 1)
                    if k == FC - 1:
                        lo(k)
                elif k < 3 * FC:
                    c = k % FC
                    dst = hB if k < 2 * FC else hA
                    dve.wait_ge(n_hi, b * 3 * FC + k + 1)
                    dve.tensor_tensor(dst[1][:, c, :], G[:, k % RING, :], dst[0][:, c, :].bitcast(F32), ALU.subtract)\
                       .then_inc(n_lo, 1)
                else:
                    dve.wait_ge(n_mm, b * NMM + NMM)
                    dve.wait_ge(kept, b + 1)
                    dve.scalar_tensor_tensor(out=keep[:, :], in0=HB[0][:, :], scalar=fsc[:, 4 * FC:4 * FC + 1],
                                             in1=keep[:, :], op0=ALU.mult, op1=ALU.add).then_inc(n_out, 1)

            schedule(dve, {"A": A_stage, "C": C_stage, "F": F_stage}, M)

        @block.gpsimd
        def _(pool):
            def gather(b):
                settled(pool)
                for n, ix in enumerate((ixp, ixc, ixm)):
                    ins = pool.tensor_copy(ixb[:, n, :], ix[:, bass.ds(b * TT, TT)])
                ins.then_inc(ixb_ready, 1)
                pool.wait_ge(ixb_ready, b + 1)
                settled(pool)
                for t in range(TT):
                    for n, (dst, src) in enumerate(((gp, "pgb"), (gc, "ctg"), (gm, "msg"))):
                        pool.indirect_dma_start(out=dst[:, t, :], out_offset=None, in_=A[src],
                                                in_offset=bass.IndirectOffsetOnAxis(ap=ixb[:, n, t:t + 1].bitcast(U32), axis=0))\
                            .then_inc(gathered, 16)

            def pow_(b, n):
                pool.wait_ge(ve_ready, b * 3 + n + 1)
                pool.tensor_tensor(rstd[:, n, :], ve[:, n, :], mhalf[:, :], ALU.pow).then_inc(rstd_ready, 1)

            pool.wait_ge(sv_ready, 1)
            pool.tensor_tensor(srs[:, :], sve[:, :], mhalf[:, 0:3], ALU.pow).then_inc(srs_ready, 1)
            pool.wait_ge(ld_small, 16 * 15)
            gather(0)

            def C_stage(b, k):
                if k == 0:
                    pow_(b, 0)
                elif k == 1:
                    pool.wait_ge(gathered, (b + 1) * 16 * 3 * TT)
                    pool.wait_ge(xh_ready, b + 1)
                    if not first(b):
                        pool.wait_ge(a_lo, b)
                    pool.tensor_tensor(tt[:, :, :], xh[:, :, :], gc[:, :, P:2 * P], ALU.mult).then_inc(ts_ready, 1)
                    pow_(b, 1)
                    pool.tensor_tensor(ss[:, :, :], xh[:, :, :], gm[:, :, :], ALU.mult).then_inc(ts_ready, 1)
                elif k == 2:
                    if not (isinstance(b, int) and b == NB - 1):
                        pool.wait_ge(h_ready, b + 1)
                        pool.wait_ge(ts_ready, b * 2 + 2)
                        gather(b + 1)
                elif k == 4:
                    pow_(b, 2)

            def F_stage(b, k):
                pass

            def A_stage(b, k):
                pass

            def keep_x(b):
                if not first(b):
                    pool.wait_ge(stored, b * 16)
                pool.wait_ge(x1_ready, b + 1)
                settled(pool)
                pool.tensor_copy(keep[:, :], x1T[:, :]).then_inc(kept, 1)

            st = {"A": A_stage, "C": C_stage, "F": F_stage}
            window(st, c=0)
            keep_x(0)
            with pool.Fori(1, NB - 1) as i:
                window(st, c=i)
                keep_x(i)
            window(st, c=NB - 1)
            keep_x(NB - 1)


def kernel(**inputs):
    import numpy as np
    import concourse.bacc as bacc
    from concourse.bass_utils import run_bass_kernel_spmd as run

    g = {k: np.asarray(v) for k, v in inputs.items()}
    c1, f1, f0 = "L1_cond_", "L1_ffn_", "L0_ffn_"
    n = P

    def chunks(w):
        return w.reshape(-1, n, w.shape[1]).transpose(1, 0, 2).reshape(n, -1)

    def tiles(ix):
        return ix.reshape(-1, n).T

    zero = np.zeros((n, 8), np.float32)
    tb = []
    for name, at in (("cp_b", 0), ("tm_b", 0), ("ms_b", 5)):
        z = zero.copy()
        w = g[c1 + name].T
        z[:, at:at + w.shape[1]] = w
        tb.append(z)
    W1 = g[f0 + "W1"].reshape(-1, n)
    W2 = g[f0 + "W2"].transpose(0, 2, 1).reshape(-1, n)
    lay = {
        "xT": g["x"].reshape(-1, n).T,
        "cond_512T": g["cond_512"].T, "cond_64T": g["cond_64"].T, "sideT": g["fside_Bx32_0"].T,
        "W_dec": g["L0_cond_W_dec"], "b_dec": g["L0_cond_b_dec"][None], "V": g["L0_cond_V"],
        "WgT": g[f0 + "Wg"].T, "bg": g[f0 + "bg"], "b1T": g[f0 + "b1"].reshape(-1, n).T, "b2": g[f0 + "b2"],
        "W1T": W1.T, "W2T": chunks(W2),
        "pgb": np.concatenate([g[c1 + "pw_g"], g[c1 + "pw_b"]], 1),
        "ctg": np.concatenate([g[c1 + "cp_g"], g[c1 + "tm_g"]], 1), "msg": g[c1 + "ms_g"],
        "tbT": np.stack(tb, 1),
        "ixp": tiles(g["itok_BxS_0_999"]), "ixc": tiles(g["itok_BxS_0_4"]), "ixm": tiles(g["mask_BxS_ik0"]),
        "ic_row": g["itok_BxS_0_4"].reshape(1, -1), "im_row": g["mask_BxS_ik0"].reshape(1, -1),
        "mem_W1": g[c1 + "mem_W1"], "noi_W1": g[c1 + "noi_W1"], "res_W1": g[c1 + "res_W1"],
        "sW2": np.stack([g[c1 + k + "_W2"] for k in ("mem", "noi", "res")], 1),
        "sb1": np.stack([g[c1 + k + "_b1"] for k in ("mem", "noi", "res")], 1),
        "sbc": np.stack([np.stack([g[c1 + k + v] for k in ("mem", "noi", "res")]) for v in ("_b2", "_g", "_be")]),
        "int_W1": g[c1 + "int_W1"].reshape(6, n, n).transpose(1, 0, 2), "int_b1": g[c1 + "int_b1"],
        "int_W2": g[c1 + "int_W2"], "int_b2": g[c1 + "int_b2"][None], "aw": g[c1 + "aw"],
        "igb": np.stack([g[c1 + "int_g"], g[c1 + "int_be"]], 1),
        "w12T": np.concatenate([g[f1 + "w1_w"].T, g[f1 + "w2_w"].T], 1),
        "h1T": chunks(g[f1 + "h1_w"].T), "h2T": chunks(g[f1 + "h2_w"].T), "w3T": chunks(g[f1 + "w3_w"].T),
        "fsc": np.concatenate([g[f1 + k + "_s"].reshape(-1, n).T for k in ("w1", "w2", "h1", "h2", "w3")]
                              + [np.zeros((n, 3), np.float32)], 1),
        "ident": np.eye(n, dtype=np.float32), "desc8": np.arange(8, 0, -1).astype(np.float32),
        "iota8": np.array([0, 1, 2, 3, 4, 0, 1, 2], np.float32)[:, None],
    }
    nc = bacc.Bacc("TRN2", target_bir_lowering=False, num_devices=1)
    arrays, A = {}, {}
    for name, a in lay.items():
        a = np.ascontiguousarray(a)
        arrays[name + "_in"] = a
        A[name] = nc.dram_tensor(name + "_in", a.shape, mybir.dt.from_np(a.dtype), kind="ExternalInput").ap()
    tok = lay["xT"].shape[1]
    out = nc.dram_tensor("outT", (n, tok), F32, kind="ExternalOutput").ap()
    build(nc, A, out)
    r = run(nc, [arrays], core_ids=[0])
    got = r.results[0]["outT"]
    return got.T.reshape(g["x"].shape)
```

```python
from contextlib import ExitStack

import concourse.bass as bass
from concourse import mybir

ALU = mybir.AluOpType
ACT = mybir.ActivationFunctionType
AX_X = mybir.AxisListType.X
F32 = mybir.dt.float32
F32R = mybir.dt.float32r
I32 = mybir.dt.int32
U32 = mybir.dt.uint32

P = 128
EPS = 1e-5
MASKED = -3.0e38


class Steps:

    def __init__(self, eng, sem, per_block, b):
        self.eng, self.sem, self.n, self.b, self.k = eng, sem, per_block, b, 0

    def __call__(self, ins):
        self.k += 1
        ins.then_inc(self.sem, 1)
        self.eng.wait_ge(self.sem, self.b * self.n + self.k)

    def end(self):
        assert self.k == self.n, (self.k, self.n)


def build(nc, A, out):
    B, D = A["cond_512T"].shape[1], P
    TOK = A["xT"].shape[1]
    S = TOK // B
    T = 512
    NB = TOK // T
    TT = T // P
    BB = T // S
    MU, KR = A["cond_512T"].shape[0], A["V"].shape[0]
    E = A["b2"].shape[0]
    NH = A["W1T"].shape[1] // P
    HE = NH // E
    FC = A["w12T"].shape[1] // (2 * P)
    NP_, NC_, NM_ = A["pgb"].shape[0], A["ctg"].shape[0], A["msg"].shape[0]
    NI = NC_ + NM_
    RING = 3
    assert E == 8 and NI == 8 and NH % 4 == 0 and FC == 4

    with ExitStack() as ctx:
        def sb(name, shape, dt=F32, stack=ctx):
            return stack.enter_context(nc.sbuf_tensor(name, shape, dt))

        def parts(t, *widths):
            at, views = 0, []
            for w in widths:
                views.append(t[:, at:at + w])
                at += w
            return views

        def sem(name):
            return ctx.enter_context(nc.semaphore(name))

        bank = [ctx.enter_context(nc.psum_tensor(f"bank{i}", [P, T], F32)) for i in range(8)]
        HB = bank[0:4]
        OACC = bank[4]
        X0, X1, X2 = bank[5:8]

        W1 = [sb(f"W1_{p}", [P, NH * P], F32R) for p in "hl"]
        W2 = [sb(f"W2_{p}", [P, NH, P], F32R) for p in "hl"]
        w12 = [sb(f"w12_{p}", [P, 2, FC * P], F32R) for p in "hl"]
        h1w = [sb(f"h1w_{p}", [P, FC, FC * P], F32R) for p in "hl"]
        h2w = [sb(f"h2w_{p}", [P, FC, FC * P], F32R) for p in "hl"]
        w3 = [sb(f"w3_{p}", [P, FC, P], F32R) for p in "hl"]
        wmix = [sb(f"wmix_{p}", [P, 4, P], F32R) for p in "hl"]
        wint = [sb(f"wint_{p}", [P, P], F32R) for p in "hl"]
        wg = [sb(f"wg_{p}", [P, E], F32R) for p in "hl"]
        tab8 = [sb(f"tab8_{p}", [NI, P], F32R) for p in "hl"]
        vec = [sb(f"vec_{p}", [P, P], F32R) for p in "hl"]
        ib2 = [sb(f"ib2_{p}", [1, P], F32R) for p in "hl"]
        keepP = sb("keepP", [P, P + NH + 5 * FC + 2])
        ident, b1c, fsc, igb = parts(keepP, P, NH, 5 * FC, 2)
        identR = sb("identR", [P, P], F32R)
        onesR = sb("onesR", [1, P], F32R)
        Vw = sb("Vw", [KR, P])
        ub = sb("ub", [KR, B])
        b2e = sb("b2e", [40, P])
        keepB = sb("keepB", [P, 2 * E])
        bgt, desc8 = parts(keepB, E, E)
        iota8 = sb("iota8", [NI, 1])
        hs1 = sb("hs1", [P, FC])
        cs12 = sb("cs12", [P, FC])
        onesf = sb("onesf", [1, P])
        mhalf = sb("mhalf", [P, TT])
        ixall = sb("ixall", [P, 3, TOK // P], I32)

        early = ExitStack()
        stage = [sb(f"stage{i}", [P, 2048], stack=early) for i in range(2)]
        Wdec = sb("Wdec", [MU + 1, (D + 1) * KR], stack=early)
        Uall = sb("Uall", [P, B, KR], stack=early)
        muT = sb("muT", [MU + 1, B], stack=early)
        states = sb("states", [64, 6, P], stack=early)
        sT, sW1 = states[:, 0:3, :], states[:, 3:6, :]
        earlyP = sb("earlyP", [P, 10 * P + 3 * NI + E + 3], stack=early)
        sW2, iW1, iW2, tbT, wgf, sb1 = parts(earlyP, 3 * P, 6 * P, P, 3 * NI, E, 3)
        sW2 = sW2.rearrange("p (n d) -> p n d", n=3)
        iW1 = iW1.rearrange("p (n d) -> p n d", n=6)
        tbT = tbT.rearrange("p (n d) -> p n d", n=3)
        earlyB = sb("earlyB", [P, 10 * P + 6], stack=early)
        sbc, ibb, aw6 = parts(earlyB, 9 * P, P, 6)
        sbc = sbc.rearrange("p (v n d) -> p v n d", v=3, n=3)
        aw_e = sb("aw_e", [P, 6], stack=early)
        awx = sb("awx", [P, 4], stack=early)
        wsc = sb("wsc", [P, 6, P], stack=early)
        sz = sb("sz", [P, 3 * B], stack=early)
        sth = sb("sth", [P, 3 * B], stack=early)
        sa = sb("sa", [P, 3 * B], stack=early)
        sy = sb("sy", [P, 3, P], stack=early)
        syT = sb("syT", [P, 3 * B], stack=early)
        ib2f = sb("ib2f", [1, P], stack=early)
        wintf = sb("wintf", [P, P], stack=early)
        wmixf = sb("wmixf", [P, 4, P], stack=early)
        tab8f = sb("tab8f", [NI, P], stack=early)
        vecf = sb("vecf", [P, P], stack=early)
        sbn = sb("sbn", [P, 3, 6], stack=early)
        smv = sb("smv", [P, 3, 2], stack=early)
        sve = sb("sve", [P, 3], stack=early)
        srs = sb("srs", [P, 3], stack=early)
        early.close()

        hA = [sb(f"hA_{p}", [P, FC, T], F32R) for p in "hl"]
        gwb = sb("gwb", [P, E, T])
        hB = [sb(f"hB_{p}", [P, 4, T], F32R) for p in "hl"]
        G = sb("G", [P, RING, T])
        Q = sb("Q", [P, RING, T])
        cx, ct, cs_, ch = [[sb(f"c{k}_{p}", [P, T], F32R) for p in "hl"] for k in "xtsh"]
        xT = sb("xT", [P, T])
        xR = sb("xR", [P, T])
        Ub = sb("Ub", [P, BB, KR])
        rows = sb("rows", [40, T])
        idx8 = sb("idx8", [NI, T], I32)
        condR = [sb(f"cond_{p}", [P, T], F32R) for p in "hl"]
        x1T = sb("x1T", [P, T])
        keep = sb("keep", [P, T])
        oh8 = sb("oh8", [NI, T], F32R)
        fin = [sb(f"fin_{p}", [P, T], F32R) for p in "hl"]
        gp = sb("gp", [P, TT, 2 * P])
        gc = sb("gc", [P, TT, 2 * P])
        gm = sb("gm", [P, TT, P])
        xh = sb("xh", [P, TT, P])
        tt = sb("tt", [P, TT, P])
        ss = sb("ss", [P, TT, P])
        hh = sb("hh", [P, TT, P])
        bn6 = sb("bn6", [P, 3, TT, 6])
        mv = sb("mv", [P, 3, TT, 2])
        ve = sb("ve", [P, 3, TT])
        rstd = sb("rstd", [P, 3, TT])
        nmr = sb("nmr", [P, 3, TT])
        gt = sb("gt", [P, TT, E])
        g1 = sb("g1", [P, 2, TT, E])
        gk = sb("gk", [P, 2, TT, E])
        gmx = sb("gmx", [P, 2, TT])
        gkx = sb("gkx", [P, 2, TT])
        gd = sb("gd", [P, TT])
        gth = sb("gth", [P, TT])
        gw2 = sb("gw2", [P, 2, TT])
        gw = sb("gw", [P, TT, E])
        ixb = sb("ixb", [P, 3, TT], I32)

        U_dram = nc.dram_tensor("U_scratch", [P, B * KR], F32, kind="Internal").ap()
        gw_dram = nc.dram_tensor("gw_scratch", [E, T], F32, kind="Internal").ap()

        ld_cond, ld_small, ld_state = sem("ld_cond"), sem("ld_small"), sem("ld_state")
        passed = sem("passed")
        ld_w = [sem(f"ld_w{i}") for i in range(6)]
        ones_row, u_mm, u_even, u_odd, u_stored, ident_r = (sem(n) for n in (
            "ones_row", "u_mm", "u_even", "u_odd", "u_stored", "ident_r"))
        w_hi, w_lo, small_src, small_hi, small_lo = (sem(n) for n in ("w_hi", "w_lo", "small_src", "small_hi", "small_lo"))
        aw_max, aw_exp, s_mm, sz_ready, s_th, sa_ready, sy_mm, sv_ready, srs_ready, sy_ready, syT_mm, syT_ready, wsc_ready, fold_mm, \
            ub_mm, dve_setup = (sem(n) for n in (
                "aw_max", "aw_exp", "s_mm", "sz_ready", "s_th", "sa_ready", "sy_mm", "sv_ready", "srs_ready", "sy_ready",
                "syT_mm", "syT_ready", "wsc_ready", "fold_mm", "ub_mm", "dve_setup"))
        x_in, xr_in, u_in, t_mm, t_ready, cond_mm, cond_hi, cond_lo = (sem(n) for n in (
            "x_in", "xr_in", "u_in", "t_mm", "t_ready", "cond_mm", "cond_hi", "cond_lo"))
        gate_mm, gate_steps, gate_d, gate_th, gw2_ready, gw_parts, gw_ready, gwT_mm, gwT_ready, gw_stored, gwb_in = (sem(n) for n in (
            "gate_mm", "gate_steps", "gate_d", "gate_th", "gw2_ready", "gw_parts", "gw_ready", "gwT_mm", "gwT_ready", "gw_stored", "gwb_in"))
        m_mm, m_gelu, m_mul, m_hi, m_lo, m_used, o_mm, x1_ready = (sem(n) for n in (
            "m_mm", "m_gelu", "m_mul", "m_hi", "m_lo", "m_used", "o_mm", "x1_ready"))
        x1_hi, x1_lo, xtok_mm, bn_steps, ve_ready, rstd_ready, nmr_ready, normed, ts_ready = (sem(n) for n in (
            "x1_hi", "x1_lo", "xtok_mm", "bn_steps", "ve_ready", "rstd_ready", "nmr_ready", "normed", "ts_ready"))
        h_steps, h_ready, oh_ready, idx8_in, ixb_ready, gathered, kept = (sem(n) for n in (
            "h_steps", "h_ready", "oh_ready", "idx8_in", "ixb_ready", "gathered", "kept"))
        tr_mm, tr_hi, tr_lo, z_mm, z_th, a_ready, a_hi, a_lo, y_mm, yT_mm, f_full, f_hi, f_lo = (sem(n) for n in (
            "tr_mm", "tr_hi", "tr_lo", "z_mm", "z_th", "a_ready", "a_hi", "a_lo", "y_mm", "yT_mm",
            "f_full", "f_hi", "f_lo"))
        n_mm, n_th, n_u, n_h, n_g, n_hi, n_lo, n_out, stored = (sem(n) for n in (
            "n_mm", "n_th", "n_u", "n_h", "n_g", "n_hi", "n_lo", "n_out", "stored"))

        NMM = 3 * FC + 1
        GATE_STEPS = 12
        NSET_W, NSMALL = 6, 6

        def settled(eng):
            eng.sem_inc(passed, 1)

        def flat(t):
            v = t[tuple(slice(None) for _ in t.shape)]
            return v if len(t.shape) == 2 else v.rearrange("p a b -> p (a b)")

        small_ops = [(wgf, (wg[0][:, :], wg[1][:, :])), (ib2f[:, :], (ib2[0][:, :], ib2[1][:, :])),
                     (wintf[:, :], (wint[0][:, :], wint[1][:, :])), (flat(wmixf), (flat(wmix[0]), flat(wmix[1]))),
                     (tab8f[:, :], (tab8[0][:, :], tab8[1][:, :])), (vecf[:, :], (vec[0][:, :], vec[1][:, :]))]

        block = ctx.enter_context(nc.Block())

        WINDOW = [("A", 0), ("F", 0), ("C", 0), ("F", 1), ("A", 1), ("C", 1), ("F", 2), ("A", 2), ("C", 2),
                  ("F", 3), ("A", 3), ("C", 3), ("F", 4), ("A", 4), ("C", 4), ("F", 5), ("C", 5), ("F", 6),
                  ("C", 6), ("F", 7), ("F", 8), ("C", 7), ("F", 9), ("C", 8), ("F", 10), ("F", 11), ("C", 9),
                  ("F", 12)]

        def window(stages, f=None, a=None, c=None, skip=0):
            for kind, k in WINDOW[skip:]:
                blk = {"F": f, "A": a, "C": c}[kind]
                if blk is not None:
                    stages[kind](blk, k)

        def schedule(eng, stages, M, skip=0, late=None):
            window(stages, a=0)
            M(0, gate_of=1)
            if late:
                late()
            window(stages, a=1, c=0, skip=skip)
            M(1, gate_of=2, ffn_of=0)
            window(stages, f=0, a=2, c=1, skip=skip)
            with eng.Fori(2, NB - 1) as i:
                M(i, gate_of=i + 1, ffn_of=i - 1)
                window(stages, f=i - 1, a=i + 1, c=i, skip=skip)
            M(NB - 1, ffn_of=NB - 2)
            window(stages, f=NB - 2, c=NB - 1, skip=skip)
            window(stages, f=NB - 1)

        def first(b, n=1):
            return isinstance(b, int) and b < n

        @block.sync
        def _(sp):
            sp.dma_start(Wdec[0:MU, :], A["W_dec"]).then_inc(ld_cond, 16)
            sp.dma_start(Wdec[MU:MU + 1, :], A["b_dec"]).then_inc(ld_cond, 16)
            sp.dma_start(muT[0:MU, :], A["cond_512T"]).then_inc(ld_cond, 16)
            sp.dma_start(states[:, :, :], A["states"]).then_inc(ld_state, 16)
            sp.dma_start(earlyP[:, :], A["earlyP"]).then_inc(ld_state, 16)
            sp.dma_start(earlyB[:, :], A["earlyB"].partition_broadcast(P)).then_inc(ld_state, 16)
            for dst, src in ((keepP[:, :], "keepP"), (Vw[:, :], "V"), (b2e[32:40, :], "b2"), (iota8[:, :], "iota8"),
                             (ixall[:, :, :], "ixall"), (ib2f[:, :], "int_b2")):
                sp.dma_start(dst, A[src]).then_inc(ld_small, 16)
            sp.dma_start(keepB[:, :], A["keepB"].partition_broadcast(P)).then_inc(ld_small, 16)

            def load_w(n):
                src, width = (("W1T", 2048), ("W2T", 2048), ("w12T", 1024), ("h1T", 2048), ("h2T", 2048), ("w3T", 512))[n]
                if n >= 2:
                    sp.wait_ge(w_lo, n - 1)
                sp.dma_start(stage[n % 2][:, 0:width], A[src]).then_inc(ld_w[n], 16)

            def load_x(b):
                if not first(b):
                    sp.wait_ge(t_mm, b)
                sp.dma_start(xT[:, :], A["xT"][:, bass.ds(b * T, T)]).then_inc(x_in, 16)
                sp.dma_start(Ub[:, :, :], U_dram[:, bass.ds(b * BB * KR, BB * KR)]).then_inc(u_in, 16)

            def load_xr(b):
                if not first(b):
                    sp.wait_ge(x1_ready, b)
                sp.dma_start(xR[:, :], A["xT"][:, bass.ds(b * T, T)]).then_inc(xr_in, 16)

            def load_idx(b):
                if not first(b):
                    sp.wait_ge(oh_ready, b)
                sp.dma_start(idx8[0:NC_, :], A["ic_row"][:, bass.ds(b * T, T)]
                             .partition_broadcast(NC_)).then_inc(idx8_in, 16)
                sp.dma_start(idx8[NC_:NI, :], A["im_row"][:, bass.ds(b * T, T)]
                             .partition_broadcast(NM_)).then_inc(idx8_in, 16)

            def spread_gw(b):
                sp.wait_ge(gwT_ready, b + 1)
                if not first(b):
                    sp.wait_ge(gwb_in, b * 16)
                    sp.wait_ge(m_mul, b * NH)
                sp.dma_start(gw_dram[:, :], rows[32:40, :]).then_inc(gw_stored, 16)
                sp.wait_ge(gw_stored, b * 16 + 16)
                sp.dma_start(gwb[:, :, :], gw_dram.partition_broadcast(P)).then_inc(gwb_in, 16)

            def store(b):
                sp.wait_ge(n_out, b + 1)
                sp.dma_start(out[:, bass.ds(b * T, T)], keep[:, :]).then_inc(stored, 16)

            load_w(0)
            load_w(1)
            sp.wait_ge(u_even, KR // 2)
            sp.wait_ge(u_odd, KR // 2)
            sp.dma_start(U_dram[:, :], Uall[:, :, :]).then_inc(u_stored, 16)
            sp.wait_ge(u_stored, 16)
            load_x(0)
            load_xr(0)
            load_idx(0)
            load_w(2)
            load_w(3)
            sp.wait_ge(small_lo, NSMALL)
            spread_gw(0)
            load_x(1)
            load_w(4)
            load_w(5)
            load_xr(1)
            spread_gw(1)
            load_idx(1)
            load_x(2)
            load_xr(2)
            spread_gw(2)
            load_idx(2)
            store(0)
            with sp.Fori(2, NB - 1) as i:
                load_x(i + 1)
                load_xr(i + 1)
                spread_gw(i + 1)
                load_idx(i + 1)
                store(i - 1)
            store(NB - 2)
            store(NB - 1)
            sp.wait_ge(stored, 16 * NB)

        @block.tensor
        def _(pe):
            pe.wait_ge(ld_cond, 48)
            pe.wait_ge(ones_row, 1)
            wd = Wdec[:, :].rearrange("m (i k) -> m i k", k=KR)
            for k in range(KR):
                if k >= 4:
                    pe.wait_ge(u_odd if k % 2 else u_even, k // 2 - 1)
                pe.matmul(HB[k % 4][:, 0:B], wd[:, 0:D, k], muT[:, :], start=True, stop=True).then_inc(u_mm, 1)
            pe.matmul(X0[0:KR, 0:B], wd[:, D, :], muT[:, :], start=True, stop=True).then_inc(ub_mm, 1)
            pe.wait_ge(ld_state, 16 * 3)
            for n, k in enumerate((64, 64, 32)):
                mm = pe.matmul(X1[:, n * B:(n + 1) * B], sW1[0:k, n, :], sT[0:k, n, :], start=True, stop=True)
            mm.then_inc(s_mm, 1)
            pe.wait_ge(sa_ready, 1)
            for n in range(3):
                mm = pe.matmul(X2[:, n * P:(n + 1) * P], sa[:, n * B:(n + 1) * B], sW2[:, n, :], start=True, stop=True)
            mm.then_inc(sy_mm, 1)
            pe.wait_ge(sy_ready, 1)
            pe.wait_ge(ld_small, 16 * 7)
            for n in range(3):
                mm = pe.transpose(X1[:, n * P:(n + 1) * P], sy[:, n, :], ident)
            mm.then_inc(syT_mm, 1)
            pe.wait_ge(syT_ready, 1)
            pe.wait_ge(wsc_ready, 1)
            for n in range(3):
                pe.matmul(X2[:, 0:P], syT[:, n * B:(n + 1) * B], wsc[:, 2 + n, :], start=(n == 0), stop=(n == 2))
            for n, w_ in enumerate((0, 1, 5)):
                mm = pe.matmul(OACC[0:NI, 0:P], tbT[:, n, :], wsc[:, w_, :], start=(n == 0), stop=(n == 2))
            mm.then_inc(fold_mm, 1)
            pe.wait_ge(small_lo, NSMALL)

            def A_stage(b, k):
                if k == 0:
                    pe.wait_ge(x_in, b * 16 + 16)
                    pe.wait_ge(u_in, b * 16 + 16)
                    if not first(b):
                        pe.wait_ge(gwT_ready, b)
                    for j in range(BB):
                        mm = pe.matmul(X0[0:KR, j * S:(j + 1) * S], Ub[:, j, :], xT[:, j * S:(j + 1) * S],
                                       start=True, stop=True)
                    mm.then_inc(t_mm, 1)
                elif k == 1:
                    pe.wait_ge(t_ready, b + 1)
                    if not first(b):
                        pe.wait_ge(x1_ready, b)
                    pe.matmul(OACC[:, :], Vw[:, :], rows[0:KR, :], start=True, stop=True).then_inc(cond_mm, 1)
                elif k == 2:
                    pe.wait_ge(cond_lo, b + 1)
                    for t in range(TT):
                        for n, (a, w_) in enumerate(((0, 0), (0, 1), (1, 0))):
                            mm = pe.matmul(X0[:, t * E:(t + 1) * E], condR[a][:, t * P:(t + 1) * P], wg[w_][:, :],
                                           start=(n == 0), stop=(n == 2))
                    mm.then_inc(gate_mm, 1)
                elif k == 4:
                    pe.wait_ge(gw_ready, b + 1)
                    for t in range(TT):
                        mm = pe.transpose(X0[0:E, t * P:(t + 1) * P], gw[:, t, :], ident)
                    mm.then_inc(gwT_mm, 1)

            def M(b, gate_of=None, ffn_of=None):
                lag = 3
                pe.wait_ge(gwT_ready, b + 1)
                pe.wait_ge(cond_lo, b + 1)
                pe.matmul(OACC[:, :], b2e[32:40, :], rows[32:40, :], start=True, stop=False)
                for c in range(NH + lag):
                    if c < NH:
                        if c >= 4:
                            pe.wait_ge(m_gelu, b * NH + c - 3)
                        elif not first(b, 2):
                            if c == 0:
                                pe.wait_ge(n_out, b - 1)
                            pe.wait_ge(n_g, (b - 1) * 2 * FC)
                        for n, (a, x_) in enumerate(((0, 0), (0, 1), (1, 0))):
                            mm = pe.matmul(HB[c % 4][:, :], W1[a][:, c * P:(c + 1) * P], condR[x_][:, :],
                                           start=(n == 0), stop=(n == 2))
                        mm.then_inc(m_mm, 1)
                    if c >= lag:
                        q = c - lag
                        if q == NH - 2 and gate_of is not None:
                            A_stage(gate_of, 0)
                        if q == NH - 1 and ffn_of is not None:
                            F_stage(ffn_of, 0)
                        pe.wait_ge(m_lo, b * NH + q + 1)
                        for n, (a, x_) in enumerate(((0, 0), (1, 0), (0, 1))):
                            mm = pe.matmul(OACC[:, :], W2[a][:, q, :], hB[x_][:, q % 4, :],
                                           start=False, stop=(q == NH - 1 and n == 2))
                        mm.then_inc(m_used, 1)

            def turn(b, n, src, dst):
                if n == 0:
                    pe.wait_ge(ts_ready, b * 2 + 1)
                    if not first(b):
                        pe.wait_ge(normed, b * 3)
                elif n == 1:
                    pe.wait_ge(ts_ready, b * 2 + 2)
                    pe.wait_ge(normed, b * 3 + 1)
                else:
                    pe.wait_ge(h_ready, b + 1)
                    pe.wait_ge(tr_lo, b * 3 + 1)
                for t in range(TT):
                    mm = pe.transpose(dst[:, t * P:(t + 1) * P], src[:, t, :], ident)
                mm.then_inc(tr_mm, 1)

            def C_stage(b, k):
                if k == 0:
                    pe.wait_ge(x1_ready, b + 1)
                    if not first(b):
                        pe.wait_ge(f_full, b)
                    for t in range(TT):
                        mm = pe.transpose(X1[:, t * P:(t + 1) * P], x1T[:, t * P:(t + 1) * P], ident)
                    mm.then_inc(xtok_mm, 1)
                elif k == 4:
                    turn(b, 0, tt, X2)
                    turn(b, 1, ss, X1)
                elif k == 5:
                    turn(b, 2, hh, X2)
                elif k == 6:
                    pe.wait_ge(tr_lo, b * 3 + 2)
                    seqs = identR[:, bass.ds(b * BB, BB)].unsqueeze(2).broadcast_to([P, BB, S])
                    pe.matmul(X1[:, :], vec[0][:, :], seqs, start=True, stop=False)
                    pe.matmul(X1[:, :], vec[1][:, :], seqs, start=False, stop=False)
                    pe.wait_ge(oh_ready, b + 1)
                    pe.matmul(X1[:, :], tab8[0][:, :], oh8[0:NI, :], start=False, stop=False)
                    pe.matmul(X1[:, :], tab8[1][:, :], oh8[0:NI, :], start=False, stop=False)
                    pe.wait_ge(x1_lo, b + 1)
                    for m, src in enumerate((cx, ct, cs_, ch)):
                        if m == 3:
                            pe.wait_ge(tr_lo, b * 3 + 3)
                        for n, (a, x_) in enumerate(((0, 0), (0, 1), (1, 0))):
                            mm = pe.matmul(X1[:, :], wmix[a][:, m, :], src[x_][:, :],
                                           start=False, stop=(m == 3 and n == 2))
                    mm.then_inc(z_mm, 1)
                elif k == 7:
                    pe.wait_ge(a_lo, b + 1)
                    for t in range(TT):
                        o = X2[:, t * P:(t + 1) * P]
                        pe.matmul(o, onesR[:, :], ib2[0][:, :], start=True, stop=False)
                        pe.matmul(o, onesR[:, :], ib2[1][:, :], start=False, stop=False)
                        for n, (x_, a) in enumerate(((0, 0), (0, 1), (1, 0))):
                            mm = pe.matmul(o, ct[x_][:, t * P:(t + 1) * P], wint[a][:, :], start=False, stop=(n == 2))
                    mm.then_inc(y_mm, 1)
                elif k == 9:
                    pe.wait_ge(normed, b * 3 + 3)
                    pe.wait_ge(a_ready, b + 1)
                    for t in range(TT):
                        mm = pe.transpose(X1[:, t * P:(t + 1) * P], hh[:, t, :], ident)
                    mm.then_inc(yT_mm, 1)

            def F_stage(b, k):
                last = isinstance(b, int) and b == NB - 1
                if k < FC:
                    if k == 0:
                        pe.wait_ge(f_lo, b + 1)
                        if last:
                            pe.wait_ge(n_out, b)
                            pe.wait_ge(n_g, b * 2 * FC)
                        else:
                            pe.wait_ge(m_gelu, (b + 2) * NH - 2)
                    elif k == 1:
                        if not last:
                            pe.wait_ge(m_gelu, (b + 2) * NH)
                    elif k >= 2:
                        pe.wait_ge(n_h, b * FC + k - 1)
                    for w_ in range(2):
                        o = HB[2 * (k % 2) + w_]
                        for n, (a, x_) in enumerate(((0, 0), (0, 1), (1, 0))):
                            mm = pe.matmul(o[:, :], w12[a][:, w_, k * P:(k + 1) * P], fin[x_][:, :],
                                           start=(n == 0), stop=(n == 2))
                    mm.then_inc(n_mm, 1)
                    return
                layer, c = (k // FC, k % FC)
                w, src = ((h1w, hA), (h2w, hB), (w3, hA))[layer - 1]
                if layer == 1:
                    pe.wait_ge(n_h, b * FC + (3 if c < 2 else 4))
                elif layer == 2:
                    pe.wait_ge(n_g, b * 2 * FC + c + 1)
                else:
                    pe.wait_ge(n_g, b * 2 * FC + FC + 1)
                for kc in range(FC):
                    if c == 0:
                        pe.wait_ge(n_lo, b * 3 * FC + (layer - 1) * FC + kc + 1)
                    for n, (a, x_) in enumerate(((0, 0), (0, 1), (1, 0))):
                        mm = pe.matmul(HB[c][:, :], w[a][:, kc, c * P:(c + 1) * P], src[x_][:, kc, :],
                                       start=(kc == 0 and n == 0), stop=(kc == FC - 1 and n == 2))
                mm.then_inc(n_mm, 1)

            schedule(pe, {"A": A_stage, "C": C_stage, "F": F_stage}, M, skip=2)

        @block.scalar
        def _(act):
            act.wait_ge(aw_max, 1)
            act.activation(aw_e[:, :], aw6, ACT.Exp, bias=awx[:, 1:2], accum_out=awx[:, 2:3]).then_inc(aw_exp, 1)
            for k in range(1, KR, 2):
                act.wait_ge(u_mm, k + 1)
                act.activation(Uall[:, :, k], HB[k % 4][:, 0:B], ACT.Copy).then_inc(u_odd, 1)
            act.wait_ge(sz_ready, 1)
            act.activation(sth[:, :], sz[:, :], ACT.Tanh, scale=0.5).then_inc(s_th, 1)

            def big_hi(n, dst):
                act.wait_ge(ld_w[n], 16)
                act.activation(dst, stage[n % 2][:, 0:dst.free_size()], ACT.Copy).then_inc(w_hi, 1)

            big_hi(0, W1[0][:, :])
            big_hi(1, flat(W2[0]))
            act.wait_ge(syT_mm, 1)
            act.activation(syT[:, :], X1[:, 0:3 * B], ACT.Copy).then_inc(syT_ready, 1)
            act.activation(identR[:, :], ident[:, :], ACT.Copy).then_inc(ident_r, 1)
            for n, (src, dst) in enumerate(small_ops):
                act.wait_ge(small_src, n + 1)
                act.activation(dst[0], src, ACT.Copy).then_inc(small_hi, 1)

            def late():
                for n, w in ((2, w12), (3, h1w), (4, h2w), (5, w3)):
                    big_hi(n, flat(w[0]))

            def A_stage(b, k):
                if k == 1:
                    act.wait_ge(cond_mm, b + 1)
                    if not first(b):
                        act.wait_ge(m_mm, b * NH)
                    act.activation(condR[0][:, :], OACC[:, :], ACT.Copy).then_inc(cond_hi, 1)
                elif k == 2:
                    act.wait_ge(gate_d, b + 1)
                    act.activation(gth[:, :], gd[:, :], ACT.Tanh, scale=0.5).then_inc(gate_th, 1)
                elif k == 4:
                    act.wait_ge(gwT_mm, b + 1)
                    if not first(b):
                        act.wait_ge(gw_stored, b * 16)
                        act.wait_ge(m_mm, b * NH)
                    act.activation(rows[32:40, :], X0[0:E, :], ACT.Copy).then_inc(gwT_ready, 1)

            def M(b, gate_of=None, ffn_of=None):
                def hi(c):
                    act.wait_ge(m_mul, b * NH + c + 1)
                    if c >= 4:
                        act.wait_ge(m_used, b * NH + c - 3)
                    elif not first(b, 2):
                        act.wait_ge(n_mm, (b - 1) * NMM)
                    act.activation(hB[0][:, c % 4, :], Q[:, c % RING, :], ACT.Copy).then_inc(m_hi, 1)

                if first(b):
                    act.wait_ge(small_lo, NSMALL)
                elif not first(b, 2):
                    act.wait_ge(n_lo, (b - 1) * 3 * FC)
                for c in range(NH):
                    act.wait_ge(m_mm, b * NH + c + 1)
                    if c >= RING:
                        act.wait_ge(m_mul, b * NH + c - RING + 1)
                    act.activation(G[:, c % RING, :], HB[c % 4][:, :], ACT.Gelu, bias=b1c[:, c:c + 1]).then_inc(m_gelu, 1)
                    if c >= 1:
                        hi(c - 1)
                hi(NH - 1)

            def norm(b, n, src, dst):
                act.wait_ge(nmr_ready, b * 3 + n + 1)
                for t in range(TT):
                    ins = act.activation(dst[:, t, :], src(t), ACT.Identity, scale=rstd[:, n, t:t + 1],
                                         bias=nmr[:, n, t:t + 1])
                ins.then_inc(normed, 1)

            def turned_hi(b, n, src, dst):
                act.wait_ge(tr_mm, b * 3 + n + 1)
                if n == 0 and not first(b):
                    act.wait_ge(y_mm, b)
                act.activation(dst[0][:, :], src[:, :], ACT.Copy).then_inc(tr_hi, 1)

            def C_stage(b, k):
                if k == 0:
                    act.wait_ge(x1_ready, b + 1)
                    if not first(b):
                        act.wait_ge(z_mm, b)
                    act.activation(cx[0][:, :], x1T[:, :], ACT.Copy).then_inc(x1_hi, 1)
                elif k == 1:
                    if not first(b):
                        act.wait_ge(ts_ready, b * 2)
                        act.wait_ge(f_lo, b)
                    norm(b, 0, lambda t: X1[:, t * P:(t + 1) * P], xh)
                elif k == 3:
                    norm(b, 1, lambda t: hh[:, t, :], hh)
                elif k == 4:
                    turned_hi(b, 0, X2, ct)
                    turned_hi(b, 1, X1, cs_)
                elif k == 5:
                    turned_hi(b, 2, X2, ch)
                elif k == 6:
                    act.wait_ge(z_mm, b + 1)
                    act.activation(flat(tt), X1[:, :], ACT.Tanh, scale=0.5).then_inc(z_th, 1)
                    act.wait_ge(a_ready, b + 1)
                    act.activation(ct[0][:, :], flat(ss), ACT.Copy).then_inc(a_hi, 1)
                elif k == 8:
                    norm(b, 2, lambda t: X2[:, t * P:(t + 1) * P], hh)
                elif k == 9:
                    act.wait_ge(f_full, b + 1)
                    act.activation(fin[0][:, :], flat(xh), ACT.Copy).then_inc(f_hi, 1)

            def F_stage(b, k):
                if k < FC:
                    def hi(c):
                        act.wait_ge(n_h, b * FC + c + 1)
                        act.activation(hA[0][:, c, :], Q[:, c % RING, :], ACT.Copy).then_inc(n_hi, 1)
                    act.wait_ge(n_mm, b * NMM + k + 1)
                    if k == 0 and not first(b):
                        act.wait_ge(n_lo, b * 3 * FC)
                    if k >= RING:
                        act.wait_ge(n_h, b * FC + k - RING + 1)
                    act.activation(G[:, k % RING, :], HB[2 * (k % 2)][:, :], ACT.Tanh, scale=hs1[:, k:k + 1]).then_inc(n_th, 1)
                    if k >= 1:
                        hi(k - 1)
                    if k == FC - 1:
                        hi(k)
                elif k < 3 * FC:
                    c = k % FC
                    dst = hB if k < 2 * FC else hA
                    act.wait_ge(n_mm, b * NMM + k + 1)
                    act.wait_ge(n_lo, b * 3 * FC + k - RING + 1)
                    act.activation(G[:, k % RING, :], HB[c][:, :], ACT.Gelu, scale=fsc[:, k + FC:k + FC + 1])\
                       .then_inc(n_g, 1)
                    act.wait_ge(n_g, b * 2 * FC + k - FC + 1)
                    act.activation(dst[0][:, c, :], G[:, k % RING, :], ACT.Copy).then_inc(n_hi, 1)

            schedule(act, {"A": A_stage, "C": C_stage, "F": F_stage}, M, late=late)

        @block.vector
        def _(dve):
            dve.memset(muT[MU:MU + 1, :], 1.0)
            dve.memset(onesf[:, :], 1.0)
            dve.memset(mhalf[:, :], -0.5).then_inc(ones_row, 1)
            dve.wait_ge(ones_row, 1)
            dve.tensor_copy(onesR[:, :], onesf[:, :])
            step = Steps(dve, dve_setup, 0, 0)
            dve.wait_ge(ld_state, 16 * 3)
            step(dve.reduce_max(awx[:, 0:1], aw6, AX_X))
            dve.tensor_scalar(awx[:, 1:2], awx[:, 0:1], -1.0, None, ALU.mult).then_inc(aw_max, 1)
            for k in range(0, KR, 2):
                dve.wait_ge(u_mm, k + 1)
                dve.tensor_copy(Uall[:, :, k], HB[k % 4][:, 0:B]).then_inc(u_even, 1)
            dve.wait_ge(ub_mm, 1)
            dve.tensor_copy(ub[:, :], X0[0:KR, 0:B])
            dve.wait_ge(s_mm, 1)
            for n in range(3):
                last = dve.tensor_scalar(sz[:, n * B:(n + 1) * B], X1[:, n * B:(n + 1) * B], sb1[:, n:n + 1], None, ALU.add)
            last.then_inc(sz_ready, 1)
            dve.wait_ge(aw_exp, 1)
            step(dve.reciprocal(awx[:, 3:4], awx[:, 2:3]))
            step(dve.tensor_scalar(aw_e[:, :], aw_e[:, :], awx[:, 3:4], None, ALU.mult))
            for n in range(6):
                last = dve.tensor_scalar(wsc[:, n, :], iW1[:, n, :], aw_e[:, n:n + 1], None, ALU.mult)
            last.then_inc(wsc_ready, 1)
            dve.wait_ge(s_th, 1)
            step(dve.scalar_tensor_tensor(out=sa[:, :], in0=sth[:, :], scalar=1.0, in1=sz[:, :], op0=ALU.add, op1=ALU.mult))
            dve.tensor_scalar(sa[:, :], sa[:, :], 0.5, None, ALU.mult).then_inc(sa_ready, 1)
            dve.wait_ge(sy_mm, 1)
            step(dve.tensor_tensor(sy[:, :, :], X2[:, 0:3 * P].rearrange("p (n d) -> p n d", n=3), sbc[:, 0, :, :], ALU.add))
            for n in range(3):
                ins = dve.bn_stats(sbn[:, n, :], sy[:, n, :])
            step(ins)
            for n in range(3):
                ins = dve.bn_aggr(smv[:, n, :], sbn[:, n, :])
            step(ins)
            dve.tensor_scalar(sve[:, :], smv[:, :, 1], EPS, None, ALU.add).then_inc(sv_ready, 1)
            dve.wait_ge(srs_ready, 1)
            for n in range(3):
                ins = dve.tensor_scalar(sy[:, n, :], sy[:, n, :], smv[:, n, 0:1], srs[:, n:n + 1], ALU.subtract, ALU.mult)
            step(ins)
            step(dve.tensor_tensor(sy[:, :, :], sy[:, :, :], sbc[:, 1, :, :], ALU.mult))
            dve.tensor_tensor(sy[:, :, :], sy[:, :, :], sbc[:, 2, :, :], ALU.add).then_inc(sy_ready, 1)
            dve.wait_ge(ld_small, 16 * 7)
            dve.tensor_scalar(wintf[:, :], iW2, 0.5, None, ALU.mult).then_inc(small_src, 3)
            dve.wait_ge(wsc_ready, 1)
            step(dve.tensor_tensor(wmixf[:, 0, :], wsc[:, 2, :], wsc[:, 3, :], ALU.add))
            dve.tensor_tensor(wmixf[:, 0, :], wmixf[:, 0, :], wsc[:, 4, :], ALU.add)
            dve.tensor_copy(wmixf[:, 1, :], wsc[:, 1, :])
            dve.tensor_copy(wmixf[:, 2, :], wsc[:, 5, :])
            dve.tensor_copy(wmixf[:, 3, :], wsc[:, 0, :]).then_inc(small_src, 1)
            step(dve.tensor_scalar(hs1[:, :], fsc[:, 0:FC], 0.5, None, ALU.mult))
            dve.tensor_tensor(cs12[:, :], hs1[:, :], fsc[:, FC:2 * FC], ALU.mult)
            dve.wait_ge(fold_mm, 1)
            dve.tensor_copy(tab8f[:, :], OACC[0:NI, 0:P]).then_inc(small_src, 1)
            dve.tensor_tensor(vecf[:, :], X2[:, 0:P], ibb, ALU.add).then_inc(small_src, 1)

            def big_lo(n, w):
                dve.wait_ge(w_hi, n + 1)
                dst = flat(w[1])
                dve.tensor_tensor(dst, stage[n % 2][:, 0:dst.free_size()], flat(w[0]).bitcast(F32), ALU.subtract)\
                   .then_inc(w_lo, 1)

            big_lo(0, W1)
            big_lo(1, W2)
            for n, (src, dst) in enumerate(small_ops):
                dve.wait_ge(small_hi, n + 1)
                dve.tensor_tensor(dst[1], src, dst[0].bitcast(F32), ALU.subtract).then_inc(small_lo, 1)

            def late():
                for n, w in ((2, w12), (3, h1w), (4, h2w), (5, w3)):
                    big_lo(n, w)

            def statistics(b, n, src, step):
                for t in range(TT):
                    ins = dve.bn_stats(bn6[:, n, t, :], src(t))
                step(ins)
                settled(dve)
                for t in range(TT):
                    ins = dve.bn_aggr(mv[:, n, t, :], bn6[:, n, t, :])
                step(ins)
                dve.tensor_scalar(ve[:, n, :], mv[:, n, :, 1], EPS, None, ALU.add).then_inc(ve_ready, 1)

            def offset(b, n):
                dve.wait_ge(rstd_ready, b * 3 + n + 1)
                dve.scalar_tensor_tensor(out=nmr[:, n, :], in0=mv[:, n, :, 0], scalar=-1.0, in1=rstd[:, n, :],
                                         op0=ALU.mult, op1=ALU.mult).then_inc(nmr_ready, 1)

            def turned_lo(b, n, src, dst):
                dve.wait_ge(tr_hi, b * 3 + n + 1)
                dve.tensor_tensor(dst[1][:, :], src[:, :], dst[0][:, :].bitcast(F32), ALU.subtract).then_inc(tr_lo, 1)

            def per_tile(v):
                return v.unsqueeze(2).broadcast_to([P, TT, E])

            def A_stage(b, k):
                if k == 0:
                    dve.wait_ge(t_mm, b + 1)
                    if not first(b):
                        dve.wait_ge(cond_mm, b)
                    dve.tensor_tensor(rows[0:KR, :].rearrange("k (b s) -> k b s", b=BB),
                                      X0[0:KR, :].rearrange("k (b s) -> k b s", b=BB),
                                      ub[:, bass.ds(b * BB, BB)].unsqueeze(2).broadcast_to([KR, BB, S]), ALU.add)\
                       .then_inc(t_ready, 1)
                elif k == 1:
                    dve.wait_ge(cond_hi, b + 1)
                    dve.tensor_tensor(condR[1][:, :], OACC[:, :], condR[0][:, :].bitcast(F32), ALU.subtract)\
                       .then_inc(cond_lo, 1)
                elif k == 2:
                    step = Steps(dve, gate_steps, GATE_STEPS, b)
                    dve.wait_ge(gate_mm, b + 1)
                    if not first(b):
                        dve.wait_ge(gw_ready, b)
                    step(dve.tensor_tensor(gt[:, :, :], X0[:, 0:TT * E].rearrange("p (t e) -> p t e", t=TT),
                                           bgt.unsqueeze(1).broadcast_to([P, TT, E]), ALU.add))
                    for r in range(2):
                        step(dve.reduce_max(gmx[:, r, :], gt[:, :, :], AX_X))
                        step(dve.tensor_tensor(gk[:, r, :, :], gt[:, :, :], per_tile(gmx[:, r, :]), ALU.is_equal))
                        step(dve.tensor_tensor(gk[:, r, :, :], gk[:, r, :, :],
                                               desc8.unsqueeze(1).broadcast_to([P, TT, E]), ALU.mult))
                        step(dve.reduce_max(gkx[:, r, :], gk[:, r, :, :], AX_X))
                        step(dve.tensor_tensor(g1[:, r, :, :], gk[:, r, :, :], per_tile(gkx[:, r, :]), ALU.is_equal))
                        if r == 0:
                            step(dve.scalar_tensor_tensor(out=gt[:, :, :], in0=g1[:, 0, :, :], scalar=MASKED,
                                                          in1=gt[:, :, :], op0=ALU.mult, op1=ALU.add))
                    dve.tensor_tensor(gd[:, :], gmx[:, 0, :], gmx[:, 1, :], ALU.subtract).then_inc(gate_d, 1)
                    step.end()
                elif k == 3:
                    dve.wait_ge(gate_th, b + 1)
                    dve.tensor_scalar(gw2[:, 0, :], gth[:, :], 0.5, 0.5, ALU.mult, ALU.add)
                    dve.tensor_scalar(gw2[:, 1, :], gth[:, :], -0.5, 0.5, ALU.mult, ALU.add).then_inc(gw2_ready, 1)
                    dve.wait_ge(gw2_ready, b + 1)
                    for r in range(2):
                        ins = dve.tensor_tensor(g1[:, r, :, :], g1[:, r, :, :], per_tile(gw2[:, r, :]), ALU.mult)
                    ins.then_inc(gw_parts, 1)
                    dve.wait_ge(gw_parts, b + 1)
                    if not first(b):
                        dve.wait_ge(gwT_mm, b)
                    dve.tensor_tensor(gw[:, :, :], g1[:, 0, :, :], g1[:, 1, :, :], ALU.add).then_inc(gw_ready, 1)

            def M(b, gate_of=None, ffn_of=None):
                def lo(c):
                    dve.wait_ge(m_hi, b * NH + c + 1)
                    dve.tensor_tensor(hB[1][:, c % 4, :], Q[:, c % RING, :], hB[0][:, c % 4, :].bitcast(F32), ALU.subtract)\
                       .then_inc(m_lo, 1)

                dve.wait_ge(gwb_in, b * 16 + 16)
                if not first(b, 2):
                    dve.wait_ge(n_lo, (b - 1) * 3 * FC)
                for c in range(NH):
                    dve.wait_ge(m_gelu, b * NH + c + 1)
                    if c >= RING:
                        dve.wait_ge(m_lo, b * NH + c - RING + 1)
                    dve.tensor_tensor(Q[:, c % RING, :], G[:, c % RING, :], gwb[:, c // HE, :], ALU.mult).then_inc(m_mul, 1)
                    if c >= 1:
                        lo(c - 1)
                lo(NH - 1)
                dve.wait_ge(m_used, b * NH + NH)
                dve.wait_ge(xr_in, b * 16 + 16)
                if not first(b):
                    dve.wait_ge(kept, b)
                    dve.wait_ge(xtok_mm, b)
                dve.tensor_tensor(x1T[:, :], OACC[:, :], xR[:, :], ALU.add).then_inc(x1_ready, 1)

            def C_stage(b, k):
                if k == 0:
                    if not first(b):
                        dve.wait_ge(f_full, b)
                    dve.wait_ge(xtok_mm, b + 1)
                    statistics(b, 0, lambda t: X1[:, t * P:(t + 1) * P], Steps(dve, bn_steps, 6, b))
                elif k == 1:
                    offset(b, 0)
                elif k == 2:
                    step = Steps(dve, h_steps, 2, b)
                    dve.wait_ge(normed, b * 3 + 1)
                    dve.wait_ge(gathered, (b + 1) * 16 * 3 * TT)
                    if not first(b):
                        dve.wait_ge(yT_mm, b)
                    step(dve.tensor_tensor(hh[:, :, :], xh[:, :, :], gp[:, :, 0:P], ALU.mult))
                    step(dve.tensor_tensor(hh[:, :, :], hh[:, :, :], gp[:, :, P:2 * P], ALU.add))
                    step.end()
                    step = Steps(dve, bn_steps, 6, b)
                    step.k = 2
                    statistics(b, 1, lambda t: hh[:, t, :], step)
                elif k == 3:
                    offset(b, 1)
                    dve.wait_ge(idx8_in, (b + 1) * 32)
                    dve.tensor_scalar(oh8[:, :], idx8[:, :], iota8[:, :], None, ALU.is_equal).then_inc(oh_ready, 1)
                elif k == 4:
                    dve.wait_ge(normed, b * 3 + 2)
                    dve.tensor_tensor(hh[:, :, :], hh[:, :, :], gc[:, :, 0:P], ALU.mult).then_inc(h_ready, 1)
                    turned_lo(b, 0, X2, ct)
                    turned_lo(b, 1, X1, cs_)
                elif k == 5:
                    turned_lo(b, 2, X2, ch)
                elif k == 6:
                    dve.wait_ge(z_th, b + 1)
                    dve.scalar_tensor_tensor(out=flat(ss), in0=flat(tt), scalar=1.0, in1=X1[:, :],
                                             op0=ALU.add, op1=ALU.mult).then_inc(a_ready, 1)
                    dve.wait_ge(a_hi, b + 1)
                    dve.tensor_tensor(ct[1][:, :], flat(ss), ct[0][:, :].bitcast(F32), ALU.subtract).then_inc(a_lo, 1)
                elif k == 7:
                    step = Steps(dve, bn_steps, 6, b)
                    step.k = 4
                    dve.wait_ge(y_mm, b + 1)
                    statistics(b, 2, lambda t: X2[:, t * P:(t + 1) * P], step)
                    step.end()
                elif k == 8:
                    offset(b, 2)
                elif k == 9:
                    dve.wait_ge(yT_mm, b + 1)
                    dve.tensor_scalar(flat(xh), X1[:, :], igb[:, 0:1], igb[:, 1:2], ALU.mult, ALU.add).then_inc(f_full, 1)

            def F_stage(b, k):
                if k < FC:
                    def lo(c):
                        dve.wait_ge(n_hi, b * 3 * FC + c + 1)
                        dve.tensor_tensor(hA[1][:, c, :], Q[:, c % RING, :], hA[0][:, c, :].bitcast(F32), ALU.subtract)\
                           .then_inc(n_lo, 1)
                    dve.wait_ge(n_th, b * FC + k + 1)
                    if k == 0:
                        last = isinstance(b, int) and b == NB - 1
                        dve.wait_ge(n_lo, b * 3 * FC) if last else dve.wait_ge(m_lo, (b + 2) * NH)
                    elif k >= RING:
                        dve.wait_ge(n_lo, b * 3 * FC + k - RING + 1)
                    dve.scalar_tensor_tensor(out=Q[:, k % RING, :], in0=G[:, k % RING, :], scalar=1.0,
                                             in1=HB[2 * (k % 2)][:, :], op0=ALU.add, op1=ALU.mult).then_inc(n_u, 1)
                    dve.wait_ge(n_u, b * FC + k + 1)
                    dve.scalar_tensor_tensor(out=Q[:, k % RING, :], in0=Q[:, k % RING, :], scalar=cs12[:, k:k + 1],
                                             in1=HB[2 * (k % 2) + 1][:, :], op0=ALU.mult, op1=ALU.mult).then_inc(n_h, 1)
                    if k >= 1:
                        lo(k - 1)
                    if k == FC - 1:
                        lo(k)
                elif k < 3 * FC:
                    c = k % FC
                    dst = hB if k < 2 * FC else hA
                    dve.wait_ge(n_hi, b * 3 * FC + k + 1)
                    dve.tensor_tensor(dst[1][:, c, :], G[:, k % RING, :], dst[0][:, c, :].bitcast(F32), ALU.subtract)\
                       .then_inc(n_lo, 1)
                else:
                    dve.wait_ge(n_mm, b * NMM + NMM)
                    dve.wait_ge(kept, b + 1)
                    dve.scalar_tensor_tensor(out=keep[:, :], in0=HB[0][:, :], scalar=fsc[:, 4 * FC:4 * FC + 1],
                                             in1=keep[:, :], op0=ALU.mult, op1=ALU.add).then_inc(n_out, 1)

            schedule(dve, {"A": A_stage, "C": C_stage, "F": F_stage}, M, late=late)

        @block.gpsimd
        def _(pool):
            def gather(b):
                settled(pool)
                pool.tensor_copy(ixb[:, :, :], ixall[:, :, bass.ds(b * TT, TT)]).then_inc(ixb_ready, 1)
                pool.wait_ge(ixb_ready, b + 1)
                settled(pool)
                for t in range(TT):
                    for n, (dst, src) in enumerate(((gp, "pgb"), (gc, "ctg"), (gm, "msg"))):
                        pool.indirect_dma_start(out=dst[:, t, :], out_offset=None, in_=A[src],
                                                in_offset=bass.IndirectOffsetOnAxis(ap=ixb[:, n, t:t + 1].bitcast(U32), axis=0))\
                            .then_inc(gathered, 16)

            def pow_(b, n):
                pool.wait_ge(ve_ready, b * 3 + n + 1)
                pool.tensor_tensor(rstd[:, n, :], ve[:, n, :], mhalf[:, :], ALU.pow).then_inc(rstd_ready, 1)

            pool.wait_ge(sv_ready, 1)
            pool.tensor_tensor(srs[:, :], sve[:, :], mhalf[:, 0:3], ALU.pow).then_inc(srs_ready, 1)
            pool.wait_ge(ld_small, 16 * 7)
            gather(0)

            def C_stage(b, k):
                if k == 0:
                    pow_(b, 0)
                    pool.wait_ge(x1_hi, b + 1)
                    pool.tensor_tensor(cx[1][:, :], x1T[:, :], cx[0][:, :].bitcast(F32), ALU.subtract).then_inc(x1_lo, 1)
                elif k == 1:
                    pool.wait_ge(gathered, (b + 1) * 16 * 3 * TT)
                    pool.wait_ge(normed, b * 3 + 1)
                    if not first(b):
                        pool.wait_ge(a_lo, b)
                    pool.tensor_tensor(tt[:, :, :], xh[:, :, :], gc[:, :, P:2 * P], ALU.mult).then_inc(ts_ready, 1)
                elif k == 2:
                    pow_(b, 1)
                    pool.tensor_tensor(ss[:, :, :], xh[:, :, :], gm[:, :, :], ALU.mult).then_inc(ts_ready, 1)
                elif k == 7:
                    pow_(b, 2)
                elif k == 9:
                    pool.wait_ge(f_hi, b + 1)
                    if not first(b):
                        pool.wait_ge(n_mm, (b - 1) * NMM + FC)
                    pool.tensor_tensor(fin[1][:, :], flat(xh), fin[0][:, :].bitcast(F32), ALU.subtract).then_inc(f_lo, 1)

            def keep_x(b):
                if not first(b):
                    pool.wait_ge(stored, b * 16)
                pool.wait_ge(x1_ready, b + 1)
                settled(pool)
                pool.tensor_copy(keep[:, :], x1T[:, :]).then_inc(kept, 1)

            def block_(b):
                for k in range(10):
                    C_stage(b, k)
                keep_x(b)

            block_(0)
            gather(1)
            with pool.Fori(1, NB - 1) as i:
                block_(i)
                pool.wait_ge(h_ready, i + 1)
                pool.wait_ge(ts_ready, i * 2 + 2)
                gather(i + 1)
            block_(NB - 1)


def kernel(**inputs):
    import numpy as np
    import concourse.bacc as bacc
    from concourse.bass_utils import run_bass_kernel_spmd as run

    g = {k: np.asarray(v) for k, v in inputs.items()}
    c1, f1, f0 = "L1_cond_", "L1_ffn_", "L0_ffn_"
    n = P

    def chunks(w):
        return w.reshape(-1, n, w.shape[1]).transpose(1, 0, 2).reshape(n, -1)

    def tiles(ix):
        return ix.reshape(-1, n).T

    def rows64(a):
        return np.concatenate([a, np.zeros((64 - a.shape[0], a.shape[1]), a.dtype)])

    st3 = ("mem", "noi", "res")
    zero = np.zeros((n, 8), np.float32)
    tb = []
    for name, at in (("cp_b", 0), ("tm_b", 0), ("ms_b", 5)):
        z = zero.copy()
        w = g[c1 + name].T
        z[:, at:at + w.shape[1]] = w
        tb.append(z)
    W1 = g[f0 + "W1"].reshape(-1, n)
    W2 = g[f0 + "W2"].transpose(0, 2, 1).reshape(-1, n)
    lay = {
        "xT": g["x"].reshape(-1, n).T,
        "cond_512T": g["cond_512"].T,
        "W_dec": g["L0_cond_W_dec"], "b_dec": g["L0_cond_b_dec"][None], "V": g["L0_cond_V"],
        "b2": g[f0 + "b2"], "W1T": W1.T, "W2T": chunks(W2),
        "pgb": np.concatenate([g[c1 + "pw_g"], g[c1 + "pw_b"]], 1),
        "ctg": np.concatenate([g[c1 + "cp_g"], g[c1 + "tm_g"]], 1), "msg": g[c1 + "ms_g"],
        "ixall": np.stack([tiles(g["itok_BxS_0_999"]), tiles(g["itok_BxS_0_4"]), tiles(g["mask_BxS_ik0"])], 1),
        "ic_row": g["itok_BxS_0_4"].reshape(1, -1), "im_row": g["mask_BxS_ik0"].reshape(1, -1),
        "states": np.stack([rows64(a) for a in (g["cond_512"].T, g["cond_64"].T, g["fside_Bx32_0"].T,
                                                g[c1 + "mem_W1"], g[c1 + "noi_W1"], g[c1 + "res_W1"])], 1),
        "earlyP": np.concatenate([g[c1 + k + "_W2"] for k in st3] + [chunks(g[c1 + "int_W1"]), g[c1 + "int_W2"]] + tb
                                 + [g[f0 + "Wg"].T] + [g[c1 + k + "_b1"][:, None] for k in st3], 1),
        "earlyB": np.concatenate([g[c1 + k + v] for v in ("_b2", "_g", "_be") for k in st3]
                                 + [g[c1 + "int_b1"], g[c1 + "aw"]]),
        "keepP": np.concatenate([np.eye(n, dtype=np.float32), g[f0 + "b1"].reshape(-1, n).T]
                                + [g[f1 + k + "_s"].reshape(-1, n).T for k in ("w1", "w2", "h1", "h2", "w3")]
                                + [np.zeros((n, 3), np.float32), g[c1 + "int_g"][:, None], g[c1 + "int_be"][:, None]], 1),
        "keepB": np.concatenate([g[f0 + "bg"], np.arange(8, 0, -1).astype(np.float32)]),
        "int_b2": g[c1 + "int_b2"][None],
        "w12T": np.concatenate([g[f1 + "w1_w"].T, g[f1 + "w2_w"].T], 1),
        "h1T": chunks(g[f1 + "h1_w"].T), "h2T": chunks(g[f1 + "h2_w"].T), "w3T": chunks(g[f1 + "w3_w"].T),
        "iota8": np.array([0, 1, 2, 3, 4, 0, 1, 2], np.float32)[:, None],
    }
    nc = bacc.Bacc("TRN2", target_bir_lowering=False, num_devices=1)
    arrays, A = {}, {}
    for name, a in lay.items():
        a = np.ascontiguousarray(a)
        arrays[name + "_in"] = a
        A[name] = nc.dram_tensor(name + "_in", a.shape, mybir.dt.from_np(a.dtype), kind="ExternalInput").ap()
    tok = lay["xT"].shape[1]
    out = nc.dram_tensor("outT", (n, tok), F32, kind="ExternalOutput").ap()
    build(nc, A, out)
    r = run(nc, [arrays], core_ids=[0])
    got = r.results[0]["outT"]
    return got.T.reshape(g["x"].shape)
```

```python
from contextlib import ExitStack
from functools import partial

import concourse.bass as bass
from concourse import mybir

ALU = mybir.AluOpType
ACT = mybir.ActivationFunctionType
AX_X = mybir.AxisListType.X
F32 = mybir.dt.float32
F32R = mybir.dt.float32r
I32 = mybir.dt.int32
U32 = mybir.dt.uint32

P = 128
EPS = 1e-5
MASKED = -3.0e38


class Steps:

    def __init__(self, eng, sem, per_block, b):
        self.eng, self.sem, self.n, self.b, self.k = eng, sem, per_block, b, 0

    def __call__(self, ins):
        self.k += 1
        ins.then_inc(self.sem, 1)
        self.eng.wait_ge(self.sem, self.b * self.n + self.k)

    def end(self):
        assert self.k == self.n, (self.k, self.n)


def build(nc, A, out):
    B, D = A["cond_512T"].shape[1], P
    TOK = A["xT"].shape[1]
    S = TOK // B
    T = 512
    NB = TOK // T
    TT = T // P
    BB = T // S
    MU, KR = A["cond_512T"].shape[0], A["V"].shape[0]
    E = A["b2"].shape[0]
    NH = A["W1T"].shape[1] // P
    HE = NH // E
    FC = A["w12T"].shape[1] // (2 * P)
    NP_, NC_, NM_ = A["pgb"].shape[0], A["ctg"].shape[0], A["msg"].shape[0]
    NI = NC_ + NM_
    RING = 3
    assert E == 8 and NI == 8 and NH % 4 == 0 and FC == 4

    with ExitStack() as ctx:
        def sb(name, shape, dt=F32, stack=ctx):
            return stack.enter_context(nc.sbuf_tensor(name, shape, dt))

        def parts(t, *widths):
            at, views = 0, []
            for w in widths:
                views.append(t[:, at:at + w])
                at += w
            return views

        def sem(name):
            return ctx.enter_context(nc.semaphore(name))

        bank = [ctx.enter_context(nc.psum_tensor(f"bank{i}", [P, T], F32)) for i in range(8)]
        HB = bank[0:4]
        OACC = bank[4]
        X0, X1, X2 = bank[5:8]

        W1 = [sb(f"W1_{p}", [P, NH * P], F32R) for p in "hl"]
        W2 = [sb(f"W2_{p}", [P, NH, P], F32R) for p in "hl"]
        w12 = [sb(f"w12_{p}", [P, 2, FC * P], F32R) for p in "hl"]
        h1w = [sb(f"h1w_{p}", [P, FC, FC * P], F32R) for p in "hl"]
        h2w = [sb(f"h2w_{p}", [P, FC, FC * P], F32R) for p in "hl"]
        w3 = [sb(f"w3_{p}", [P, FC, P], F32R) for p in "hl"]
        wmix = [sb(f"wmix_{p}", [P, 4, P], F32R) for p in "hl"]
        wint = [sb(f"wint_{p}", [P, P], F32R) for p in "hl"]
        wg = [sb(f"wg_{p}", [P, E], F32R) for p in "hl"]
        tab8 = [sb(f"tab8_{p}", [NI, P], F32R) for p in "hl"]
        vec = [sb(f"vec_{p}", [P, P], F32R) for p in "hl"]
        ib2 = [sb(f"ib2_{p}", [1, P], F32R) for p in "hl"]
        keepP = sb("keepP", [P, P + NH + 5 * FC + 2])
        ident, b1c, fsc, igb = parts(keepP, P, NH, 5 * FC, 2)
        identR = sb("identR", [P, P], F32R)
        onesR = sb("onesR", [1, P], F32R)
        Vw = sb("Vw", [KR, P])
        ub = sb("ub", [KR, B])
        b2e = sb("b2e", [40, P])
        keepB = sb("keepB", [P, 2 * E])
        bgt, desc8 = parts(keepB, E, E)
        iota8 = sb("iota8", [NI, 1])
        hs1 = sb("hs1", [P, FC])
        cs12 = sb("cs12", [P, FC])
        onesf = sb("onesf", [1, P])
        lowm = sb("lowm", [P, 7])
        lowr = sb("lowr", [1, 1])
        lowi = sb("lowi", [1, 1], I32)
        mhalf = sb("mhalf", [P, TT])
        ixall = sb("ixall", [P, 3, TOK // P], I32)

        early = ExitStack()
        stage = [sb(f"stage{i}", [P, 2048], stack=early) for i in range(2)]
        Wdec = sb("Wdec", [MU + 1, (D + 1) * KR], stack=early)
        Uall = sb("Uall", [P, B, KR], stack=early)
        muT = sb("muT", [MU + 1, B], stack=early)
        states = sb("states", [64, 6, P], stack=early)
        sT, sW1 = states[:, 0:3, :], states[:, 3:6, :]
        earlyP = sb("earlyP", [P, 10 * P + 3 * NI + E + 3], stack=early)
        sW2, iW1, iW2, tbT, wgf, sb1 = parts(earlyP, 3 * P, 6 * P, P, 3 * NI, E, 3)
        sW2 = sW2.rearrange("p (n d) -> p n d", n=3)
        iW1 = iW1.rearrange("p (n d) -> p n d", n=6)
        tbT = tbT.rearrange("p (n d) -> p n d", n=3)
        earlyB = sb("earlyB", [P, 10 * P + 6], stack=early)
        sbc, ibb, aw6 = parts(earlyB, 9 * P, P, 6)
        sbc = sbc.rearrange("p (v n d) -> p v n d", v=3, n=3)
        aw_e = sb("aw_e", [P, 6], stack=early)
        awx = sb("awx", [P, 4], stack=early)
        wsc = sb("wsc", [P, 6, P], stack=early)
        sz = sb("sz", [P, 3 * B], stack=early)
        sth = sb("sth", [P, 3 * B], stack=early)
        sa = sb("sa", [P, 3 * B], stack=early)
        sy = sb("sy", [P, 3, P], stack=early)
        syT = sb("syT", [P, 3 * B], stack=early)
        ib2f = sb("ib2f", [1, P], stack=early)
        wintf = sb("wintf", [P, P], stack=early)
        wmixf = sb("wmixf", [P, 4, P], stack=early)
        tab8f = sb("tab8f", [NI, P], stack=early)
        vecf = sb("vecf", [P, P], stack=early)
        sbn = sb("sbn", [P, 3, 6], stack=early)
        smv = sb("smv", [P, 3, 2], stack=early)
        sve = sb("sve", [P, 3], stack=early)
        srs = sb("srs", [P, 3], stack=early)
        early.close()

        hA = [sb(f"hA_{p}", [P, FC, T], F32R) for p in "hl"]
        gwb = sb("gwb", [P, E, T])
        hB = [sb(f"hB_{p}", [P, 4, T], F32R) for p in "hl"]
        G = sb("G", [P, RING, T])
        Q = sb("Q", [P, RING, T])
        cx, ct, cs_, ch = [[sb(f"c{k}_{p}", [P, T], F32R) for p in "hl"] for k in "xtsh"]
        xT = sb("xT", [P, T])
        xR = sb("xR", [P, T])
        Ub = sb("Ub", [P, BB, KR])
        rows = sb("rows", [40, T])
        idx8 = sb("idx8", [NI, T], I32)
        condR = [sb(f"cond_{p}", [P, T], F32R) for p in "hl"]
        xk = sb("xk", [P, 2, T])
        x1T, keep = xk[:, 0, :], xk[:, 1, :]
        oh8 = sb("oh8", [NI, T], F32R)
        fin = [sb(f"fin_{p}", [P, T], F32R) for p in "hl"]
        gp = sb("gp", [P, TT, 2 * P])
        gc = sb("gc", [P, TT, 2 * P])
        gm = sb("gm", [P, TT, P])
        norms = sb("norms", [P, 4, TT, P])
        xh, tt, ss, hh = [norms[:, i, :, :] for i in range(4)]
        bn6 = sb("bn6", [P, 3, TT, 6])
        mv = sb("mv", [P, 3, TT, 2])
        ve = sb("ve", [P, 3, TT])
        rstd = sb("rstd", [P, 3, TT])
        nmr = sb("nmr", [P, 3, TT])
        gt = sb("gt", [P, TT, E])
        g1 = sb("g1", [P, 2, TT, E])
        gk = sb("gk", [P, 2, TT, E])
        gmx = sb("gmx", [P, 2, TT])
        gkx = sb("gkx", [P, 2, TT])
        gd = sb("gd", [P, TT])
        gth = sb("gth", [P, TT])
        gw2 = sb("gw2", [P, 2, TT])
        gw = sb("gw", [P, TT, E])
        ixb = sb("ixb", [P, 3, TT], I32)

        U_dram = nc.dram_tensor("U_scratch", [P, B * KR], F32, kind="Internal").ap()
        gw_dram = nc.dram_tensor("gw_scratch", [E, T], F32, kind="Internal").ap()

        ld_cond, ld_small, ld_state = sem("ld_cond"), sem("ld_small"), sem("ld_state")
        passed = sem("passed")
        ld_w = [sem(f"ld_w{i}") for i in range(6)]
        ones_row, u_mm, u_even, u_odd, u_stored, ident_r = (sem(n) for n in (
            "ones_row", "u_mm", "u_even", "u_odd", "u_stored", "ident_r"))
        low_parts, low_max, low_row, low_flag = (sem(n) for n in ("low_parts", "low_max", "low_row", "low_flag"))
        w_hi, w_lo, small_src, small_hi, small_lo = (sem(n) for n in ("w_hi", "w_lo", "small_src", "small_hi", "small_lo"))
        aw_max, aw_exp, s_mm, sz_ready, s_th, sa_ready, sy_mm, sv_ready, srs_ready, sy_ready, syT_mm, syT_ready, wsc_ready, fold_mm, \
            ub_mm, dve_setup = (sem(n) for n in (
                "aw_max", "aw_exp", "s_mm", "sz_ready", "s_th", "sa_ready", "sy_mm", "sv_ready", "srs_ready", "sy_ready",
                "syT_mm", "syT_ready", "wsc_ready", "fold_mm", "ub_mm", "dve_setup"))
        x_in, xr_in, u_in, t_mm, t_ready, cond_mm, cond_hi, cond_lo = (sem(n) for n in (
            "x_in", "xr_in", "u_in", "t_mm", "t_ready", "cond_mm", "cond_hi", "cond_lo"))
        gate_mm, gate_steps, gate_d, gate_th, gw2_ready, gw_parts, gw_ready, gwT_mm, gwT_ready, gw_stored, gwb_in = (sem(n) for n in (
            "gate_mm", "gate_steps", "gate_d", "gate_th", "gw2_ready", "gw_parts", "gw_ready", "gwT_mm", "gwT_ready", "gw_stored", "gwb_in"))
        m_mm, m_gelu, m_mul, m_hi, m_lo, m_used, o_mm, x1_ready = (sem(n) for n in (
            "m_mm", "m_gelu", "m_mul", "m_hi", "m_lo", "m_used", "o_mm", "x1_ready"))
        x1_hi, x1_lo, xtok_mm, bn_steps, ve_ready, rstd_ready, nmr_ready, normed, ts_ready = (sem(n) for n in (
            "x1_hi", "x1_lo", "xtok_mm", "bn_steps", "ve_ready", "rstd_ready", "nmr_ready", "normed", "ts_ready"))
        h_steps, h_ready, oh_ready, idx8_in, ixb_ready, gathered, kept = (sem(n) for n in (
            "h_steps", "h_ready", "oh_ready", "idx8_in", "ixb_ready", "gathered", "kept"))
        tr_mm, tr_hi, tr_lo, z_mm, z_th, a_ready, a_hi, a_lo, y_mm, yT_mm, f_full, f_hi, f_lo = (sem(n) for n in (
            "tr_mm", "tr_hi", "tr_lo", "z_mm", "z_th", "a_ready", "a_hi", "a_lo", "y_mm", "yT_mm",
            "f_full", "f_hi", "f_lo"))
        n_mm, n_th, n_u, n_h, n_g, n_hi, n_lo, n_out, stored = (sem(n) for n in (
            "n_mm", "n_th", "n_u", "n_h", "n_g", "n_hi", "n_lo", "n_out", "stored"))

        NMM = 3 * FC + 1
        GATE_STEPS = 12
        PASSES = ((0, 0), (0, 1), (1, 0))
        NPIECE = 6
        NSET_W, NSMALL = 6, 6

        def settled(eng):
            eng.sem_inc(passed, 1)

        staged = [stage[0][:, :], stage[1][:, :], xk[:, :, :].rearrange("p a t -> p (a t)"),
                  norms[:, :, :, :].rearrange("p n t d -> p (n t d)"), stage[0][:, :], stage[1][:, 0:FC * P]]

        def flat(t):
            v = t[tuple(slice(None) for _ in t.shape)]
            return v if len(t.shape) == 2 else v.rearrange("p a b -> p (a b)")

        small_ops = [(wgf, (wg[0][:, :], wg[1][:, :])), (ib2f[:, :], (ib2[0][:, :], ib2[1][:, :])),
                     (wintf[:, :], (wint[0][:, :], wint[1][:, :])), (flat(wmixf), (flat(wmix[0]), flat(wmix[1]))),
                     (tab8f[:, :], (tab8[0][:, :], tab8[1][:, :])), (vecf[:, :], (vec[0][:, :], vec[1][:, :]))]

        block = ctx.enter_context(nc.Block())

        ORDER = {
            "PE": ("+A0 H0 H1 H2 -YT H3 H4 H5 O0 H6 O1 H7 O2 H8 O3 H9 O4 H10 O5 H11 O6 O7 H12 O8 H13 O9 H14 O10 H15 "
                  "O11 -F0 O12 -F1 O13 O14 O15 C0 +A1 -F2 -F3 +A2 Tt -F4 -F5 -F6 Ts -F7 Th +A4 Z -F8 -F9 -F10 -F11 "
                  "Y +B2 -F12 "),
            "ACT": ("hi10 g12 hi11 g13 hi12 g14 hi13 g15 hi14 hi15 -th0 -th1 -fh0 +chi xhi -th2 -fh1 -th3 nx -fh2 "
                   "-fh3 thi -fg4 -fh4 -fg5 nh shi +gth -fh5 hhi +gwT -fg6 -fh6 -fg7 -fh7 zt -fg8 ahi -fg9 -fh8 "
                   "-fh9 -fg10 -fh10 -fg11 -fh11 ny +g0 +g1 +hi0 +g2 +hi1 fhi +g3 +hi2 +g4 +hi3 +g5 +hi4 +g6 +hi5 "
                   "+g7 +hi6 +g8 +hi7 +g9 +hi8 +g10 +hi9 +g11 "),
            "DVE": ("lo1 q3 lo2 q4 lo3 q5 lo4 q6 lo5 q7 lo6 q8 lo7 q9 lo8 q10 lo9 q11 lo10 q12 lo11 q13 lo12 q14 "
                   "lo13 q15 lo14 lo15 +tb -u0 x1 -u1 st0 -fl0 -u2 nm0 +clo -fl1 -u3 -fl2 -fl3 h1 oh tlo nm1 +top "
                   "h0 +gw slo hlo -fl4 -fl5 -fl6 -fl7 a -fl8 alo -fl9 -fl10 -fl11 st2 -fo nm2 +q0 +q1 ff +lo0 +q2 "),
            "Pool": ("-xlo -pw2 gath -flo -keep pw0 t s pw1 "),
        }

        def turn_of(steps, order, i, extra=None, done=()):
            for word in order.split():
                off = {"-": -1, "+": 1}.get(word[0], 0)
                word = word.lstrip("+-")
                name = word.rstrip("0123456789")
                b = i + off if off else i
                if isinstance(i, int) and not 0 <= b < NB or word in done:
                    continue
                if word == name:
                    steps[name](b)
                else:
                    steps[name](b, int(word[len(name):]))
                if extra and isinstance(i, int) and (i, word) in extra:
                    extra[(i, word)]()

        def begin(steps, order, extra=None, done=()):
            turn_of(steps, order, -1, extra, done)
            turn_of(steps, order, 0, extra)

        def go_on(eng, steps, order):
            turn_of(steps, order, 1)
            with eng.Fori(2, NB - 1) as i:
                turn_of(steps, order, i)
            turn_of(steps, order, NB - 1)
            turn_of(steps, order, NB)

        def first(b, n=1):
            return isinstance(b, int) and b < n

        @block.sync
        def _(sp):
            sp.dma_start(Wdec[0:MU, :], A["W_dec"]).then_inc(ld_cond, 16)
            sp.dma_start(Wdec[MU:MU + 1, :], A["b_dec"]).then_inc(ld_cond, 16)
            sp.dma_start(muT[0:MU, :], A["cond_512T"]).then_inc(ld_cond, 16)
            sp.dma_start(states[:, :, :], A["states"]).then_inc(ld_state, 16)
            sp.dma_start(earlyP[:, :], A["earlyP"]).then_inc(ld_state, 16)
            sp.dma_start(earlyB[:, :], A["earlyB"].partition_broadcast(P)).then_inc(ld_state, 16)
            for dst, src in ((keepP[:, :], "keepP"), (Vw[:, :], "V"), (b2e[32:40, :], "b2"), (iota8[:, :], "iota8"),
                             (ixall[:, :, :], "ixall"), (ib2f[:, :], "int_b2")):
                sp.dma_start(dst, A[src]).then_inc(ld_small, 16)
            sp.dma_start(keepB[:, :], A["keepB"].partition_broadcast(P)).then_inc(ld_small, 16)

            def load_w(n):
                src = ("W1T", "W2T", "w12T", "h1T", "h2T", "w3T")[n]
                if n >= 4:
                    sp.wait_ge(w_lo, n - 3)
                sp.dma_start(staged[n], A[src]).then_inc(ld_w[n], 16)

            def load_x(b):
                if not first(b):
                    sp.wait_ge(t_mm, b)
                sp.dma_start(xT[:, :], A["xT"][:, bass.ds(b * T, T)]).then_inc(x_in, 16)
                sp.dma_start(Ub[:, :, :], U_dram[:, bass.ds(b * BB * KR, BB * KR)]).then_inc(u_in, 16)

            def load_xr(b):
                if not first(b):
                    sp.wait_ge(x1_ready, b)
                sp.dma_start(xR[:, :], A["xT"][:, bass.ds(b * T, T)]).then_inc(xr_in, 16)

            def load_idx(b):
                if not first(b):
                    sp.wait_ge(oh_ready, b)
                sp.dma_start(idx8[0:NC_, :], A["ic_row"][:, bass.ds(b * T, T)]
                             .partition_broadcast(NC_)).then_inc(idx8_in, 16)
                sp.dma_start(idx8[NC_:NI, :], A["im_row"][:, bass.ds(b * T, T)]
                             .partition_broadcast(NM_)).then_inc(idx8_in, 16)

            def spread_gw(b):
                sp.wait_ge(gwT_ready, b + 1)
                if not first(b):
                    sp.wait_ge(gwb_in, b * 16)
                    sp.wait_ge(m_mul, b * NH)
                sp.dma_start(gw_dram[:, :], rows[32:40, :]).then_inc(gw_stored, 16)
                sp.wait_ge(gw_stored, b * 16 + 16)
                sp.dma_start(gwb[:, :, :], gw_dram.partition_broadcast(P)).then_inc(gwb_in, 16)

            def store(b):
                sp.wait_ge(n_out, b + 1)
                sp.dma_start(out[:, bass.ds(b * T, T)], keep[:, :]).then_inc(stored, 16)

            for n in range(4):
                load_w(n)
            sp.wait_ge(u_even, KR // 2)
            sp.wait_ge(u_odd, KR // 2)
            sp.dma_start(U_dram[:, :], Uall[:, :, :]).then_inc(u_stored, 16)
            sp.wait_ge(u_stored, 16)
            load_x(0)
            load_xr(0)
            load_idx(0)
            load_x(1)
            load_w(4)
            spread_gw(0)
            load_w(5)

            def turn(i, n=2):
                spread_gw(i + 1)
                load_xr(i + 1)
                if n == 2:
                    load_x(i + 2)
                load_idx(i + 1)
                if not isinstance(i, int) or i:
                    store(i - 1)

            turn(0)
            with sp.Fori(1, NB - 2) as i:
                turn(i)
            turn(NB - 2, n=1)
            store(NB - 2)
            store(NB - 1)
            sp.wait_ge(stored, 16 * NB)

        @block.tensor
        def _(pe):
            def A0(b):
                pe.wait_ge(x_in, b * 16 + 16)
                pe.wait_ge(u_in, b * 16 + 16)
                if not first(b):
                    pe.wait_ge(gwT_ready, b)
                for j in range(BB):
                    mm = pe.matmul(X0[0:KR, j * S:(j + 1) * S], Ub[:, j, :], xT[:, j * S:(j + 1) * S],
                                   start=True, stop=True)
                mm.then_inc(t_mm, 1)

            def A1(b):
                pe.wait_ge(t_ready, b + 1)
                if not first(b):
                    pe.wait_ge(x1_ready, b)
                pe.matmul(OACC[:, :], Vw[:, :], rows[0:KR, :], start=True, stop=True).then_inc(cond_mm, 1)

            def A2(b):
                pe.wait_ge(cond_lo, b + 1)
                for t in range(TT):
                    for n, (a, w_) in enumerate(((0, 0), (0, 1), (1, 0))):
                        mm = pe.matmul(X0[:, t * E:(t + 1) * E], condR[a][:, t * P:(t + 1) * P], wg[w_][:, :],
                                       start=(n == 0), stop=(n == 2))
                mm.then_inc(gate_mm, 1)

            def A4(b):
                pe.wait_ge(gw_ready, b + 1)
                for t in range(TT):
                    mm = pe.transpose(X0[0:E, t * P:(t + 1) * P], gw[:, t, :], ident)
                mm.then_inc(gwT_mm, 1)

            def B2(b):
                pe.wait_ge(gwT_ready, b + 1)
                pe.wait_ge(cond_lo, b + 1)
                pe.matmul(OACC[:, :], b2e[32:40, :], rows[32:40, :], start=True, stop=False)

            def H(b, c):
                if c == 0:
                    pe.wait_ge(cond_lo, b + 1)
                if c >= 4:
                    pe.wait_ge(m_gelu, b * NH + c - 3)
                elif not first(b, 2):
                    if c == 0:
                        pe.wait_ge(n_out, b - 1)
                    else:
                        pe.wait_ge(n_g, (b - 1) * 2 * FC - 3 + c)
                elif not first(b):
                    pe.wait_ge(m_gelu, b * NH - 3 + c)
                for n, (a, x_) in enumerate(PASSES):
                    mm = pe.matmul(HB[c % 4][:, :], W1[a][:, c * P:(c + 1) * P], condR[x_][:, :],
                                   start=(n == 0), stop=(n == 2))
                mm.then_inc(m_mm, 1)

            def O(b, c):
                pe.wait_ge(m_lo, b * NH + c + 1)
                for n, (a, x_) in enumerate(((0, 0), (1, 0), (0, 1))):
                    mm = pe.matmul(OACC[:, :], W2[a][:, c, :], hB[x_][:, c % 4, :],
                                   start=False, stop=(c == NH - 1 and n == 2))
                mm.then_inc(m_used, 1)

            def C0(b):
                pe.wait_ge(x1_ready, b + 1)
                if not first(b):
                    pe.wait_ge(f_full, b)
                for t in range(TT):
                    mm = pe.transpose(X1[:, t * P:(t + 1) * P], x1T[:, t * P:(t + 1) * P], ident)
                mm.then_inc(xtok_mm, 1)

            def turned(src, dst):
                for t in range(TT):
                    mm = pe.transpose(dst[:, t * P:(t + 1) * P], src[:, t, :], ident)
                mm.then_inc(tr_mm, 1)

            def Tt(b):
                pe.wait_ge(ts_ready, b * 2 + 1)
                if not first(b):
                    pe.wait_ge(normed, b * 3)
                turned(tt, X2)

            def Ts(b):
                pe.wait_ge(ts_ready, b * 2 + 2)
                pe.wait_ge(normed, b * 3 + 1)
                turned(ss, X1)

            def Th(b):
                pe.wait_ge(h_ready, b + 1)
                pe.wait_ge(tr_lo, b * 3 + 1)
                turned(hh, X2)

            def Z(b):
                pe.wait_ge(tr_lo, b * 3 + 2)
                seqs = identR[:, bass.ds(b * BB, BB)].unsqueeze(2).broadcast_to([P, BB, S])
                pe.matmul(X1[:, :], vec[0][:, :], seqs, start=True, stop=False)
                pe.matmul(X1[:, :], vec[1][:, :], seqs, start=False, stop=False)
                pe.wait_ge(oh_ready, b + 1)
                pe.matmul(X1[:, :], tab8[0][:, :], oh8[0:NI, :], start=False, stop=False)
                pe.matmul(X1[:, :], tab8[1][:, :], oh8[0:NI, :], start=False, stop=False)
                pe.wait_ge(x1_lo, b + 1)
                for m, src in enumerate((cx, ct, cs_, ch)):
                    if m == 3:
                        pe.wait_ge(tr_lo, b * 3 + 3)
                    for n, (a, x_) in enumerate(((0, 0), (0, 1), (1, 0))):
                        mm = pe.matmul(X1[:, :], wmix[a][:, m, :], src[x_][:, :],
                                       start=False, stop=(m == 3 and n == 2))
                mm.then_inc(z_mm, 1)

            def Y(b):
                pe.wait_ge(a_lo, b + 1)
                pe.wait_ge(tr_lo, b * 3 + 3)
                for t in range(TT):
                    o = X2[:, t * P:(t + 1) * P]
                    pe.matmul(o, onesR[:, :], ib2[0][:, :], start=True, stop=False)
                    pe.matmul(o, onesR[:, :], ib2[1][:, :], start=False, stop=False)
                    for n, (x_, a) in enumerate(((0, 0), (0, 1), (1, 0))):
                        mm = pe.matmul(o, ct[x_][:, t * P:(t + 1) * P], wint[a][:, :], start=False, stop=(n == 2))
                mm.then_inc(y_mm, 1)

            def YT(b):
                pe.wait_ge(normed, b * 3 + 3)
                pe.wait_ge(a_ready, b + 1)
                for t in range(TT):
                    mm = pe.transpose(X1[:, t * P:(t + 1) * P], hh[:, t, :], ident)
                mm.then_inc(yT_mm, 1)

            def F(passes, b, k):
                last = isinstance(b, int) and b == NB - 1
                end = len(passes) - 1
                if k < FC:
                    if k == 0:
                        pe.wait_ge(f_lo, b + 1)
                        if last:
                            pe.wait_ge(n_out, b)
                            pe.wait_ge(n_g, b * 2 * FC)
                        else:
                            pe.wait_ge(m_gelu, (b + 2) * NH - 2)
                    elif k == 1:
                        if not last:
                            pe.wait_ge(m_gelu, (b + 2) * NH)
                    elif k >= 2:
                        pe.wait_ge(n_h, b * FC + k - 1)
                    for w_ in range(2):
                        o = HB[2 * (k % 2) + w_]
                        for n, (a, x_) in enumerate(passes):
                            mm = pe.matmul(o[:, :], w12[a][:, w_, k * P:(k + 1) * P], fin[x_][:, :],
                                           start=(n == 0), stop=(n == end))
                    mm.then_inc(n_mm, 1)
                    return
                layer, c = (k // FC, k % FC)
                w, src = ((h1w, hA), (h2w, hB), (w3, hA))[layer - 1]
                if layer == 1:
                    pe.wait_ge(n_h, b * FC + (3 if c < 2 else 4))
                elif layer == 2:
                    pe.wait_ge(n_g, b * 2 * FC + c + 1)
                else:
                    pe.wait_ge(n_g, b * 2 * FC + FC + 1)
                for kc in range(FC):
                    if c == 0:
                        pe.wait_ge(n_lo, b * 3 * FC + (layer - 1) * FC + kc + 1)
                    for n, (a, x_) in enumerate(passes):
                        mm = pe.matmul(HB[c][:, :], w[a][:, kc, c * P:(c + 1) * P], src[x_][:, kc, :],
                                       start=(kc == 0 and n == 0), stop=(kc == FC - 1 and n == end))
                mm.then_inc(n_mm, 1)

            steps = {"A": lambda b, k: (A0, A1, A2, None, A4)[k](b), "B": lambda b, k: B2(b), "H": H, "O": O,
                     "C": lambda b, k: C0(b), "Tt": Tt, "Ts": Ts, "Th": Th, "Z": Z, "Y": Y, "YT": YT,
                     "F": partial(F, PASSES)}

            def low_over_partitions():
                pe.wait_ge(low_max, 1)
                pe.wait_ge(m_gelu, NH)
                pe.transpose(HB[3][0:1, 0:P], lowm[:, NPIECE:NPIECE + 1], ident).then_inc(low_row, 1)

            pe.wait_ge(ld_cond, 48)
            pe.wait_ge(ones_row, 1)
            wd = Wdec[:, :].rearrange("m (i k) -> m i k", k=KR)
            for k in range(KR):
                if k >= 4:
                    pe.wait_ge(u_odd if k % 2 else u_even, k // 2 - 1)
                pe.matmul(HB[k % 4][:, 0:B], wd[:, 0:D, k], muT[:, :], start=True, stop=True).then_inc(u_mm, 1)
            pe.matmul(X0[0:KR, 0:B], wd[:, D, :], muT[:, :], start=True, stop=True).then_inc(ub_mm, 1)
            pe.wait_ge(ld_state, 16 * 3)
            for n, k in enumerate((64, 64, 32)):
                mm = pe.matmul(X1[:, n * B:(n + 1) * B], sW1[0:k, n, :], sT[0:k, n, :], start=True, stop=True)
            mm.then_inc(s_mm, 1)
            pe.wait_ge(sa_ready, 1)
            for n in range(3):
                mm = pe.matmul(X2[:, n * P:(n + 1) * P], sa[:, n * B:(n + 1) * B], sW2[:, n, :], start=True, stop=True)
            mm.then_inc(sy_mm, 1)
            A0(0)
            pe.wait_ge(sy_ready, 1)
            pe.wait_ge(ld_small, 16 * 7)
            for n in range(3):
                mm = pe.transpose(X1[:, n * P:(n + 1) * P], sy[:, n, :], ident)
            mm.then_inc(syT_mm, 1)
            A1(0)
            pe.wait_ge(syT_ready, 1)
            pe.wait_ge(wsc_ready, 1)
            for n in range(3):
                pe.matmul(X2[:, 0:P], syT[:, n * B:(n + 1) * B], wsc[:, 2 + n, :], start=(n == 0), stop=(n == 2))
            for n, w_ in enumerate((0, 1, 5)):
                mm = pe.matmul(X1[0:NI, 3 * P:4 * P], tbT[:, n, :], wsc[:, w_, :], start=(n == 0), stop=(n == 2))
            mm.then_inc(fold_mm, 1)
            pe.wait_ge(small_lo, 1)
            A2(0)
            pe.wait_ge(small_lo, NSMALL)
            pe.wait_ge(w_lo, 1)
            begin(steps, ORDER["PE"], {(0, "Z"): low_over_partitions}, done=("A0", "A1", "A2"))
            pe.wait_ge(low_flag, 1)
            flag = pe.value_load(lowi[0:1, 0:1], min_val=0, max_val=1)

            with pe.If(flag > 0):
                go_on(pe, steps, ORDER["PE"])
            with pe.Else():
                go_on(pe, dict(steps, F=partial(F, PASSES[0:2])), ORDER["PE"])

        @block.scalar
        def _(act):
            def big_hi(n, dst):
                act.wait_ge(ld_w[n], 16)
                act.activation(dst, staged[n], ACT.Copy).then_inc(w_hi, 1)

            def late_hi(*ns):
                for n in ns:
                    big_hi(n, flat((w12, h1w, h2w, w3)[n - 2][0]))

            def chi(b):
                act.wait_ge(cond_mm, b + 1)
                if not first(b):
                    act.wait_ge(m_mm, b * NH)
                act.activation(condR[0][:, :], OACC[:, :], ACT.Copy).then_inc(cond_hi, 1)

            def gth_(b):
                act.wait_ge(gate_d, b + 1)
                act.activation(gth[:, :], gd[:, :], ACT.Tanh, scale=0.5).then_inc(gate_th, 1)

            def gwT(b):
                act.wait_ge(gwT_mm, b + 1)
                if not first(b):
                    act.wait_ge(gw_stored, b * 16)
                    act.wait_ge(m_mm, b * NH)
                act.activation(rows[32:40, :], X0[0:E, :], ACT.Copy).then_inc(gwT_ready, 1)

            def g(b, c):
                if c == 0:
                    if first(b):
                        act.wait_ge(small_lo, NSMALL)
                    else:
                        act.wait_ge(m_mul, b * NH)
                    if not first(b, 2):
                        act.wait_ge(n_lo, (b - 1) * 3 * FC)
                act.wait_ge(m_mm, b * NH + c + 1)
                if c >= RING:
                    act.wait_ge(m_mul, b * NH + c - RING + 1)
                act.activation(G[:, c % RING, :], HB[c % 4][:, :], ACT.Gelu, bias=b1c[:, c:c + 1]).then_inc(m_gelu, 1)

            def hi(b, c):
                act.wait_ge(m_mul, b * NH + c + 1)
                if c >= 4:
                    act.wait_ge(m_used, b * NH + c - 3)
                elif not first(b):
                    act.wait_ge(m_used, b * NH - 3 + c)
                    if not first(b, 2):
                        act.wait_ge(n_mm, (b - 1) * NMM - 1)
                act.activation(hB[0][:, c % 4, :], Q[:, c % RING, :], ACT.Copy).then_inc(m_hi, 1)

            def norm(b, n, src, dst):
                act.wait_ge(nmr_ready, b * 3 + n + 1)
                for t in range(TT):
                    ins = act.activation(dst[:, t, :], src(t), ACT.Identity, scale=rstd[:, n, t:t + 1],
                                         bias=nmr[:, n, t:t + 1])
                ins.then_inc(normed, 1)

            def xhi(b):
                act.wait_ge(x1_ready, b + 1)
                if not first(b):
                    act.wait_ge(z_mm, b)
                act.activation(cx[0][:, :], x1T[:, :], ACT.Copy).then_inc(x1_hi, 1)

            def nx(b):
                if not first(b):
                    act.wait_ge(ts_ready, b * 2)
                    act.wait_ge(f_lo, b)
                norm(b, 0, lambda t: X1[:, t * P:(t + 1) * P], xh)

            def nh(b):
                norm(b, 1, lambda t: hh[:, t, :], hh)

            def ny(b):
                norm(b, 2, lambda t: X2[:, t * P:(t + 1) * P], hh)

            def turned_hi(b, n):
                src, dst = ((X2, ct), (X1, cs_), (X2, ch))[n]
                act.wait_ge(tr_mm, b * 3 + n + 1)
                if n == 0 and not first(b):
                    act.wait_ge(y_mm, b)
                act.activation(dst[0][:, :], src[:, :], ACT.Copy).then_inc(tr_hi, 1)

            def zt(b):
                act.wait_ge(z_mm, b + 1)
                act.activation(flat(tt), X1[:, :], ACT.Tanh, scale=0.5).then_inc(z_th, 1)

            def ahi(b):
                act.wait_ge(a_ready, b + 1)
                act.activation(ct[0][:, :], flat(ss), ACT.Copy).then_inc(a_hi, 1)

            def fhi(b):
                act.wait_ge(f_full, b + 1)
                if not first(b):
                    act.wait_ge(n_mm, (b - 1) * NMM + FC)
                act.activation(fin[0][:, :], flat(xh), ACT.Copy).then_inc(f_hi, 1)

            def last(b):
                return isinstance(b, int) and b == NB - 1

            def th(b, k):
                act.wait_ge(n_mm, b * NMM + k + 1)
                if k == 0:
                    if not first(b):
                        act.wait_ge(n_lo, b * 3 * FC)
                    if not last(b):
                        act.wait_ge(m_mul, (b + 2) * NH)
                elif k >= RING:
                    act.wait_ge(n_h, b * FC + k - RING + 1)
                act.activation(G[:, k % RING, :], HB[2 * (k % 2)][:, :], ACT.Tanh, scale=hs1[:, k:k + 1]).then_inc(n_th, 1)

            def fg(b, k):
                act.wait_ge(n_mm, b * NMM + k + 1)
                act.wait_ge(n_lo, b * 3 * FC + k - RING + 1)
                act.activation(G[:, k % RING, :], HB[k % FC][:, :], ACT.Gelu, scale=fsc[:, k + FC:k + FC + 1])\
                   .then_inc(n_g, 1)

            def fh(b, k):
                c = k % FC
                if k < FC:
                    act.wait_ge(n_h, b * FC + k + 1)
                    if k == 0 and not first(b):
                        act.wait_ge(n_mm, b * NMM)
                    src, dst = Q, hA
                else:
                    act.wait_ge(n_g, b * 2 * FC + k - FC + 1)
                    if k == FC and not last(b):
                        act.wait_ge(m_used, (b + 2) * NH)
                    src, dst = G, (hB if k < 2 * FC else hA)
                act.activation(dst[0][:, c, :], src[:, k % RING, :], ACT.Copy).then_inc(n_hi, 1)

            steps = {"chi": chi, "gth": gth_, "gwT": gwT, "g": g, "hi": hi, "xhi": xhi, "nx": nx, "nh": nh, "ny": ny,
                     "thi": lambda b: turned_hi(b, 0), "shi": lambda b: turned_hi(b, 1), "hhi": lambda b: turned_hi(b, 2),
                     "zt": zt, "ahi": ahi, "fhi": fhi, "th": th, "fg": fg, "fh": fh}
            act.wait_ge(aw_max, 1)
            act.activation(aw_e[:, :], aw6, ACT.Exp, bias=awx[:, 1:2], accum_out=awx[:, 2:3]).then_inc(aw_exp, 1)
            for k in range(1, KR, 2):
                act.wait_ge(u_mm, k + 1)
                act.activation(Uall[:, :, k], HB[k % 4][:, 0:B], ACT.Copy).then_inc(u_odd, 1)
            act.wait_ge(sz_ready, 1)
            act.activation(sth[:, :], sz[:, :], ACT.Tanh, scale=0.5).then_inc(s_th, 1)

            big_hi(0, W1[0][:, :])
            big_hi(1, flat(W2[0]))
            act.wait_ge(ld_small, 16 * 7)
            act.activation(identR[:, :], ident[:, :], ACT.Copy).then_inc(ident_r, 1)

            def small_hi_(n):
                src, dst = small_ops[n]
                act.wait_ge(small_src, n + 1)
                act.activation(dst[0], src, ACT.Copy).then_inc(small_hi, 1)

            small_hi_(0)
            act.wait_ge(syT_mm, 1)
            act.activation(syT[:, :], X1[:, 0:3 * B], ACT.Copy).then_inc(syT_ready, 1)
            chi(0)
            for n in range(1, NSMALL):
                small_hi_(n)
            late_hi(2, 3)
            begin(steps, ORDER["ACT"], {(-1, "gwT"): partial(late_hi, 4, 5)}, done=("chi",))
            go_on(act, steps, ORDER["ACT"])

        @block.vector
        def _(dve):
            def big_lo(n, w):
                dve.wait_ge(w_hi, n + 1)
                dst = flat(w[1])
                dve.tensor_tensor(dst, staged[n], flat(w[0]).bitcast(F32), ALU.subtract)\
                   .then_inc(w_lo, 1)

            def late_lo(*ns):
                for n in ns:
                    big_lo(n, (w12, h1w, h2w, w3)[n - 2])

            def low_check(n):
                w, half = ((w12, None), (h1w, 0), (h1w, 1), (h2w, 0), (h2w, 1), (w3, None))[n]
                v = flat(w[1]).bitcast(F32)
                if half is not None:
                    v = v[:, half * (FC * FC * P // 2):(half + 1) * (FC * FC * P // 2)]
                dve.wait_ge(w_lo, 6)
                dve.tensor_reduce(lowm[:, n:n + 1], v, AX_X, ALU.max, apply_absolute_value=True).then_inc(low_parts, 1)
                if n == NPIECE - 1:
                    dve.wait_ge(low_parts, NPIECE)
                    dve.reduce_max(lowm[:, NPIECE:NPIECE + 1], lowm[:, 0:NPIECE], AX_X).then_inc(low_max, 1)

            def statistics(b, n, src, step):
                for t in range(TT):
                    ins = dve.bn_stats(bn6[:, n, t, :], src(t))
                step(ins)
                settled(dve)
                for t in range(TT):
                    ins = dve.bn_aggr(mv[:, n, t, :], bn6[:, n, t, :])
                step(ins)
                dve.tensor_scalar(ve[:, n, :], mv[:, n, :, 1], EPS, None, ALU.add).then_inc(ve_ready, 1)

            def offset(b, n):
                dve.wait_ge(rstd_ready, b * 3 + n + 1)
                dve.scalar_tensor_tensor(out=nmr[:, n, :], in0=mv[:, n, :, 0], scalar=-1.0, in1=rstd[:, n, :],
                                         op0=ALU.mult, op1=ALU.mult).then_inc(nmr_ready, 1)

            def turned_lo(b, n):
                src, dst = ((X2, ct), (X1, cs_), (X2, ch))[n]
                dve.wait_ge(tr_hi, b * 3 + n + 1)
                dve.tensor_tensor(dst[1][:, :], src[:, :], dst[0][:, :].bitcast(F32), ALU.subtract).then_inc(tr_lo, 1)

            def per_tile(v):
                return v.unsqueeze(2).broadcast_to([P, TT, E])

            def tb(b):
                dve.wait_ge(t_mm, b + 1)
                if not first(b):
                    dve.wait_ge(cond_mm, b)
                dve.tensor_tensor(rows[0:KR, :].rearrange("k (b s) -> k b s", b=BB),
                                  X0[0:KR, :].rearrange("k (b s) -> k b s", b=BB),
                                  ub[:, bass.ds(b * BB, BB)].unsqueeze(2).broadcast_to([KR, BB, S]), ALU.add)\
                   .then_inc(t_ready, 1)

            def clo(b):
                dve.wait_ge(cond_hi, b + 1)
                dve.tensor_tensor(condR[1][:, :], OACC[:, :], condR[0][:, :].bitcast(F32), ALU.subtract)\
                   .then_inc(cond_lo, 1)

            def top(b):
                step = Steps(dve, gate_steps, GATE_STEPS, b)
                dve.wait_ge(gate_mm, b + 1)
                if not first(b):
                    dve.wait_ge(gw_ready, b)
                step(dve.tensor_tensor(gt[:, :, :], X0[:, 0:TT * E].rearrange("p (t e) -> p t e", t=TT),
                                       bgt.unsqueeze(1).broadcast_to([P, TT, E]), ALU.add))
                for r in range(2):
                    step(dve.reduce_max(gmx[:, r, :], gt[:, :, :], AX_X))
                    step(dve.tensor_tensor(gk[:, r, :, :], gt[:, :, :], per_tile(gmx[:, r, :]), ALU.is_equal))
                    step(dve.tensor_tensor(gk[:, r, :, :], gk[:, r, :, :],
                                           desc8.unsqueeze(1).broadcast_to([P, TT, E]), ALU.mult))
                    step(dve.reduce_max(gkx[:, r, :], gk[:, r, :, :], AX_X))
                    step(dve.tensor_tensor(g1[:, r, :, :], gk[:, r, :, :], per_tile(gkx[:, r, :]), ALU.is_equal))
                    if r == 0:
                        step(dve.scalar_tensor_tensor(out=gt[:, :, :], in0=g1[:, 0, :, :], scalar=MASKED,
                                                      in1=gt[:, :, :], op0=ALU.mult, op1=ALU.add))
                dve.tensor_tensor(gd[:, :], gmx[:, 0, :], gmx[:, 1, :], ALU.subtract).then_inc(gate_d, 1)
                step.end()

            def gw_(b):
                dve.wait_ge(gate_th, b + 1)
                dve.tensor_scalar(gw2[:, 0, :], gth[:, :], 0.5, 0.5, ALU.mult, ALU.add)
                dve.tensor_scalar(gw2[:, 1, :], gth[:, :], -0.5, 0.5, ALU.mult, ALU.add).then_inc(gw2_ready, 1)
                dve.wait_ge(gw2_ready, b + 1)
                for r in range(2):
                    ins = dve.tensor_tensor(g1[:, r, :, :], g1[:, r, :, :], per_tile(gw2[:, r, :]), ALU.mult)
                ins.then_inc(gw_parts, 1)
                dve.wait_ge(gw_parts, b + 1)
                if not first(b):
                    dve.wait_ge(gwT_mm, b)
                dve.tensor_tensor(gw[:, :, :], g1[:, 0, :, :], g1[:, 1, :, :], ALU.add).then_inc(gw_ready, 1)

            def q(b, c):
                if c == 0:
                    dve.wait_ge(gwb_in, b * 16 + 16)
                    if not first(b):
                        dve.wait_ge(m_lo, b * NH)
                    if not first(b, 2):
                        dve.wait_ge(n_lo, (b - 1) * 3 * FC)
                dve.wait_ge(m_gelu, b * NH + c + 1)
                if c >= RING:
                    dve.wait_ge(m_lo, b * NH + c - RING + 1)
                dve.tensor_tensor(Q[:, c % RING, :], G[:, c % RING, :], gwb[:, c // HE, :], ALU.mult).then_inc(m_mul, 1)

            def lo(b, c):
                dve.wait_ge(m_hi, b * NH + c + 1)
                dve.tensor_tensor(hB[1][:, c % 4, :], Q[:, c % RING, :], hB[0][:, c % 4, :].bitcast(F32), ALU.subtract)\
                   .then_inc(m_lo, 1)

            def x1(b):
                dve.wait_ge(m_used, b * NH + NH)
                dve.wait_ge(xr_in, b * 16 + 16)
                if not first(b):
                    dve.wait_ge(kept, b)
                    dve.wait_ge(x1_lo, b)
                    dve.wait_ge(xtok_mm, b)
                dve.tensor_tensor(x1T[:, :], OACC[:, :], xR[:, :], ALU.add).then_inc(x1_ready, 1)

            def st0(b):
                if not first(b):
                    dve.wait_ge(f_full, b)
                dve.wait_ge(xtok_mm, b + 1)
                statistics(b, 0, lambda t: X1[:, t * P:(t + 1) * P], Steps(dve, bn_steps, 6, b))

            def h1(b):
                step = Steps(dve, h_steps, 2, b)
                dve.wait_ge(normed, b * 3 + 1)
                dve.wait_ge(gathered, (b + 1) * 16 * 3 * TT)
                if not first(b):
                    dve.wait_ge(yT_mm, b)
                step(dve.tensor_tensor(hh[:, :, :], xh[:, :, :], gp[:, :, 0:P], ALU.mult))
                step(dve.tensor_tensor(hh[:, :, :], hh[:, :, :], gp[:, :, P:2 * P], ALU.add))
                step.end()
                step = Steps(dve, bn_steps, 6, b)
                step.k = 2
                statistics(b, 1, lambda t: hh[:, t, :], step)

            def oh(b):
                dve.wait_ge(idx8_in, (b + 1) * 32)
                if not first(b):
                    dve.wait_ge(z_mm, b)
                dve.tensor_scalar(oh8[:, :], idx8[:, :], iota8[:, :], None, ALU.is_equal).then_inc(oh_ready, 1)

            def h(b):
                dve.wait_ge(normed, b * 3 + 2)
                dve.tensor_tensor(hh[:, :, :], hh[:, :, :], gc[:, :, 0:P], ALU.mult).then_inc(h_ready, 1)

            def a(b):
                dve.wait_ge(z_th, b + 1)
                dve.scalar_tensor_tensor(out=flat(ss), in0=flat(tt), scalar=1.0, in1=X1[:, :],
                                         op0=ALU.add, op1=ALU.mult).then_inc(a_ready, 1)

            def alo(b):
                dve.wait_ge(a_hi, b + 1)
                dve.tensor_tensor(ct[1][:, :], flat(ss), ct[0][:, :].bitcast(F32), ALU.subtract).then_inc(a_lo, 1)

            def st2(b):
                step = Steps(dve, bn_steps, 6, b)
                step.k = 4
                dve.wait_ge(y_mm, b + 1)
                statistics(b, 2, lambda t: X2[:, t * P:(t + 1) * P], step)
                step.end()

            def ff(b):
                dve.wait_ge(yT_mm, b + 1)
                dve.tensor_scalar(flat(xh), X1[:, :], igb[:, 0:1], igb[:, 1:2], ALU.mult, ALU.add).then_inc(f_full, 1)

            def u(b, k):
                dve.wait_ge(n_th, b * FC + k + 1)
                if k == 0:
                    last = isinstance(b, int) and b == NB - 1
                    dve.wait_ge(n_lo, b * 3 * FC) if last else dve.wait_ge(m_lo, (b + 2) * NH)
                elif k >= RING:
                    dve.wait_ge(n_lo, b * 3 * FC + k - RING + 1)
                dve.scalar_tensor_tensor(out=Q[:, k % RING, :], in0=G[:, k % RING, :], scalar=1.0,
                                         in1=HB[2 * (k % 2)][:, :], op0=ALU.add, op1=ALU.mult).then_inc(n_u, 1)
                dve.wait_ge(n_u, b * FC + k + 1)
                dve.scalar_tensor_tensor(out=Q[:, k % RING, :], in0=Q[:, k % RING, :], scalar=cs12[:, k:k + 1],
                                         in1=HB[2 * (k % 2) + 1][:, :], op0=ALU.mult, op1=ALU.mult).then_inc(n_h, 1)

            def fl(b, k):
                src, dst = (Q, hA) if k < FC else (G, hB) if k < 2 * FC else (G, hA)
                dve.wait_ge(n_hi, b * 3 * FC + k + 1)
                dve.tensor_tensor(dst[1][:, k % FC, :], src[:, k % RING, :], dst[0][:, k % FC, :].bitcast(F32), ALU.subtract)\
                   .then_inc(n_lo, 1)

            def fo(b):
                dve.wait_ge(n_mm, b * NMM + NMM)
                dve.wait_ge(kept, b + 1)
                dve.scalar_tensor_tensor(out=keep[:, :], in0=HB[0][:, :], scalar=fsc[:, 4 * FC:4 * FC + 1],
                                         in1=keep[:, :], op0=ALU.mult, op1=ALU.add).then_inc(n_out, 1)

            steps = {"tb": tb, "clo": clo, "top": top, "gw": gw_, "q": q, "lo": lo, "x": lambda b, k: x1(b), "nm": offset,
                     "st": lambda b, k: (st0, None, st2)[k](b), "h": lambda b, k: (h, h1)[k](b), "oh": oh,
                     "tlo": lambda b: turned_lo(b, 0), "slo": lambda b: turned_lo(b, 1), "hlo": lambda b: turned_lo(b, 2),
                     "a": a, "alo": alo, "ff": ff, "u": u, "fl": fl, "fo": fo}

            def low_any():
                dve.wait_ge(low_row, 1)
                dve.reduce_max(lowr[:, 0:1], HB[3][0:1, 0:P], AX_X).then_inc(low_parts, 1)
                dve.wait_ge(low_parts, NPIECE + 1)
                dve.tensor_scalar(lowi[:, :], lowr[:, 0:1], 0.0, None, ALU.is_gt).then_inc(low_flag, 1)

            dve.memset(muT[MU:MU + 1, :], 1.0)
            dve.memset(onesf[:, :], 1.0)
            dve.memset(mhalf[:, :], -0.5).then_inc(ones_row, 1)
            dve.wait_ge(ones_row, 1)
            dve.tensor_copy(onesR[:, :], onesf[:, :])
            step = Steps(dve, dve_setup, 0, 0)
            dve.wait_ge(ld_state, 16 * 3)
            step(dve.reduce_max(awx[:, 0:1], aw6, AX_X))
            dve.tensor_scalar(awx[:, 1:2], awx[:, 0:1], -1.0, None, ALU.mult).then_inc(aw_max, 1)
            for k in range(0, KR, 2):
                dve.wait_ge(u_mm, k + 1)
                dve.tensor_copy(Uall[:, :, k], HB[k % 4][:, 0:B]).then_inc(u_even, 1)
            dve.wait_ge(ub_mm, 1)
            dve.tensor_copy(ub[:, :], X0[0:KR, 0:B])
            dve.wait_ge(ld_small, 16 * 7)
            dve.sem_inc(small_src, 1)
            dve.wait_ge(s_mm, 1)
            for n in range(3):
                last = dve.tensor_scalar(sz[:, n * B:(n + 1) * B], X1[:, n * B:(n + 1) * B], sb1[:, n:n + 1], None, ALU.add)
            last.then_inc(sz_ready, 1)
            dve.wait_ge(aw_exp, 1)
            step(dve.reciprocal(awx[:, 3:4], awx[:, 2:3]))
            step(dve.tensor_scalar(aw_e[:, :], aw_e[:, :], awx[:, 3:4], None, ALU.mult))
            for n in range(6):
                last = dve.tensor_scalar(wsc[:, n, :], iW1[:, n, :], aw_e[:, n:n + 1], None, ALU.mult)
            last.then_inc(wsc_ready, 1)
            dve.wait_ge(s_th, 1)
            step(dve.scalar_tensor_tensor(out=sa[:, :], in0=sth[:, :], scalar=1.0, in1=sz[:, :], op0=ALU.add, op1=ALU.mult))
            dve.tensor_scalar(sa[:, :], sa[:, :], 0.5, None, ALU.mult).then_inc(sa_ready, 1)
            dve.wait_ge(sy_mm, 1)
            step(dve.tensor_tensor(sy[:, :, :], X2[:, 0:3 * P].rearrange("p (n d) -> p n d", n=3), sbc[:, 0, :, :], ALU.add))
            for n in range(3):
                ins = dve.bn_stats(sbn[:, n, :], sy[:, n, :])
            step(ins)
            for n in range(3):
                ins = dve.bn_aggr(smv[:, n, :], sbn[:, n, :])
            step(ins)
            dve.tensor_scalar(sve[:, :], smv[:, :, 1], EPS, None, ALU.add).then_inc(sv_ready, 1)
            dve.wait_ge(srs_ready, 1)
            for n in range(3):
                ins = dve.tensor_scalar(sy[:, n, :], sy[:, n, :], smv[:, n, 0:1], srs[:, n:n + 1], ALU.subtract, ALU.mult)
            step(ins)
            step(dve.tensor_tensor(sy[:, :, :], sy[:, :, :], sbc[:, 1, :, :], ALU.mult))
            dve.tensor_tensor(sy[:, :, :], sy[:, :, :], sbc[:, 2, :, :], ALU.add).then_inc(sy_ready, 1)
            tb(0)
            dve.wait_ge(ld_small, 16 * 7)
            dve.tensor_scalar(wintf[:, :], iW2, 0.5, None, ALU.mult).then_inc(small_src, 2)
            dve.wait_ge(wsc_ready, 1)
            step(dve.tensor_tensor(wmixf[:, 0, :], wsc[:, 2, :], wsc[:, 3, :], ALU.add))
            dve.tensor_tensor(wmixf[:, 0, :], wmixf[:, 0, :], wsc[:, 4, :], ALU.add)
            dve.tensor_copy(wmixf[:, 1, :], wsc[:, 1, :])
            dve.tensor_copy(wmixf[:, 2, :], wsc[:, 5, :])
            dve.tensor_copy(wmixf[:, 3, :], wsc[:, 0, :]).then_inc(small_src, 1)
            step(dve.tensor_scalar(hs1[:, :], fsc[:, 0:FC], 0.5, None, ALU.mult))
            dve.tensor_tensor(cs12[:, :], hs1[:, :], fsc[:, FC:2 * FC], ALU.mult)
            clo(0)

            def small_lo_(n):
                src, dst = small_ops[n]
                dve.wait_ge(small_hi, n + 1)
                dve.tensor_tensor(dst[1], src, dst[0].bitcast(F32), ALU.subtract).then_inc(small_lo, 1)

            small_lo_(0)
            dve.wait_ge(fold_mm, 1)
            dve.tensor_copy(tab8f[:, :], X1[0:NI, 3 * P:4 * P]).then_inc(small_src, 1)
            dve.tensor_tensor(vecf[:, :], X2[:, 0:P], ibb, ALU.add).then_inc(small_src, 1)
            big_lo(0, W1)
            top(0)
            for n in range(1, NSMALL):
                small_lo_(n)
            gw_(0)
            big_lo(1, W2)
            late_lo(2, 3, 4, 5)
            begin(steps, ORDER["DVE"],
                  {(0, word): partial(low_check, n) for n, word in enumerate(("st0", "nm0", "h1", "nm1", "top", "h0"))}
                  | {(0, "a"): low_any}, done=("tb", "clo", "top", "gw"))
            go_on(dve, steps, ORDER["DVE"])

        @block.gpsimd
        def _(pool):
            def gather(b):
                settled(pool)
                pool.tensor_copy(ixb[:, :, :], ixall[:, :, bass.ds(b * TT, TT)]).then_inc(ixb_ready, 1)
                pool.wait_ge(ixb_ready, b + 1)
                settled(pool)
                for t in range(TT):
                    for n, (dst, src) in enumerate(((gp, "pgb"), (gc, "ctg"), (gm, "msg"))):
                        pool.indirect_dma_start(out=dst[:, t, :], out_offset=None, in_=A[src],
                                                in_offset=bass.IndirectOffsetOnAxis(ap=ixb[:, n, t:t + 1].bitcast(U32), axis=0))\
                            .then_inc(gathered, 16)

            def pow_(b, n):
                pool.wait_ge(ve_ready, b * 3 + n + 1)
                pool.tensor_tensor(rstd[:, n, :], ve[:, n, :], mhalf[:, :], ALU.pow).then_inc(rstd_ready, 1)

            pool.wait_ge(sv_ready, 1)
            pool.tensor_tensor(srs[:, :], sve[:, :], mhalf[:, 0:3], ALU.pow).then_inc(srs_ready, 1)
            pool.wait_ge(ld_small, 16 * 7)

            def xlo(b):
                pool.wait_ge(x1_hi, b + 1)
                pool.tensor_tensor(cx[1][:, :], x1T[:, :], cx[0][:, :].bitcast(F32), ALU.subtract).then_inc(x1_lo, 1)

            def t_(b):
                pool.wait_ge(gathered, (b + 1) * 16 * 3 * TT)
                pool.wait_ge(normed, b * 3 + 1)
                if not first(b):
                    pool.wait_ge(a_lo, b)
                pool.tensor_tensor(tt[:, :, :], xh[:, :, :], gc[:, :, P:2 * P], ALU.mult).then_inc(ts_ready, 1)

            def s_(b):
                pool.tensor_tensor(ss[:, :, :], xh[:, :, :], gm[:, :, :], ALU.mult).then_inc(ts_ready, 1)

            def flo(b):
                pool.wait_ge(f_hi, b + 1)
                if not first(b):
                    pool.wait_ge(n_mm, (b - 1) * NMM + FC)
                pool.tensor_tensor(fin[1][:, :], flat(xh), fin[0][:, :].bitcast(F32), ALU.subtract).then_inc(f_lo, 1)

            def keep_x(b):
                if not first(b):
                    pool.wait_ge(stored, b * 16)
                pool.wait_ge(x1_ready, b + 1)
                settled(pool)
                pool.tensor_copy(keep[:, :], x1T[:, :]).then_inc(kept, 1)

            def gather_(b):
                if not first(b):
                    pool.wait_ge(h_ready, b)
                    pool.wait_ge(ts_ready, b * 2)
                gather(b)

            steps = {"pw": pow_, "xlo": xlo, "t": t_, "s": s_, "flo": flo, "keep": keep_x, "gath": gather_}
            begin(steps, ORDER["Pool"])
            go_on(pool, steps, ORDER["Pool"])


def kernel(**inputs):
    import numpy as np
    import concourse.bacc as bacc
    from concourse.bass_utils import run_bass_kernel_spmd as run

    g = {k: np.asarray(v) for k, v in inputs.items()}
    c1, f1, f0 = "L1_cond_", "L1_ffn_", "L0_ffn_"
    n = P

    def chunks(w):
        return w.reshape(-1, n, w.shape[1]).transpose(1, 0, 2).reshape(n, -1)

    def tiles(ix):
        return ix.reshape(-1, n).T

    def rows64(a):
        return np.concatenate([a, np.zeros((64 - a.shape[0], a.shape[1]), a.dtype)])

    st3 = ("mem", "noi", "res")
    zero = np.zeros((n, 8), np.float32)
    tb = []
    for name, at in (("cp_b", 0), ("tm_b", 0), ("ms_b", 5)):
        z = zero.copy()
        w = g[c1 + name].T
        z[:, at:at + w.shape[1]] = w
        tb.append(z)
    W1 = g[f0 + "W1"].reshape(-1, n)
    W2 = g[f0 + "W2"].transpose(0, 2, 1).reshape(-1, n)
    lay = {
        "xT": g["x"].reshape(-1, n).T,
        "cond_512T": g["cond_512"].T,
        "W_dec": g["L0_cond_W_dec"], "b_dec": g["L0_cond_b_dec"][None], "V": g["L0_cond_V"],
        "b2": g[f0 + "b2"], "W1T": W1.T, "W2T": chunks(W2),
        "pgb": np.concatenate([g[c1 + "pw_g"], g[c1 + "pw_b"]], 1),
        "ctg": np.concatenate([g[c1 + "cp_g"], g[c1 + "tm_g"]], 1), "msg": g[c1 + "ms_g"],
        "ixall": np.stack([tiles(g["itok_BxS_0_999"]), tiles(g["itok_BxS_0_4"]), tiles(g["mask_BxS_ik0"])], 1),
        "ic_row": g["itok_BxS_0_4"].reshape(1, -1), "im_row": g["mask_BxS_ik0"].reshape(1, -1),
        "states": np.stack([rows64(a) for a in (g["cond_512"].T, g["cond_64"].T, g["fside_Bx32_0"].T,
                                                g[c1 + "mem_W1"], g[c1 + "noi_W1"], g[c1 + "res_W1"])], 1),
        "earlyP": np.concatenate([g[c1 + k + "_W2"] for k in st3] + [chunks(g[c1 + "int_W1"]), g[c1 + "int_W2"]] + tb
                                 + [g[f0 + "Wg"].T] + [g[c1 + k + "_b1"][:, None] for k in st3], 1),
        "earlyB": np.concatenate([g[c1 + k + v] for v in ("_b2", "_g", "_be") for k in st3]
                                 + [g[c1 + "int_b1"], g[c1 + "aw"]]),
        "keepP": np.concatenate([np.eye(n, dtype=np.float32), g[f0 + "b1"].reshape(-1, n).T]
                                + [g[f1 + k + "_s"].reshape(-1, n).T for k in ("w1", "w2", "h1", "h2", "w3")]
                                + [np.zeros((n, 3), np.float32), g[c1 + "int_g"][:, None], g[c1 + "int_be"][:, None]], 1),
        "keepB": np.concatenate([g[f0 + "bg"], np.arange(8, 0, -1).astype(np.float32)]),
        "int_b2": g[c1 + "int_b2"][None],
        "w12T": np.concatenate([g[f1 + "w1_w"].T, g[f1 + "w2_w"].T], 1),
        "h1T": chunks(g[f1 + "h1_w"].T), "h2T": chunks(g[f1 + "h2_w"].T), "w3T": chunks(g[f1 + "w3_w"].T),
        "iota8": np.array([0, 1, 2, 3, 4, 0, 1, 2], np.float32)[:, None],
    }
    nc = bacc.Bacc("TRN2", target_bir_lowering=False, num_devices=1)
    arrays, A = {}, {}
    for name, a in lay.items():
        a = np.ascontiguousarray(a)
        arrays[name + "_in"] = a
        A[name] = nc.dram_tensor(name + "_in", a.shape, mybir.dt.from_np(a.dtype), kind="ExternalInput").ap()
    tok = lay["xT"].shape[1]
    out = nc.dram_tensor("outT", (n, tok), F32, kind="ExternalOutput").ap()
    build(nc, A, out)
    r = run(nc, [arrays], core_ids=[0])
    got = r.results[0]["outT"]
    return got.T.reshape(g["x"].shape)
```
